# Optimizing a Trainium2 kernel written in Bass

```python
import numpy as np
import jax
import jax.numpy as jnp

def _softmax(x, axis=-1):
    return jax.nn.softmax(x, axis=axis)

def _gelu(x):
    return jax.nn.gelu(x, approximate=True)

def _silu(x):
    return jax.nn.silu(x)

def _sigmoid(x):
    return jax.nn.sigmoid(x)

def _layernorm(x, axis=-1, eps=1e-05):
    m = jnp.mean(x, axis=axis, keepdims=True)
    v = jnp.var(x, axis=axis, keepdims=True)
    return (x - m) / jnp.sqrt(v + eps)

def _scatter_add(tgt, idx, src, axis=0):
    return tgt.at[idx].add(src)

def _segment_sum(src, seg, n):
    return jax.ops.segment_sum(src, seg, n)
kernel_name = 'mk_audio_tower_d4_tok_audfeat256_r4_d6affa'

def setup_inputs(seed: int=0):
    np.random.seed(seed)
    _w = jnp.asarray

    def _rec_inputs():
        import jax
        import jax.numpy as jnp
        _rk = jax.random.key(seed)
        x = -0.000392918 + 0.999932 * jax.random.normal(jax.random.fold_in(_rk, 1), (8, 375, 128), jnp.float32)
        return x
    x = _rec_inputs()

    def _L0_tok_setup():
        import jax, jax.numpy as jnp
        from jax import lax
        import numpy as np
        BN_EPS = 0.001

        @jax.custom_vjp
        def ste_sign(x):
            return jnp.where(x >= 0, 1.0, -1.0).astype(x.dtype)

        def _ste_fwd(x):
            return (ste_sign(x), x)

        def _ste_bwd(x, g):
            return (g * (jnp.abs(x) <= 1.0).astype(g.dtype),)
        ste_sign.defvjp(_ste_fwd, _ste_bwd)
        key = jax.random.key(seed)
        ks = jax.random.split(key, 6)
        x = jax.random.normal(ks[0], (64, 512, 128), dtype=jnp.float32)
        kernel = jax.random.normal(ks[1], (3, 128, 64), dtype=jnp.float32) * 0.05
        bias = jax.random.normal(ks[2], (64,), dtype=jnp.float32) * 0.01
        beta = jax.random.normal(ks[3], (64,), dtype=jnp.float32) * 0.01
        moving_mean = jax.random.normal(ks[4], (64,), dtype=jnp.float32) * 0.1
        moving_var = jax.random.uniform(ks[5], (64,), dtype=jnp.float32) + 0.5
        return {'x': x, 'kernel': kernel, 'bias': bias, 'beta': beta, 'moving_mean': moving_mean, 'moving_var': moving_var}
    _L0_tok_all = _L0_tok_setup()
    _L0_tok_in = {k: v for k, v in _L0_tok_all.items() if k in ('kernel', 'bias', 'beta', 'moving_mean', 'moving_var')}
    del _L0_tok_all

    def _L0_attn_setup():
        import jax, jax.numpy as jnp
        import numpy as np
        B, T, H, D, N, R, K = (2, 256, 64, 256, 16, 16, 4)
        EPS = 1e-05

        def layer_norm(x, g, b):
            m = jnp.mean(x, -1, keepdims=True)
            v = jnp.mean((x - m) ** 2, -1, keepdims=True)
            return (x - m) * jax.lax.rsqrt(v + EPS) * g + b

        def rms_norm(x, w):
            return x * jax.lax.rsqrt(jnp.mean(x * x, -1, keepdims=True) + EPS) * w

        def selective_scan(u, dt, A, Bm, Cm, Dp):
            dA = jnp.exp(dt[..., None] * A)
            dBu = (dt * u)[..., None] * Bm[:, :, None, :]

            def step(h, inp):
                dA_t, dBu_t, C_t = inp
                h = dA_t * h + dBu_t
                return (h, jnp.einsum('bdn,bn->bd', h, C_t))
            h0 = jnp.zeros((u.shape[0], u.shape[2], A.shape[1]), u.dtype)
            _, ys = jax.lax.scan(step, h0, (dA.swapaxes(0, 1), dBu.swapaxes(0, 1), Cm.swapaxes(0, 1)))
            return ys.swapaxes(0, 1) + u * Dp

        def mamba_mixer(h, inproj_w, conv_w, conv_b, xproj_w, dtproj_w, dtproj_b, A_log, Dp, outproj_w):
            proj = jnp.einsum('bth,eh->bte', h, inproj_w)
            u, gate = (proj[..., :D], proj[..., D:])
            uc = jax.lax.conv_general_dilated(u.swapaxes(1, 2), conv_w, (1,), [(K - 1, 0)], dimension_numbers=('NCH', 'OIH', 'NCH'), feature_group_count=D)
            u = jax.nn.silu(uc + conv_b[None, :, None]).swapaxes(1, 2)
            ssm = jnp.einsum('btd,ed->bte', u, xproj_w)
            dt_r, Bm, Cm = (ssm[..., :R], ssm[..., R:R + N], ssm[..., R + N:])
            dt = jax.nn.softplus(jnp.einsum('btr,dr->btd', dt_r, dtproj_w) + dtproj_b)
            A = -jnp.exp(A_log)
            y = selective_scan(u, dt, A, Bm, Cm, Dp)
            y = y * jax.nn.silu(gate)
            return jnp.einsum('btd,hd->bth', y, outproj_w)

        def _forward(x, pre_g, pre_b, post_g, post_b, norm_w, inproj_w, conv_w, conv_b, xproj_w, dtproj_w, dtproj_b, A_log, D_param, outproj_w, normf_w):
            h = layer_norm(x, pre_g, pre_b)
            for i in range(2):
                h = h + mamba_mixer(rms_norm(h, norm_w[i]), inproj_w[i], conv_w[i], conv_b[i], xproj_w[i], dtproj_w[i], dtproj_b[i], A_log[i], D_param[i], outproj_w[i])
            h = rms_norm(h, normf_w)
            return layer_norm(h, post_g, post_b)
        key = jax.random.key(seed)
        ks = jax.random.split(key, 8)
        s = 0.05
        A0 = jnp.log(jnp.arange(1, N + 1, dtype=jnp.float32))
        return {'x': jax.random.normal(ks[0], (B, T, H), jnp.float32), 'pre_g': jnp.ones((H,), jnp.float32), 'pre_b': jnp.zeros((H,), jnp.float32), 'post_g': jnp.ones((H,), jnp.float32), 'post_b': jnp.zeros((H,), jnp.float32), 'norm_w': jnp.ones((2, H), jnp.float32), 'inproj_w': jax.random.normal(ks[1], (2, 2 * D, H), jnp.float32) * s, 'conv_w': jax.random.normal(ks[2], (2, D, 1, K), jnp.float32) * s, 'conv_b': jnp.zeros((2, D), jnp.float32), 'xproj_w': jax.random.normal(ks[3], (2, R + 2 * N, D), jnp.float32) * s, 'dtproj_w': jax.random.normal(ks[4], (2, D, R), jnp.float32) * s, 'dtproj_b': jax.random.normal(ks[5], (2, D), jnp.float32) * s, 'A_log': jnp.broadcast_to(A0, (2, D, N)) + 0.0, 'D_param': jnp.ones((2, D), jnp.float32), 'outproj_w': jax.random.normal(ks[6], (2, H, D), jnp.float32) * s, 'normf_w': jnp.ones((H,), jnp.float32)}
    _L0_attn_all = _L0_attn_setup()
    _L0_attn_in = {k: v for k, v in _L0_attn_all.items() if k in ('pre_g', 'pre_b', 'post_g', 'post_b', 'norm_w', 'inproj_w', 'conv_w', 'conv_b', 'xproj_w', 'dtproj_w', 'dtproj_b', 'A_log', 'D_param', 'outproj_w', 'normf_w')}
    del _L0_attn_all

    def _L0_ffn_setup():
        import jax, jax.numpy as jnp
        import numpy as np
        B, S, D = (8, 1024, 64)
        H = 4 * D
        CAPACITY = 0.5
        key = jax.random.key(seed)
        ks = jax.random.split(key, 6)
        x = jax.random.normal(ks[0], (B, S, D), dtype=jnp.float32)
        attention_mask = jnp.zeros((B, 1, 1, S), dtype=jnp.float32)
        wr = jax.random.normal(ks[1], (D, 1), dtype=jnp.float32) * 0.02
        br = jnp.zeros((1,), dtype=jnp.float32)
        w1 = jax.random.normal(ks[2], (D, H), dtype=jnp.float32) * 0.02
        b1 = jnp.zeros((H,), dtype=jnp.float32)
        w2 = jax.random.normal(ks[3], (H, D), dtype=jnp.float32) * 0.02
        b2 = jnp.zeros((D,), dtype=jnp.float32)
        return {'x': x, 'attention_mask': attention_mask, 'wr': wr, 'br': br, 'w1': w1, 'b1': b1, 'w2': w2, 'b2': b2}
    _L0_ffn_all = _L0_ffn_setup()
    _L0_ffn_in = {k: v for k, v in _L0_ffn_all.items() if k in ('attention_mask', 'wr', 'br', 'w1', 'b1', 'w2', 'b2')}
    del _L0_ffn_all

    def _L1_attn_setup():
        import jax, jax.numpy as jnp
        import numpy as np
        B, N, D = (4, 1024, 64)
        key = jax.random.key(seed)
        ks = jax.random.split(key, 7)

        def xavier(k, shape):
            fan_in, fan_out = (shape[1], shape[0])
            a = jnp.sqrt(6.0 / (fan_in + fan_out))
            return jax.random.uniform(k, shape, jnp.float32, -a, a)
        return {'x': jax.random.normal(ks[0], (B, N, D), jnp.float32), 'Wq': xavier(ks[1], (D, D)), 'bq': jnp.zeros((D,), jnp.float32), 'Wk': xavier(ks[2], (D, D)), 'bk': jnp.zeros((D,), jnp.float32), 'Wv': xavier(ks[3], (D, D)), 'bv': jnp.zeros((D,), jnp.float32), 'scale': jnp.asarray([jnp.sqrt(jnp.float32(D))])}
    _L1_attn_all = _L1_attn_setup()
    _L1_attn_in = {k: v for k, v in _L1_attn_all.items() if k in ('Wq', 'bq', 'Wk', 'bk', 'Wv', 'bv', 'scale')}
    del _L1_attn_all

    def _L1_ffn_setup():
        import jax, jax.numpy as jnp
        import numpy as np
        B, S, H, NH, NE = (4, 256, 64, 4, 4)
        D = H // NH
        EPS = 1e-08

        def layernorm(x, g, b):
            m = jnp.mean(x, axis=-1, keepdims=True)
            v = jnp.mean((x - m) ** 2, axis=-1, keepdims=True)
            return (x - m) / jnp.sqrt(v + EPS) * g + b
        key = jax.random.key(seed)
        ks = jax.random.split(key, 18)
        sc = 0.05
        return {'x': jax.random.normal(ks[0], (B, S, H), jnp.float32), 'hl_w': jax.random.normal(ks[1], (NH, D, H), jnp.float32) * sc, 'hl_b': jax.random.normal(ks[2], (NH, D), jnp.float32) * sc, 'wq': jax.random.normal(ks[3], (NH, NE, D, D), jnp.float32) * sc, 'wk': jax.random.normal(ks[4], (NH, D, D), jnp.float32) * sc, 'wv': jax.random.normal(ks[5], (NH, D, D), jnp.float32) * sc, 'gate_w': jax.random.normal(ks[6], (NH, NE, NE * D), jnp.float32) * sc, 'gate_b': jax.random.normal(ks[7], (NH, NE), jnp.float32) * sc, 'ln_g': jnp.ones((D,), jnp.float32), 'ln_b': jnp.zeros((D,), jnp.float32), 'fc1_w': jax.random.normal(ks[8], (D, D), jnp.float32) * sc, 'fc1_b': jax.random.normal(ks[9], (D,), jnp.float32) * sc, 'fc2_w': jax.random.normal(ks[10], (D, D), jnp.float32) * sc, 'fc2_b': jax.random.normal(ks[11], (D,), jnp.float32) * sc, 'fnorm_g': jnp.ones((D,), jnp.float32), 'fnorm_b': jnp.zeros((D,), jnp.float32), 'fgate_w': jax.random.normal(ks[12], (NH, H), jnp.float32) * sc}
    _L1_ffn_all = _L1_ffn_setup()
    _L1_ffn_in = {k: v for k, v in _L1_ffn_all.items() if k in ('hl_w', 'hl_b', 'wq', 'wk', 'wv', 'gate_w', 'gate_b', 'ln_g', 'ln_b', 'fc1_w', 'fc1_b', 'fc2_w', 'fc2_b', 'fnorm_g', 'fnorm_b', 'fgate_w')}
    del _L1_ffn_all

    def _L2_attn_setup():
        import jax, jax.numpy as jnp
        import numpy as np
        from math import sqrt
        DIM = 64
        key = jax.random.key(seed)
        k1, k2, k3, k4 = jax.random.split(key, 4)
        B, T, D, H, R = (2, 1024, DIM, 8, 32)

        def xavier(k, shape, fan_in, fan_out):
            a = sqrt(6.0 / (fan_in + fan_out))
            return jax.random.uniform(k, shape, jnp.float32, -a, a)
        x = jax.random.normal(k1, (B, T, D), jnp.float32)
        Q = xavier(k2, (H, R, D), D, R)
        K = xavier(k3, (H, R, D), D, R)
        VO = xavier(k4, (H, D, D), D, D)
        return {'x': x, 'Q': Q, 'K': K, 'VO': VO}
    _L2_attn_all = _L2_attn_setup()
    _L2_attn_in = {k: v for k, v in _L2_attn_all.items() if k in ('Q', 'K', 'VO')}
    del _L2_attn_all

    def _L2_ffn_setup():
        import jax, jax.numpy as jnp
        import numpy as np
        D_MODEL = 64
        EXPERT_DIM = 128
        NUM_EXPERTS = 8
        TOP_K = 2
        SEQ_LEN = 512
        BATCH = 2
        key = jax.random.key(seed)
        ks = jax.random.split(key, 8)
        s = 0.02
        x = jax.random.normal(ks[0], (SEQ_LEN, BATCH, D_MODEL), dtype=jnp.float32)
        Wg = jax.random.normal(ks[1], (D_MODEL, NUM_EXPERTS), dtype=jnp.float32) * s
        bg = jax.random.normal(ks[2], (NUM_EXPERTS,), dtype=jnp.float32) * s
        bias = jnp.zeros((NUM_EXPERTS,), dtype=jnp.float32)
        W1 = jax.random.normal(ks[3], (NUM_EXPERTS, D_MODEL, EXPERT_DIM), dtype=jnp.float32) * s
        b1 = jax.random.normal(ks[4], (NUM_EXPERTS, EXPERT_DIM), dtype=jnp.float32) * s
        W2 = jax.random.normal(ks[5], (NUM_EXPERTS, EXPERT_DIM, D_MODEL), dtype=jnp.float32) * s
        b2 = jax.random.normal(ks[6], (NUM_EXPERTS, D_MODEL), dtype=jnp.float32) * s
        return {'x': x, 'Wg': Wg, 'bg': bg, 'bias': bias, 'W1': W1, 'b1': b1, 'W2': W2, 'b2': b2}
    _L2_ffn_all = _L2_ffn_setup()
    _L2_ffn_in = {k: v for k, v in _L2_ffn_all.items() if k in ('Wg', 'bg', 'bias', 'W1', 'b1', 'W2', 'b2')}
    del _L2_ffn_all

    def _L3_attn_setup():
        import jax, jax.numpy as jnp
        import numpy as np
        HEADS = 8
        DIM = 64
        DIM_HEAD = 64
        DH = DIM_HEAD // HEADS
        SCALE = DIM_HEAD ** (-0.5)
        LN_EPS = 1e-05
        key = jax.random.key(seed)
        k1, k2, k3 = jax.random.split(key, 3)
        b, n = (8, 2048)
        x = jax.random.normal(k1, (b, n, DIM), dtype=jnp.float32)
        Wqkv = jax.random.normal(k2, (DIM, 3 * DIM_HEAD), dtype=jnp.float32) * 0.02
        Wout = jax.random.normal(k3, (DIM_HEAD, DIM), dtype=jnp.float32) * 0.02
        bout = jnp.zeros((DIM,), dtype=jnp.float32)
        gamma = jnp.ones((DIM,), dtype=jnp.float32)
        beta = jnp.zeros((DIM,), dtype=jnp.float32)
        return {'x': x, 'Wqkv': Wqkv, 'Wout': Wout, 'bout': bout, 'gamma': gamma, 'beta': beta}
    _L3_attn_all = _L3_attn_setup()
    _L3_attn_in = {k: v for k, v in _L3_attn_all.items() if k in ('Wqkv', 'Wout', 'bout', 'gamma', 'beta')}
    del _L3_attn_all

    def _L3_ffn_setup():
        import jax, jax.numpy as jnp
        import numpy as np
        E = 8
        K = 2
        D = 64
        H = 128
        DOUT = 64
        EPS = 1e-05
        key = jax.random.key(seed)
        ks = jax.random.split(key, 9)
        s = 0.02
        return {'x': jax.random.normal(ks[0], (4, 2048, D), jnp.float32), 'gamma': 1.0 + 0.05 * jax.random.normal(ks[1], (D,), jnp.float32), 'beta': 0.05 * jax.random.normal(ks[2], (D,), jnp.float32), 'Wr': 0.01 * jax.random.normal(ks[3], (D, E), jnp.float32), 'br': jnp.zeros((E,), jnp.float32), 'W1': s * jax.random.normal(ks[4], (E, D, H), jnp.float32), 'b1': s * jax.random.normal(ks[5], (E, H), jnp.float32), 'W2': s * jax.random.normal(ks[6], (E, H, DOUT), jnp.float32), 'b2': s * jax.random.normal(ks[7], (E, DOUT), jnp.float32)}
    _L3_ffn_all = _L3_ffn_setup()
    _L3_ffn_in = {k: v for k, v in _L3_ffn_all.items() if k in ('gamma', 'beta', 'Wr', 'br', 'W1', 'b1', 'W2', 'b2')}
    del _L3_ffn_all
    return {'x': x, 'L0_tok_kernel': _L0_tok_in['kernel'], 'L0_tok_bias': _L0_tok_in['bias'], 'L0_tok_beta': _L0_tok_in['beta'], 'L0_tok_moving_mean': _L0_tok_in['moving_mean'], 'L0_tok_moving_var': _L0_tok_in['moving_var'], 'L0_attn_pre_g': _L0_attn_in['pre_g'], 'L0_attn_pre_b': _L0_attn_in['pre_b'], 'L0_attn_post_g': _L0_attn_in['post_g'], 'L0_attn_post_b': _L0_attn_in['post_b'], 'L0_attn_norm_w': _L0_attn_in['norm_w'], 'L0_attn_inproj_w': _L0_attn_in['inproj_w'], 'L0_attn_conv_w': _L0_attn_in['conv_w'], 'L0_attn_conv_b': _L0_attn_in['conv_b'], 'L0_attn_xproj_w': _L0_attn_in['xproj_w'], 'L0_attn_dtproj_w': _L0_attn_in['dtproj_w'], 'L0_attn_dtproj_b': _L0_attn_in['dtproj_b'], 'L0_attn_A_log': _L0_attn_in['A_log'], 'L0_attn_D_param': _L0_attn_in['D_param'], 'L0_attn_outproj_w': _L0_attn_in['outproj_w'], 'L0_attn_normf_w': _L0_attn_in['normf_w'], 'L0_ffn_attention_mask': _L0_ffn_in['attention_mask'], 'L0_ffn_wr': _L0_ffn_in['wr'], 'L0_ffn_br': _L0_ffn_in['br'], 'L0_ffn_w1': _L0_ffn_in['w1'], 'L0_ffn_b1': _L0_ffn_in['b1'], 'L0_ffn_w2': _L0_ffn_in['w2'], 'L0_ffn_b2': _L0_ffn_in['b2'], 'L1_attn_Wq': _L1_attn_in['Wq'], 'L1_attn_bq': _L1_attn_in['bq'], 'L1_attn_Wk': _L1_attn_in['Wk'], 'L1_attn_bk': _L1_attn_in['bk'], 'L1_attn_Wv': _L1_attn_in['Wv'], 'L1_attn_bv': _L1_attn_in['bv'], 'L1_attn_scale': _L1_attn_in['scale'], 'L1_ffn_hl_w': _L1_ffn_in['hl_w'], 'L1_ffn_hl_b': _L1_ffn_in['hl_b'], 'L1_ffn_wq': _L1_ffn_in['wq'], 'L1_ffn_wk': _L1_ffn_in['wk'], 'L1_ffn_wv': _L1_ffn_in['wv'], 'L1_ffn_gate_w': _L1_ffn_in['gate_w'], 'L1_ffn_gate_b': _L1_ffn_in['gate_b'], 'L1_ffn_ln_g': _L1_ffn_in['ln_g'], 'L1_ffn_ln_b': _L1_ffn_in['ln_b'], 'L1_ffn_fc1_w': _L1_ffn_in['fc1_w'], 'L1_ffn_fc1_b': _L1_ffn_in['fc1_b'], 'L1_ffn_fc2_w': _L1_ffn_in['fc2_w'], 'L1_ffn_fc2_b': _L1_ffn_in['fc2_b'], 'L1_ffn_fnorm_g': _L1_ffn_in['fnorm_g'], 'L1_ffn_fnorm_b': _L1_ffn_in['fnorm_b'], 'L1_ffn_fgate_w': _L1_ffn_in['fgate_w'], 'L2_attn_Q': _L2_attn_in['Q'], 'L2_attn_K': _L2_attn_in['K'], 'L2_attn_VO': _L2_attn_in['VO'], 'L2_ffn_Wg': _L2_ffn_in['Wg'], 'L2_ffn_bg': _L2_ffn_in['bg'], 'L2_ffn_bias': _L2_ffn_in['bias'], 'L2_ffn_W1': _L2_ffn_in['W1'], 'L2_ffn_b1': _L2_ffn_in['b1'], 'L2_ffn_W2': _L2_ffn_in['W2'], 'L2_ffn_b2': _L2_ffn_in['b2'], 'L3_attn_Wqkv': _L3_attn_in['Wqkv'], 'L3_attn_Wout': _L3_attn_in['Wout'], 'L3_attn_bout': _L3_attn_in['bout'], 'L3_attn_gamma': _L3_attn_in['gamma'], 'L3_attn_beta': _L3_attn_in['beta'], 'L3_ffn_gamma': _L3_ffn_in['gamma'], 'L3_ffn_beta': _L3_ffn_in['beta'], 'L3_ffn_Wr': _L3_ffn_in['Wr'], 'L3_ffn_br': _L3_ffn_in['br'], 'L3_ffn_W1': _L3_ffn_in['W1'], 'L3_ffn_b1': _L3_ffn_in['b1'], 'L3_ffn_W2': _L3_ffn_in['W2'], 'L3_ffn_b2': _L3_ffn_in['b2']}

def reference(x, L0_tok_kernel, L0_tok_bias, L0_tok_beta, L0_tok_moving_mean, L0_tok_moving_var, L0_attn_pre_g, L0_attn_pre_b, L0_attn_post_g, L0_attn_post_b, L0_attn_norm_w, L0_attn_inproj_w, L0_attn_conv_w, L0_attn_conv_b, L0_attn_xproj_w, L0_attn_dtproj_w, L0_attn_dtproj_b, L0_attn_A_log, L0_attn_D_param, L0_attn_outproj_w, L0_attn_normf_w, L0_ffn_attention_mask, L0_ffn_wr, L0_ffn_br, L0_ffn_w1, L0_ffn_b1, L0_ffn_w2, L0_ffn_b2, L1_attn_Wq, L1_attn_bq, L1_attn_Wk, L1_attn_bk, L1_attn_Wv, L1_attn_bv, L1_attn_scale, L1_ffn_hl_w, L1_ffn_hl_b, L1_ffn_wq, L1_ffn_wk, L1_ffn_wv, L1_ffn_gate_w, L1_ffn_gate_b, L1_ffn_ln_g, L1_ffn_ln_b, L1_ffn_fc1_w, L1_ffn_fc1_b, L1_ffn_fc2_w, L1_ffn_fc2_b, L1_ffn_fnorm_g, L1_ffn_fnorm_b, L1_ffn_fgate_w, L2_attn_Q, L2_attn_K, L2_attn_VO, L2_ffn_Wg, L2_ffn_bg, L2_ffn_bias, L2_ffn_W1, L2_ffn_b1, L2_ffn_W2, L2_ffn_b2, L3_attn_Wqkv, L3_attn_Wout, L3_attn_bout, L3_attn_gamma, L3_attn_beta, L3_ffn_gamma, L3_ffn_beta, L3_ffn_Wr, L3_ffn_br, L3_ffn_W1, L3_ffn_b1, L3_ffn_W2, L3_ffn_b2):
    import jax
    import jax.numpy as jnp

    def _L0_tok_ref(x, kernel, bias, beta, moving_mean, moving_var):
        import jax, jax.numpy as jnp
        from jax import lax
        import numpy as np
        BN_EPS = 0.001

        @jax.custom_vjp
        def ste_sign(x):
            return jnp.where(x >= 0, 1.0, -1.0).astype(x.dtype)

        def _ste_fwd(x):
            return (ste_sign(x), x)

        def _ste_bwd(x, g):
            return (g * (jnp.abs(x) <= 1.0).astype(g.dtype),)
        ste_sign.defvjp(_ste_fwd, _ste_bwd)
        xq = ste_sign(x)
        kq = ste_sign(kernel)
        y = lax.conv_general_dilated(xq, kq, window_strides=(1,), padding='VALID', dimension_numbers=('NWC', 'WIO', 'NWC'))
        y = y + bias
        inv = lax.rsqrt(moving_var + BN_EPS)
        return (y - moving_mean) * inv + beta

    def _L0_attn_ref(x, pre_g, pre_b, post_g, post_b, norm_w, inproj_w, conv_w, conv_b, xproj_w, dtproj_w, dtproj_b, A_log, D_param, outproj_w, normf_w):
        import jax, jax.numpy as jnp
        import numpy as np
        B, T, H, D, N, R, K = (2, 256, 64, 256, 16, 16, 4)
        EPS = 1e-05

        def layer_norm(x, g, b):
            m = jnp.mean(x, -1, keepdims=True)
            v = jnp.mean((x - m) ** 2, -1, keepdims=True)
            return (x - m) * jax.lax.rsqrt(v + EPS) * g + b

        def rms_norm(x, w):
            return x * jax.lax.rsqrt(jnp.mean(x * x, -1, keepdims=True) + EPS) * w

        def selective_scan(u, dt, A, Bm, Cm, Dp):
            dA = jnp.exp(dt[..., None] * A)
            dBu = (dt * u)[..., None] * Bm[:, :, None, :]

            def step(h, inp):
                dA_t, dBu_t, C_t = inp
                h = dA_t * h + dBu_t
                return (h, jnp.einsum('bdn,bn->bd', h, C_t))
            h0 = jnp.zeros((u.shape[0], u.shape[2], A.shape[1]), u.dtype)
            _, ys = jax.lax.scan(step, h0, (dA.swapaxes(0, 1), dBu.swapaxes(0, 1), Cm.swapaxes(0, 1)))
            return ys.swapaxes(0, 1) + u * Dp

        def mamba_mixer(h, inproj_w, conv_w, conv_b, xproj_w, dtproj_w, dtproj_b, A_log, Dp, outproj_w):
            proj = jnp.einsum('bth,eh->bte', h, inproj_w)
            u, gate = (proj[..., :D], proj[..., D:])
            uc = jax.lax.conv_general_dilated(u.swapaxes(1, 2), conv_w, (1,), [(K - 1, 0)], dimension_numbers=('NCH', 'OIH', 'NCH'), feature_group_count=D)
            u = jax.nn.silu(uc + conv_b[None, :, None]).swapaxes(1, 2)
            ssm = jnp.einsum('btd,ed->bte', u, xproj_w)
            dt_r, Bm, Cm = (ssm[..., :R], ssm[..., R:R + N], ssm[..., R + N:])
            dt = jax.nn.softplus(jnp.einsum('btr,dr->btd', dt_r, dtproj_w) + dtproj_b)
            A = -jnp.exp(A_log)
            y = selective_scan(u, dt, A, Bm, Cm, Dp)
            y = y * jax.nn.silu(gate)
            return jnp.einsum('btd,hd->bth', y, outproj_w)

        def _forward(x, pre_g, pre_b, post_g, post_b, norm_w, inproj_w, conv_w, conv_b, xproj_w, dtproj_w, dtproj_b, A_log, D_param, outproj_w, normf_w):
            h = layer_norm(x, pre_g, pre_b)
            for i in range(2):
                h = h + mamba_mixer(rms_norm(h, norm_w[i]), inproj_w[i], conv_w[i], conv_b[i], xproj_w[i], dtproj_w[i], dtproj_b[i], A_log[i], D_param[i], outproj_w[i])
            h = rms_norm(h, normf_w)
            return layer_norm(h, post_g, post_b)
        return _forward(x, pre_g, pre_b, post_g, post_b, norm_w, inproj_w, conv_w, conv_b, xproj_w, dtproj_w, dtproj_b, A_log, D_param, outproj_w, normf_w)

    def _L0_ffn_ref(x, attention_mask, wr, br, w1, b1, w2, b2):
        import jax, jax.numpy as jnp
        import numpy as np
        B, S, D = (8, 1024, 64)
        H = 4 * D
        CAPACITY = 0.5
        b, s, d = x.shape
        weights = (jnp.einsum('bsd,do->bso', x, wr) + br)[..., 0]
        k = max(1, int(CAPACITY * s))
        kk = k - 1 if k > 1 else 1
        _, idx = jax.lax.top_k(weights, k)
        sel_idx = idx[:, :kk]
        sel = jnp.take_along_axis(x, sel_idx[:, :, None], axis=1)
        h = jax.nn.gelu(jnp.einsum('bkd,dh->bkh', sel, w1) + b1)
        y = jnp.einsum('bkh,hd->bkd', h, w2) + b2
        w_sel = jnp.take_along_axis(weights, sel_idx, axis=1)
        y = y * w_sel[..., None]
        batch_idx = jnp.arange(b)[:, None]
        processed = jnp.zeros_like(x).at[batch_idx, sel_idx].set(y)
        return processed + x

    def _L1_attn_ref(x, Wq, bq, Wk, bk, Wv, bv, scale):
        import jax, jax.numpy as jnp
        import numpy as np
        B, N, D = (4, 1024, 64)
        q = jnp.einsum('bnd,ed->bne', x, Wq) + bq
        k = jnp.einsum('bnd,ed->bne', x, Wk) + bk
        v = jnp.einsum('bnd,ed->bne', x, Wv) + bv
        scores = jnp.einsum('bqd,bkd->bqk', q, k) / scale[0]
        attn = jax.nn.softmax(scores, axis=-1)
        out = jnp.einsum('bqk,bkd->bqd', attn, v)
        return out

    def _L1_ffn_ref(x, hl_w, hl_b, wq, wk, wv, gate_w, gate_b, ln_g, ln_b, fc1_w, fc1_b, fc2_w, fc2_b, fnorm_g, fnorm_b, fgate_w):
        import jax, jax.numpy as jnp
        import numpy as np
        B, S, H, NH, NE = (4, 256, 64, 4, 4)
        D = H // NH
        EPS = 1e-08

        def layernorm(x, g, b):
            m = jnp.mean(x, axis=-1, keepdims=True)
            v = jnp.mean((x - m) ** 2, axis=-1, keepdims=True)
            return (x - m) / jnp.sqrt(v + EPS) * g + b
        b, s, h = x.shape
        nh, d, _ = wk.shape
        ne = wq.shape[1]
        sx = jnp.einsum('bsh,ndh->bnsd', x, hl_w) + hl_b[None, :, None, :]
        pad = sx == 0
        q = jnp.einsum('bnsd,neod->bneso', sx, wq)
        k = jnp.einsum('bnsd,nod->bnso', sx, wk)
        v = jnp.einsum('bnsd,nod->bnso', sx, wv)
        causal = jnp.where(jnp.tril(jnp.ones((s, s), bool)), 0.0, -jnp.inf).astype(x.dtype)
        scores = jnp.einsum('bnesd,bntd->bnest', q, k) * d ** 0.5 + causal
        att = jax.nn.softmax(scores, axis=-1)
        qkv = jnp.einsum('bnest,bntd->bnesd', att, v)
        qkv = jnp.where(pad[:, :, None], 0.0, qkv)
        out = jnp.transpose(qkv, (0, 1, 3, 2, 4)).reshape(b, nh, s, ne * d)
        gs = jax.nn.softmax(jnp.einsum('bnsf,nef->bnse', out, gate_w) + gate_b[None, :, None, :], axis=-1)
        mixed = jnp.einsum('bnsed,bnse->bnsd', out.reshape(b, nh, s, ne, d), gs)
        resid = sx[jnp.arange(nh), jnp.arange(nh)]
        hn = layernorm(mixed + resid, ln_g, ln_b)
        f_n = jnp.transpose(hn, (0, 2, 1, 3)).reshape(b, s, h)
        fx = f_n.reshape(b, s, nh, d)
        pm = fx == 0
        hx = jnp.where(pm, 0.0, fx @ fc1_w.T + fc1_b)
        hx = jax.nn.relu(hx)
        hx = jnp.where(pm, 0.0, hx @ fc2_w.T + fc2_b)
        hx = layernorm(hx + fx, fnorm_g, fnorm_b)
        fout = hx.reshape(b, s, h)
        fg = jax.nn.softmax(fout @ fgate_w.T, axis=-1)
        return (fout.reshape(b, s, nh, d) * fg[..., None]).reshape(b, s, h)

    def _L2_attn_ref(x, Q, K, VO):
        import jax, jax.numpy as jnp
        import numpy as np
        from math import sqrt
        DIM = 64
        d = x.shape[-1]
        q = jnp.einsum('btd,hrd->bhtr', x, Q)
        k = jnp.einsum('bud,hrd->bhur', x, K)
        scores = jnp.einsum('bhtr,bhur->bhtu', q, k) / sqrt(d)
        attn = jax.nn.softmax(scores, axis=-1)
        ctx = jnp.einsum('bhtu,bud->bhtd', attn, x)
        out = jnp.einsum('bhtd,hde->bte', ctx, VO)
        return out

    def _L2_ffn_ref(x, Wg, bg, bias, W1, b1, W2, b2):
        import jax, jax.numpy as jnp
        import numpy as np
        D_MODEL = 64
        EXPERT_DIM = 128
        NUM_EXPERTS = 8
        TOP_K = 2
        SEQ_LEN = 512
        BATCH = 2
        x_flat = x.reshape(-1, D_MODEL)
        gate_logits = x_flat @ Wg + bg + bias
        topk_vals, topk_idx = jax.lax.top_k(gate_logits, TOP_K)
        topk_w = jax.nn.softmax(topk_vals, axis=-1)
        combine = (jax.nn.one_hot(topk_idx, NUM_EXPERTS, dtype=x.dtype) * topk_w[..., None]).sum(axis=1)
        h = jax.nn.relu(jnp.einsum('td,edh->teh', x_flat, W1) + b1)
        y = jnp.einsum('teh,ehd->ted', h, W2) + b2
        out = jnp.einsum('ted,te->td', y, combine)
        return out.reshape(x.shape)

    def _L3_attn_ref(x, Wqkv, Wout, bout, gamma, beta):
        import jax, jax.numpy as jnp
        import numpy as np
        HEADS = 8
        DIM = 64
        DIM_HEAD = 64
        DH = DIM_HEAD // HEADS
        SCALE = DIM_HEAD ** (-0.5)
        LN_EPS = 1e-05
        b, n, c = x.shape
        qkv = x @ Wqkv
        qkv = qkv.reshape(b, n, 3, HEADS, DH).transpose(2, 0, 3, 1, 4)
        q, k, v = (qkv[0], qkv[1], qkv[2])
        k = jax.nn.softmax(k, axis=-2)
        q = q * SCALE
        A = jnp.einsum('bhid,bhie->bhde', k, q)
        out = jnp.einsum('bhjd,bhde->bhje', v, A)
        out = out.reshape(b, n, c)
        out = out @ Wout + bout
        mu = jnp.mean(out, axis=-1, keepdims=True)
        var = jnp.var(out, axis=-1, keepdims=True)
        out = (out - mu) * jax.lax.rsqrt(var + LN_EPS) * gamma + beta
        return out

    def _L3_ffn_ref(x, gamma, beta, Wr, br, W1, b1, W2, b2):
        import jax, jax.numpy as jnp
        import numpy as np
        E = 8
        K = 2
        D = 64
        H = 128
        DOUT = 64
        EPS = 1e-05
        mu = jnp.mean(x, axis=-1, keepdims=True)
        var = jnp.mean(jnp.square(x - mu), axis=-1, keepdims=True)
        xn = (x - mu) * jax.lax.rsqrt(var + EPS) * gamma + beta
        logits = jnp.einsum('bsd,de->bse', xn, Wr) + br
        top_vals, top_idx = jax.lax.top_k(logits, K)
        w = jax.nn.softmax(top_vals, axis=-1)
        w_full = jnp.einsum('bsk,bske->bse', w, jax.nn.one_hot(top_idx, E, dtype=w.dtype))
        y = jnp.zeros(x.shape[:-1] + (DOUT,), x.dtype)
        for e in range(E):
            h = jax.nn.gelu(jnp.einsum('bsd,dh->bsh', xn, W1[e]) + b1[e], approximate=False)
            y_e = jnp.einsum('bsh,hd->bsd', h, W2[e]) + b2[e]
            y = y + y_e * w_full[..., e, None]
        return y
    h = _L0_tok_ref(x, L0_tok_kernel, L0_tok_bias, L0_tok_beta, L0_tok_moving_mean, L0_tok_moving_var)
    h = h + _L0_attn_ref(_layernorm(h, axis=-1), L0_attn_pre_g, L0_attn_pre_b, L0_attn_post_g, L0_attn_post_b, L0_attn_norm_w, L0_attn_inproj_w, L0_attn_conv_w, L0_attn_conv_b, L0_attn_xproj_w, L0_attn_dtproj_w, L0_attn_dtproj_b, L0_attn_A_log, L0_attn_D_param, L0_attn_outproj_w, L0_attn_normf_w)
    h = h + _L0_ffn_ref(_layernorm(h, axis=-1), L0_ffn_attention_mask, L0_ffn_wr, L0_ffn_br, L0_ffn_w1, L0_ffn_b1, L0_ffn_w2, L0_ffn_b2)
    h = h + _L1_attn_ref(_layernorm(h, axis=-1), L1_attn_Wq, L1_attn_bq, L1_attn_Wk, L1_attn_bk, L1_attn_Wv, L1_attn_bv, L1_attn_scale)
    h = h + _L1_ffn_ref(_layernorm(h, axis=-1), L1_ffn_hl_w, L1_ffn_hl_b, L1_ffn_wq, L1_ffn_wk, L1_ffn_wv, L1_ffn_gate_w, L1_ffn_gate_b, L1_ffn_ln_g, L1_ffn_ln_b, L1_ffn_fc1_w, L1_ffn_fc1_b, L1_ffn_fc2_w, L1_ffn_fc2_b, L1_ffn_fnorm_g, L1_ffn_fnorm_b, L1_ffn_fgate_w)
    h = h + _L2_attn_ref(_layernorm(h, axis=-1), L2_attn_Q, L2_attn_K, L2_attn_VO)
    h = h + _L2_ffn_ref(_layernorm(h, axis=-1), L2_ffn_Wg, L2_ffn_bg, L2_ffn_bias, L2_ffn_W1, L2_ffn_b1, L2_ffn_W2, L2_ffn_b2)
    h = h + _L3_attn_ref(_layernorm(h, axis=-1), L3_attn_Wqkv, L3_attn_Wout, L3_attn_bout, L3_attn_gamma, L3_attn_beta)
    h = h + _L3_ffn_ref(_layernorm(h, axis=-1), L3_ffn_gamma, L3_ffn_beta, L3_ffn_Wr, L3_ffn_br, L3_ffn_W1, L3_ffn_b1, L3_ffn_W2, L3_ffn_b2)
    return h

_drawn_inputs = setup_inputs


def setup_inputs(seed=0):
    import zlib

    import numpy as np

    out = dict(_drawn_inputs(seed))
    spreads = {'L0_attn_pre_g': (1.0, 0.6),
     'L0_attn_pre_b': (0.0, 0.8),
     'L0_attn_post_g': (1.0, 0.6),
     'L0_attn_post_b': (0.0, 0.8),
     'L0_attn_norm_w': (1.0, 0.6),
     'L0_attn_conv_b': (0.0, 0.8),
     'L0_attn_D_param': (1.0, 0.6),
     'L0_attn_normf_w': (1.0, 0.6),
     'L0_ffn_b1': (0.0, 0.8),
     'L0_ffn_b2': (0.0, 0.8),
     'L1_attn_bq': (0.0, 0.8),
     'L1_attn_bk': (0.0, 2.0),
     'L1_attn_bv': (0.0, 0.8),
     'L1_ffn_ln_g': (1.0, 0.6),
     'L1_ffn_ln_b': (0.0, 0.8),
     'L1_ffn_fnorm_g': (1.0, 0.6),
     'L1_ffn_fnorm_b': (0.0, 0.8),
     'L2_ffn_bias': (0.0, 0.8),
     'L3_attn_bout': (0.0, 0.1),
     'L3_attn_gamma': (1.0, 0.6),
     'L3_attn_beta': (0.0, 0.8),
     'L3_ffn_br': (0.0, 0.8)}
    factors = {'L0_tok_bias': 8.0,
     'L0_tok_beta': 8.0,
     'L0_tok_moving_mean': 8.0,
     'L0_attn_inproj_w': 8.0,
     'L0_attn_conv_w': 8.0,
     'L0_attn_xproj_w': 8.0,
     'L0_attn_dtproj_w': 8.0,
     'L0_attn_dtproj_b': 8.0,
     'L0_attn_A_log': 8.0,
     'L0_attn_outproj_w': 8.0,
     'L0_ffn_wr': 8.0,
     'L0_ffn_w1': 8.0,
     'L0_ffn_w2': 8.0,
     'L1_attn_Wq': 7.542,
     'L1_attn_Wk': 7.602,
     'L1_attn_Wv': 6.878,
     'L1_ffn_hl_w': 4.75,
     'L1_ffn_hl_b': 8.0,
     'L1_ffn_wq': 8.0,
     'L1_ffn_wk': 8.0,
     'L1_ffn_wv': 8.0,
     'L1_ffn_gate_w': 8.0,
     'L1_ffn_gate_b': 40.959,
     'L1_ffn_fc1_w': 8.0,
     'L1_ffn_fc1_b': 25.171,
     'L1_ffn_fc2_w': 8.0,
     'L1_ffn_fc2_b': 8.0,
     'L1_ffn_fgate_w': 8.0,
     'L2_attn_Q': 2.99,
     'L2_attn_K': 2.899,
     'L2_attn_VO': 2.707,
     'L2_ffn_Wg': 8.0,
     'L2_ffn_bg': 22.95,
     'L2_ffn_W1': 8.0,
     'L2_ffn_b1': 30.451,
     'L2_ffn_W2': 8.0,
     'L2_ffn_b2': 33.444,
     'L3_attn_Wqkv': 8.0,
     'L3_attn_Wout': 8.0,
     'L3_ffn_gamma': 8.0,
     'L3_ffn_beta': 8.0,
     'L3_ffn_Wr': 8.0,
     'L3_ffn_W1': 8.0,
     'L3_ffn_b1': 61.799,
     'L3_ffn_W2': 8.0,
     'L3_ffn_b2': 64.0}
    for name, (base, spread) in spreads.items():
        noise = np.random.default_rng([zlib.crc32(name.encode()), seed]).standard_normal(out[name].shape)
        drawn = base * np.exp(spread * noise) if base else spread * noise
        out[name] = jnp.asarray(drawn.astype(out[name].dtype))
    for name, factor in factors.items():
        out[name] = (out[name] * factor).astype(out[name].dtype)
    return out
```

```python
from contextlib import ExitStack

import numpy as np
import concourse.bass as bass
from concourse import mybir

ALU = mybir.AluOpType
ACT = mybir.ActivationFunctionType
AX = mybir.AxisListType
F32 = mybir.dt.float32
BF16 = mybir.dt.bfloat16

P = 128
B, T_IN, C_IN = 8, 375, 128
TAPS = 3
T = T_IN - TAPS + 1
D = 64
NT = 3
TP = NT * P
LAST = T - 2 * P
TK = [P, P, LAST]
DI, NS, RK, KC, LAYERS = 256, 16, 16, 4, 2
KEEP = max(1, int(0.5 * T)) - 1
LH, LE, LD = 4, 4, 16
AH, AR = 8, 32
NE, EH = 8, 128
PADL = 4
BIG = 1.0e30
N_SEMAPHORES = 256


class Signal:

    def __init__(self, nc, ctx, name, buffers=2):
        self.sem = ctx.enter_context(nc.semaphore(name))
        self.buffers = buffers

    def at(self, step):
        return step + (self.buffers + 1)


class Chain:

    def __init__(self, nc, ctx, eng, name):
        self.sem = ctx.enter_context(nc.semaphore(name))
        self.eng, self.base, self.count = eng, 0, 0

    def loop(self, step, links):
        self.base, self.count, self.links = step * links, 0, links

    def close(self):
        assert self.count == self.links, self.count

    def link(self, ins):
        self.count += 1
        ins.then_inc(self.sem, 1)
        self.eng.wait_ge(self.sem, self.base + self.count)


def column_table():
    names = [("ident", P, P), ("tri_lower", P, NT * T), ("causal", P, P), ("head_mask", D, D), ("ones_row", 1, P)]
    names += [("tok_kernel", C_IN, TAPS * D)]
    for l in range(LAYERS):
        names += [(f"in_u{l}", D, DI), (f"in_g{l}", D, DI), (f"conv_b{l}", P, 2), (f"x_bc{l}", P, 2 * 96), (f"x_dt{l}", P, 2 * RK),
                  (f"dt_w{l}", RK, DI), (f"dt_b{l}", P, 2), (f"a_log{l}", P, 2 * NS), (f"skip{l}", P, 2), (f"out_w{l}", P, 2 * D)]
    names += [("route", D + 1, P), ("f0_w1", D + 1, 4 * D), ("f0_w2", P, 2 * D), ("f0_b2", 1, D)]
    late = len(names)
    names += [("a1_q", D + 1, D), ("a1_k", D + 1, D), ("a1_v", D + 1, D), ("a1_scale", D, 1)]
    names += [("hl_tok", D + 1, D), ("hl_wide", D + 1, P), ("wq_wide", P, LE * P), ("wk_wide", P, P), ("wv_wide", P, D)]
    names += [("gate_w", P, 2 * 8), ("fc1", D + 1, D), ("fc2", D + 1, D)]
    names += [("a2_q", D, AH * AR), ("a2_k", D, AH * AR), ("a2_vo", D, AH * D)]
    for m in ("m2", "m3"):
        names += [(f"{m}_gate", D + 1, NE), (f"{m}_w1", D + 1, NE * EH), (f"{m}_w2", EH, NE * D), (f"{m}_b2", 1, NE * D)]
    names += [("a3_qkv", D, 3 * D), ("a3_out", 8, 8 * D), ("a3_bias", 1, D)]
    table, at = {}, [0, 0]
    for i, (name, rows, cols) in enumerate(names):
        part = int(i >= late)
        table[name] = (part, rows, at[part], cols)
        at[part] += cols
    return table, at


def row_table():
    names = [("tok_bias", D), ("tok_beta", D), ("tok_mean", D), ("tok_var", D), ("pre_g", D), ("pre_b", D), ("post_g", D),
             ("post_b", D), ("norm_w0", D), ("norm_w1", D), ("normf_w", D), ("conv_w0", KC * DI), ("conv_w1", KC * DI),
             ("gate_b", LH * LE), ("ln_g", LD), ("ln_b", LD), ("fnorm_g", LD), ("fnorm_b", LD), ("fgate", LH * D),
             ("m2_bias", NE), ("a3_gamma", D), ("a3_beta", D), ("m3_gamma", D), ("m3_beta", D), ("countdown", NE)]
    table, at = {}, 0
    for name, cols in names:
        table[name] = (at, cols)
        at += cols
    return table, at


COLS, N_COLS = column_table()
ROWS, N_ROWS = row_table()


def tower(nc, x_in, w_in, w2_in, r_in, sel_in, out):
    with ExitStack() as whole:
        def sb(name, shape, dt=F32, ctx=whole):
            return ctx.enter_context(nc.sbuf_tensor(name, shape, dt))

        bearer = whole.enter_context(nc.semaphore("wait_bearer"))
        late_loaded = whole.enter_context(nc.semaphore("late_loaded"))

        def renew_semaphores():
            with ExitStack() as ctx:
                block = ctx.enter_context(nc.Block())

                @block.sync
                def _(sp):
                    sp.sem_clear(range(late_loaded.num + 1, N_SEMAPHORES))

        weights = [sb("early_weights", [P, N_COLS[0]])]
        rows = sb("rows", [P, N_ROWS])
        state = sb("state", [P, B, NT, D])
        normed = sb("normed", [P, B, NT, D])
        scratch = sb("scratch", [P, B, NT, D])
        stat = sb("stat", [P, 4, B * NT * LH])
        flipped = sb("flipped", [D + 1, B, PADL + TP])
        ident_bf = sb("ident_bf", [P, P], BF16)
        causal_bf = sb("causal_bf", [P, P], BF16)

        def pairs(t):
            rest = " ".join("xyz"[0:len(t.shape) - 2])
            return t[tuple([slice(None)] * len(t.shape))].rearrange(f"p (c s) {rest} -> p c s {rest}", s=2)

        def W(name, lo=0, hi=None, rows_=None):
            part, r, at, cols = COLS[name]
            return weights[part][0:(rows_ or r), at + lo:at + (cols if hi is None else hi)]

        def R(name, parts=P):
            at, cols = ROWS[name]
            return rows[0:parts, at:at + cols]

        ident = W("ident")

        with ExitStack() as ctx:
            x_sb = sb("x_sb", [C_IN, B, TP + TAPS - 1], F32, ctx)
            x_sign = sb("x_sign", [C_IN, B, TP + TAPS - 1], BF16, ctx)
            k_sign = sb("k_sign", [C_IN, TAPS * D], BF16, ctx)
            affine = sb("affine", [P, 4, D], F32, ctx)
            conv_ps = ctx.enter_context(nc.psum_tensor("conv_ps", [P, 2, 512], F32))
            loaded = ctx.enter_context(nc.semaphore("tok_loaded"))
            signs = ctx.enter_context(nc.semaphore("tok_signs"))
            root = ctx.enter_context(nc.semaphore("tok_root"))
            var_ready = ctx.enter_context(nc.semaphore("tok_var_ready"))
            conv_done = Signal(nc, ctx, "tok_conv_done")
            placed = Signal(nc, ctx, "tok_placed")
            block = ctx.enter_context(nc.Block())

            @block.sync
            def _(sp):
                sp.dma_start(x_sb[:, :, :], x_in).then_inc(loaded, 16)
                sp.dma_start(weights[0][:, :], w_in).then_inc(loaded, 16)
                sp.dma_start(rows[:, :], r_in.rearrange("(a n) -> a n", a=1).broadcast_to([P, N_ROWS])).then_inc(loaded, 16)

            @block.scalar
            def _(act):
                act.wait_ge(var_ready, 1)
                act.activation(affine[:, 1, :], affine[:, 0, :], ACT.Sqrt).then_inc(root, 1)

            @block.vector
            def _(dve):
                chain = Chain(nc, ctx, dve, "tok_chain")
                dve.sem_inc(placed.sem, placed.buffers)
                dve.wait_ge(loaded, 48)
                dve.tensor_scalar(affine[:, 0, :], R("tok_var"), 1e-3, None, ALU.add).then_inc(var_ready, 1)
                dve.tensor_scalar(k_sign[:, :], W("tok_kernel"), 0.0, 0.5, ALU.is_ge, ALU.subtract).then_inc(signs, 1)
                dve.tensor_scalar(x_sign[:, :, :], x_sb[:, :, :], 0.0, 0.5, ALU.is_ge, ALU.subtract).then_inc(signs, 1)
                dve.tensor_copy(ident_bf[:, :], ident)
                dve.tensor_copy(causal_bf[:, :], W("causal"))
                dve.memset(flipped[D:D + 1, :, :], 1.0)
                dve.memset(flipped[0:D, :, 0:PADL], 0.0)
                chain.link(dve.tensor_tensor(affine[:, 3, :], R("tok_bias"), R("tok_mean"), ALU.subtract))
                dve.wait_ge(root, 1)
                chain.link(dve.reciprocal(affine[:, 2, :], affine[:, 1, :]))
                chain.link(dve.tensor_tensor(affine[:, 3, :], affine[:, 3, :], affine[:, 2, :], ALU.mult))
                chain.link(dve.tensor_tensor(affine[:, 3, :], affine[:, 3, :], R("tok_beta"), ALU.add))
                chain.link(dve.tensor_scalar(affine[:, 2, :], affine[:, 2, :], 4.0, None, ALU.mult))
                scale = affine[:, 2:3, :].broadcast_to([P, NT, D])
                shift = affine[:, 3:4, :].broadcast_to([P, NT, D])
                mul_sem = Chain(nc, ctx, dve, "tok_scaled")
                with dve.Fori(0, B // 2) as c:
                    b = 2 * c
                    mul_sem.loop(c, 2)
                    for s in range(2):
                        dve.wait_ge(conv_done.sem, conv_done.at(b + s))
                        ps = conv_ps[:, s, 0:NT * D].rearrange("p (j d) -> p j d", d=D)
                        mul_sem.link(dve.tensor_tensor(pairs(state)[:, c, s, :, :], ps, scale, ALU.mult))
                        dve.tensor_tensor(pairs(state)[:, c, s, :, :], pairs(state)[:, c, s, :, :], shift, ALU.add).then_inc(placed.sem, 1)
                    mul_sem.close()

            @block.tensor
            def _(pe):
                pe.sem_inc(conv_done.sem, conv_done.buffers)
                pe.wait_ge(signs, 2)
                with pe.Fori(0, B // 2) as c:
                    b = 2 * c
                    for s in range(2):
                        pe.wait_ge(placed.sem, placed.at(b + s - 2))
                        pe.sem_inc(bearer, 1)
                        for j in range(NT):
                            for k in range(TAPS):
                                mm = pe.matmul(conv_ps[:, s, j * D:(j + 1) * D], pairs(x_sign)[:, c, s, j * P + k:j * P + k + P],
                                               k_sign[:, k * D:(k + 1) * D], start=(k == 0), stop=(k == TAPS - 1))
                        mm.then_inc(conv_done.sem, 1)

        def normalise(name, src, dst, eps, centre=True, gain=None, shift=None, add_to=None, width=D):
            with ExitStack() as ctx:
                group = B * NT * D // width
                root = ctx.enter_context(nc.semaphore(f"{name}_root"))
                spread = ctx.enter_context(nc.semaphore(f"{name}_spread"))
                block = ctx.enter_context(nc.Block())

                def v(t):
                    return t[:, :, :, :].rearrange("p b j (g w) -> p (b j g) w", w=width)

                def wide(k):
                    return stat[:, k, 0:group].unsqueeze(2).broadcast_to([P, group, width])

                @block.vector
                def _(dve):
                    chain = Chain(nc, ctx, dve, f"{name}_chain")
                    centred = src
                    if centre:
                        chain.link(dve.tensor_reduce(stat[:, 0, 0:group], v(src), AX.X, ALU.add))
                        chain.link(dve.tensor_scalar(stat[:, 0, 0:group], stat[:, 0, 0:group], 1.0 / width, None, ALU.mult))
                        chain.link(dve.tensor_tensor(v(dst), v(src), wide(0), ALU.subtract))
                        centred = dst
                    chain.link(dve.tensor_tensor(v(scratch), v(centred), v(centred), ALU.mult))
                    chain.link(dve.tensor_reduce(stat[:, 1, 0:group], v(scratch), AX.X, ALU.add))
                    dve.tensor_scalar(stat[:, 1, 0:group], stat[:, 1, 0:group], 1.0 / width, eps, ALU.mult, ALU.add).then_inc(spread, 1)
                    dve.wait_ge(root, 1)
                    chain.link(dve.reciprocal(stat[:, 3, 0:group], stat[:, 2, 0:group]))
                    chain.link(dve.tensor_tensor(v(dst), v(centred), wide(3), ALU.mult))
                    for vec, op in ((gain, ALU.mult), (shift, ALU.add)):
                        if vec is not None:
                            chain.link(dve.tensor_tensor(v(dst), v(dst), R(vec).unsqueeze(1).broadcast_to([P, group, width]), op))
                    if add_to is not None:
                        chain.link(dve.tensor_tensor(v(add_to), v(add_to), v(dst), ALU.add))

                @block.scalar
                def _(act):
                    act.wait_ge(spread, 1)
                    act.activation(stat[:, 2, 0:group], stat[:, 1, 0:group], ACT.Sqrt).then_inc(root, 1)

        def flip(name, src, logits=None, gate=None):
            with ExitStack() as ctx:
                tile = sb(f"{name}_tile", [P, 2, NT, D], F32, ctx)
                turned = sb(f"{name}_turned", [D + 1, 2, TP], F32, ctx)
                ps = ctx.enter_context(nc.psum_tensor(f"{name}_ps", [P, 2, 512], F32))
                lps = ctx.enter_context(nc.psum_tensor(f"{name}_lps", [P, 2, 512], F32))
                staged = Signal(nc, ctx, f"{name}_staged")
                turned_ps = Signal(nc, ctx, f"{name}_turned_ps")
                turned_sb = Signal(nc, ctx, f"{name}_turned_sb")
                kept = Signal(nc, ctx, f"{name}_kept")
                logit_ps = Signal(nc, ctx, f"{name}_logit_ps")
                logit_sb = Signal(nc, ctx, f"{name}_logit_sb")
                ones = ctx.enter_context(nc.semaphore(f"{name}_ones"))
                block = ctx.enter_context(nc.Block())

                @block.gpsimd
                def _(pool):
                    pool.sem_inc(staged.sem, staged.buffers)
                    pool.memset(turned[D:D + 1, :, :], 1.0).then_inc(ones, 1)
                    pool.wait_ge(ones, 1)
                    with pool.Fori(0, B // 2) as c:
                        b = 2 * c
                        for s in range(2):
                            pool.wait_ge(turned_ps.sem, turned_ps.at(b + s - 2))
                            pool.tensor_copy(tile[:, s, :, :], pairs(src)[:, c, s, :, :]).then_inc(staged.sem, 1)

                @block.tensor
                def _(pe):
                    pe.sem_inc(turned_ps.sem, turned_ps.buffers)
                    pe.sem_inc(logit_ps.sem, logit_ps.buffers)
                    pe.wait_ge(ones, 1)
                    with pe.Fori(0, B // 2) as c:
                        b = 2 * c
                        for s in range(2):
                            pe.wait_ge(staged.sem, staged.at(b + s))
                            pe.sem_inc(bearer, 1)
                            pe.wait_ge(turned_sb.sem, turned_sb.at(b + s - 2))
                            pe.sem_inc(bearer, 1)
                            for j in range(NT):
                                mm = pe.transpose(ps[0:D, s, j * P:(j + 1) * P], tile[:, s, j, :], ident)
                            mm.then_inc(turned_ps.sem, 1)
                        for s in range(2):
                            pe.wait_ge(turned_sb.sem, turned_sb.at(b + s))
                            pe.sem_inc(bearer, 1)
                            if logits is not None:
                                pe.wait_ge(logit_sb.sem, logit_sb.at(b + s - 2))
                                pe.sem_inc(bearer, 1)
                                for j in range(NT):
                                    mm = pe.matmul(lps[:, s, j * NE:(j + 1) * NE], turned[:, s, j * P:(j + 1) * P], W(gate),
                                                   start=True, stop=True)
                                mm.then_inc(logit_ps.sem, 1)

                @block.scalar
                def _(act):
                    act.sem_inc(turned_sb.sem, turned_sb.buffers)
                    with act.Fori(0, B // 2) as c:
                        b = 2 * c
                        for s in range(2):
                            act.wait_ge(turned_ps.sem, turned_ps.at(b + s))
                            act.sem_inc(bearer, 1)
                            act.wait_ge(kept.sem, kept.at(b + s - 2))
                            act.sem_inc(bearer, 1)
                            if logits is not None:
                                act.wait_ge(logit_ps.sem, logit_ps.at(b + s - 2))
                                act.sem_inc(bearer, 1)
                            act.activation(turned[0:D, s, :], ps[0:D, s, 0:TP], ACT.Copy).then_inc(turned_sb.sem, 1)

                @block.vector
                def _(dve):
                    dve.sem_inc(kept.sem, kept.buffers)
                    dve.sem_inc(logit_sb.sem, logit_sb.buffers)
                    with dve.Fori(0, B // 2) as c:
                        b = 2 * c
                        for s in range(2):
                            dve.wait_ge(turned_sb.sem, turned_sb.at(b + s))
                            dve.tensor_copy(pairs(flipped)[0:D, c, s, PADL:PADL + TP], turned[0:D, s, :]).then_inc(kept.sem, 1)
                        for s in range(2):
                            if logits is not None:
                                dve.wait_ge(logit_ps.sem, logit_ps.at(b + s))
                                dve.tensor_copy(pairs(logits)[:, c, s, :, :], lps[:, s, 0:NT * NE].rearrange("p (j e) -> p j e", e=NE))\
                                   .then_inc(logit_sb.sem, 1)

        def store():
            with ExitStack() as ctx:
                stored = ctx.enter_context(nc.semaphore("stored"))
                block = ctx.enter_context(nc.Block())

                @block.sync
                def _(sp):
                    for j in range(NT):
                        sp.dma_start(out[:, j * P:j * P + TK[j], :].rearrange("b p d -> p b d"), state[0:TK[j], :, j, :]).then_inc(stored, 16)
                    sp.wait_ge(stored, 16 * NT)

        normalise("a0_ln", state, normed, 1e-5)
        with ExitStack() as mamba:
            mix = sb("mix", [P, B, NT, D], F32, mamba)
            conv_in = sb("conv_in", [P, 2, B, T], F32, mamba)
            gates = sb("gates", [P, 2, B, T], F32, mamba)
            steps = sb("steps", [P, 2, B, T], F32, mamba)
            drive = sb("drive", [P, 2, B, T], F32, mamba)
            bc_parts = sb("bc_parts", [96, B, T], BF16, mamba)
            spread = sb("spread", [96, 2 * NS, P], BF16, mamba)
            tap_w = sb("tap_w", [D, KC, DI], F32, mamba)
            decay = sb("decay", [P, 2, 2 * NS], F32, mamba)
            skip = sb("skip", [P, 2, P], F32, mamba)
            normalise("a0_pre", normed, mix, 1e-5, gain="pre_g", shift="pre_b")

            with ExitStack() as ctx:
                sel_loaded = ctx.enter_context(nc.semaphore("sel_loaded"))
                block = ctx.enter_context(nc.Block())
                sel_f32 = drive[0:96, :, :, :].rearrange("p a b t -> p (a b t)")[:, 0:2 * NS * P]

                @block.sync
                def _(sp):
                    sp.dma_start(sel_f32, sel_in.rearrange("k c m -> k (c m)")).then_inc(sel_loaded, 16)

                @block.vector
                def _(dve):
                    dve.wait_ge(sel_loaded, 16)
                    dve.tensor_copy(spread[:, :, :].rearrange("k c m -> k (c m)"), sel_f32)

            def project(l):
                with ExitStack() as ctx:
                    low_rank = sb(f"low_rank{l}", [RK, T], F32, ctx)
                    rest = sb(f"rest{l}", [96, T], F32, ctx)
                    middle = sb(f"middle{l}", [96, T], BF16, ctx)
                    u_ps = ctx.enter_context(nc.psum_tensor(f"u_ps{l}", [P, 2, 512], F32))
                    g_ps = ctx.enter_context(nc.psum_tensor(f"g_ps{l}", [P, 2, 512], F32))
                    bc_ps = ctx.enter_context(nc.psum_tensor(f"bc_ps{l}", [P, 512], F32))
                    low_ps = ctx.enter_context(nc.psum_tensor(f"low_ps{l}", [P, 512], F32))
                    dt_ps = ctx.enter_context(nc.psum_tensor(f"dt_ps{l}", [P, 2, 512], F32))
                    exps = ctx.enter_context(nc.semaphore(f"decay_exp{l}"))
                    taps = ctx.enter_context(nc.semaphore(f"tap_weights{l}"))

                    def sig(n):
                        return Signal(nc, ctx, f"{n}{l}", 1)

                    u_sum, g_sum, u_done, g_done = sig("u_sum"), sig("g_sum"), sig("u_done"), sig("g_done")
                    bc_sum, low_sum, low_done, dt_sum = sig("bc_sum"), sig("low_sum"), sig("low_done"), sig("dt_sum")
                    bc_read, bc_done, dt_done = sig("bc_read"), sig("bc_done"), sig("dt_done")
                    block = ctx.enter_context(nc.Block())

                    @block.tensor
                    def _(pe):
                        for x in (u_sum, g_sum, bc_sum, low_sum, dt_sum):
                            pe.sem_inc(x.sem, x.buffers)
                        pe.wait_ge(taps, 1)
                        with pe.Fori(0, B) as b:
                            pe.wait_ge(u_done.sem, u_done.at(b - 1))
                            pe.sem_inc(bearer, 1)
                            for h in range(2):
                                for k in range(KC):
                                    at = PADL - (KC - 1) + k
                                    mm = pe.matmul(u_ps[:, h, 0:T], tap_w[:, k, h * P:(h + 1) * P], flipped[0:D, b, at:at + T],
                                                   start=(k == 0), stop=(k == KC - 1))
                            mm.then_inc(u_sum.sem, 1)
                            pe.wait_ge(g_done.sem, g_done.at(b - 1))
                            pe.sem_inc(bearer, 1)
                            for h in range(2):
                                mm = pe.matmul(g_ps[:, h, 0:T], W(f"in_g{l}", h * P, (h + 1) * P), flipped[0:D, b, PADL:PADL + T],
                                               start=True, stop=True)
                            mm.then_inc(g_sum.sem, 1)
                            pe.wait_ge(u_done.sem, u_done.at(b))
                            pe.sem_inc(bearer, 1)
                            pe.wait_ge(low_done.sem, low_done.at(b - 1))
                            pe.sem_inc(bearer, 1)
                            for h in range(2):
                                mm = pe.matmul(low_ps[0:RK, 0:T], W(f"x_dt{l}", h * RK, (h + 1) * RK), conv_in[:, h, b, :],
                                               start=(h == 0), stop=(h == 1))
                            mm.then_inc(low_sum.sem, 1)
                            pe.wait_ge(bc_read.sem, bc_read.at(b - 1))
                            pe.sem_inc(bearer, 1)
                            for h in range(2):
                                mm = pe.matmul(bc_ps[0:96, 0:T], W(f"x_bc{l}", h * 96, (h + 1) * 96), conv_in[:, h, b, :],
                                               start=(h == 0), stop=(h == 1))
                            mm.then_inc(bc_sum.sem, 1)
                            pe.wait_ge(low_done.sem, low_done.at(b))
                            pe.sem_inc(bearer, 1)
                            pe.wait_ge(dt_done.sem, dt_done.at(b - 1))
                            pe.sem_inc(bearer, 1)
                            for h in range(2):
                                mm = pe.matmul(dt_ps[:, h, 0:T], W(f"dt_w{l}", h * P, (h + 1) * P), low_rank[:, :], start=True, stop=True)
                            mm.then_inc(dt_sum.sem, 1)

                    @block.scalar
                    def _(act):
                        for x in (u_done, g_done, low_done):
                            act.sem_inc(x.sem, x.buffers)
                        act.activation(decay[:, 0, :], W(f"a_log{l}"), ACT.Exp).then_inc(exps, 1)
                        with act.Fori(0, B) as b:
                            act.wait_ge(u_sum.sem, u_sum.at(b))
                            act.sem_inc(bearer, 1)
                            for h in range(2):
                                ins = act.activation(conv_in[:, h, b, :], u_ps[:, h, 0:T], ACT.Silu, bias=W(f"conv_b{l}", h, h + 1))
                            ins.then_inc(u_done.sem, 1)
                            act.wait_ge(g_sum.sem, g_sum.at(b))
                            act.sem_inc(bearer, 1)
                            for h in range(2):
                                ins = act.activation(gates[:, h, b, :], g_ps[:, h, 0:T], ACT.Silu)
                            ins.then_inc(g_done.sem, 1)
                            act.wait_ge(low_sum.sem, low_sum.at(b))
                            act.sem_inc(bearer, 1)
                            act.wait_ge(dt_sum.sem, dt_sum.at(b - 1))
                            act.sem_inc(bearer, 1)
                            act.activation(low_rank[:, :], low_ps[0:RK, 0:T], ACT.Copy).then_inc(low_done.sem, 1)

                    @block.vector
                    def _(dve):
                        chain = Chain(nc, ctx, dve, f"project_chain{l}")
                        for x in (bc_read, bc_done, dt_done):
                            dve.sem_inc(x.sem, x.buffers)
                        taps_row = R(f"conv_w{l}", D).rearrange("p (k d) -> p k d", k=KC)
                        dve.tensor_tensor(tap_w[:, :, :], taps_row, W(f"in_u{l}").unsqueeze(1).broadcast_to([D, KC, DI]), ALU.mult)\
                           .then_inc(taps, 1)
                        for h in range(2):
                            dve.tensor_scalar(skip[:, h, :], ident, W(f"skip{l}", h, h + 1), None, ALU.mult)
                        dve.wait_ge(exps, 1)
                        dve.tensor_scalar(decay[:, 1, :], decay[:, 0, :], -1.0, None, ALU.mult)
                        with dve.Fori(0, B) as b:
                            chain.loop(b, 4)
                            dve.wait_ge(bc_sum.sem, bc_sum.at(b))
                            chain.link(dve.tensor_copy(bc_parts[:, b, :], bc_ps[0:96, 0:T]))
                            chain.link(dve.tensor_tensor(rest[:, :], bc_ps[0:96, 0:T], bc_parts[:, b, :], ALU.subtract))
                            dve.tensor_copy(bc_parts[32:64, b, :], rest[32:64, :])
                            chain.link(dve.tensor_copy(middle[64:96, :], rest[64:96, :]))
                            chain.link(dve.tensor_tensor(bc_parts[64:96, b, :], rest[64:96, :], middle[64:96, :], ALU.subtract))
                            chain.close()
                            dve.sem_inc(bc_read.sem, 1)
                            dve.wait_ge(dt_sum.sem, dt_sum.at(b))
                            for h in range(2):
                                ins = dve.tensor_scalar(steps[:, h, b, :], dt_ps[:, h, 0:T], W(f"dt_b{l}", h, h + 1), None, ALU.add)
                            ins.then_inc(dt_done.sem, 1)

            def softplus(l):
                batches = B // 2
                with ExitStack() as ctx:
                    def flat(t):
                        return t[:, :, :, :].rearrange("p b j d -> p (b j d)")[:, 0:batches * T].rearrange("p (b t) -> p b t", b=batches)

                    one_plus, logs = flat(scratch), flat(normed)
                    log_ready = ctx.enter_context(nc.semaphore(f"log_ready{l}"))
                    log_used = ctx.enter_context(nc.semaphore(f"log_used{l}"))
                    block = ctx.enter_context(nc.Block())
                    chunks = [(h, slice(batches * k, batches * k + batches)) for h in range(2) for k in range(2)]

                    @block.scalar
                    def _(act):
                        chain = Chain(nc, ctx, act, f"softplus_chain{l}")
                        for i, (h, bs) in enumerate(chunks):
                            chain.link(act.activation(drive[:, h, bs, :], steps[:, h, bs, :], ACT.Abs))
                            chain.link(act.activation(drive[:, h, bs, :], drive[:, h, bs, :], ACT.Exp, scale=-1.0))
                            if i > 0:
                                act.wait_ge(log_used, i)
                            chain.link(act.activation(one_plus, drive[:, h, bs, :], ACT.Identity, bias=1.0))
                            act.activation(logs, one_plus, ACT.Ln).then_inc(log_ready, 1)

                    @block.vector
                    def _(dve):
                        chain = Chain(nc, ctx, dve, f"steps_chain{l}")
                        for i, (h, bs) in enumerate(chunks):
                            dve.wait_ge(log_ready, i + 1)
                            chain.link(dve.scalar_tensor_tensor(one_plus, one_plus, 1.0, drive[:, h, bs, :], ALU.subtract, ALU.subtract))
                            chain.link(dve.scalar_tensor_tensor(steps[:, h, bs, :], steps[:, h, bs, :], 0.0, logs, ALU.max, ALU.add))
                            dve.tensor_tensor(steps[:, h, bs, :], steps[:, h, bs, :], one_plus, ALU.subtract).then_inc(log_used, 1)
                            dve.wait_ge(log_used, i + 1)
                            dve.tensor_tensor(drive[:, h, bs, :], steps[:, h, bs, :], conv_in[:, h, bs, :], ALU.mult)

            def scan(l):
                units = 2 * NS
                with ExitStack() as ctx:
                    c_all = sb(f"c_all{l}", [P, 2, T], F32, ctx)
                    keep = sb(f"keep{l}", [P, 4, T], F32, ctx)
                    add = scratch[:, :, :, :].rearrange("p b j d -> p (b j d)")[:, 0:4 * T].rearrange("p (s t) -> p s t", s=4)
                    seen = normed[:, :, :, :].rearrange("p b j d -> p (b j d)")[:, 0:4 * T].rearrange("p (s t) -> p s t", s=4)
                    hidden = sb(f"hidden{l}", [P, 4, T], F32, ctx)
                    gated = sb(f"gated{l}", [P, 2, TP], F32, ctx)
                    b_ps = ctx.enter_context(nc.psum_tensor(f"b_ps{l}", [P, 2, 512], F32))
                    c_ps = ctx.enter_context(nc.psum_tensor(f"c_ps{l}", [P, 2, 512], F32))
                    y_ps = ctx.enter_context(nc.psum_tensor(f"y_ps{l}", [P, 2, 512], F32))
                    o_ps = ctx.enter_context(nc.psum_tensor(f"o_ps{l}", [P, 512], F32))

                    def sig(n, buffers):
                        return Signal(nc, ctx, f"{n}{l}", buffers)

                    b_spread, c_spread, c_copied = sig("b_spread", 2), sig("c_spread", 2), sig("c_copied", 2)
                    keep_ready, add_ready, hidden_ready = sig("keep_ready", 4), sig("add_ready", 4), sig("hidden_ready", 4)
                    seen_ready, seen_summed = sig("seen_ready", 4), sig("seen_summed", 4)
                    gated_ready, o_ready, mixed = sig("gated_ready", 1), sig("o_ready", 1), sig("mixed", 1)
                    block = ctx.enter_context(nc.Block())

                    @block.tensor
                    def _(pe):
                        for x in (b_spread, c_spread, seen_summed, o_ready):
                            pe.sem_inc(x.sem, x.buffers)

                        def spread_out(b, n):
                            pe.wait_ge(add_ready.sem, add_ready.at(units * b + 2 * (n - 2) + 1))
                            pe.sem_inc(bearer, 1)
                            pe.matmul(b_ps[:, n % 2, 0:T], spread[:, n, :], bc_parts[:, b, :], start=True, stop=True).then_inc(b_spread.sem, 1)
                            pe.wait_ge(c_copied.sem, c_copied.at(NS * b + n - 2))
                            pe.sem_inc(bearer, 1)
                            pe.matmul(c_ps[:, n % 2, 0:T], spread[:, NS + n, :], bc_parts[:, b, :], start=True, stop=True).then_inc(c_spread.sem, 1)

                        with pe.Fori(0, B) as b:
                            spread_out(b, 0)
                            spread_out(b, 1)
                            pe.wait_ge(gated_ready.sem, gated_ready.at(b - 1))
                            pe.sem_inc(bearer, 1)
                            for h in range(2):
                                pe.matmul(y_ps[:, h, 0:T], skip[:, h, :], conv_in[:, h, b, :], start=True, stop=False)
                            for n in range(NS):
                                for h in range(2):
                                    pe.wait_ge(seen_ready.sem, seen_ready.at(units * b + 2 * n + h))
                                    pe.sem_inc(bearer, 1)
                                    pe.matmul(y_ps[:, h, 0:T], ident, seen[:, (2 * n + h) % 4, :], start=False, stop=(n == NS - 1))\
                                      .then_inc(seen_summed.sem, 1)
                                if n + 2 < NS:
                                    spread_out(b, n + 2)
                            pe.wait_ge(gated_ready.sem, gated_ready.at(b))
                            pe.sem_inc(bearer, 1)
                            pe.wait_ge(mixed.sem, mixed.at(b - 1))
                            pe.sem_inc(bearer, 1)
                            for j in range(NT):
                                for h in range(2):
                                    mm = pe.matmul(o_ps[:, j * D:(j + 1) * D], gated[:, h, j * P:(j + 1) * P], W(f"out_w{l}", h * D, (h + 1) * D),
                                                   start=(h == 0), stop=(h == 1))
                            mm.then_inc(o_ready.sem, 1)

                    @block.scalar
                    def _(act):
                        for x in (c_copied, keep_ready):
                            act.sem_inc(x.sem, x.buffers)
                        with act.Fori(0, B) as b:
                            for n in range(NS):
                                act.wait_ge(c_spread.sem, c_spread.at(NS * b + n))
                                act.sem_inc(bearer, 1)
                                act.wait_ge(seen_ready.sem, seen_ready.at(units * b + 2 * (n - 2) + 1))
                                act.sem_inc(bearer, 1)
                                act.activation(c_all[:, n % 2, :], c_ps[:, n % 2, 0:T], ACT.Copy).then_inc(c_copied.sem, 1)
                                for h in range(2):
                                    u = 2 * n + h
                                    act.wait_ge(hidden_ready.sem, hidden_ready.at(units * b + u - 4))
                                    act.sem_inc(bearer, 1)
                                    act.activation(keep[:, u % 4, :], steps[:, h, b, :], ACT.Exp, scale=decay[:, 1, h * NS + n:h * NS + n + 1])\
                                       .then_inc(keep_ready.sem, 1)

                    @block.vector
                    def _(dve):
                        for x in (add_ready, hidden_ready, gated_ready, mixed):
                            dve.sem_inc(x.sem, x.buffers)
                        dve.memset(gated[:, :, T:TP], 0.0)

                        def inputs(b, u):
                            n, h = u // 2, u % 2
                            dve.wait_ge(b_spread.sem, b_spread.at(NS * b + n))
                            dve.wait_ge(hidden_ready.sem, hidden_ready.at(units * b + u - 4))
                            dve.tensor_tensor(add[:, u % 4, :], drive[:, h, b, :], b_ps[:, n % 2, 0:T], ALU.mult).then_inc(add_ready.sem, 1)

                        with dve.Fori(0, B) as b:
                            inputs(b, 0)
                            for u in range(units):
                                if u + 1 < units:
                                    inputs(b, u + 1)
                                dve.wait_ge(keep_ready.sem, keep_ready.at(units * b + u))
                                dve.wait_ge(add_ready.sem, add_ready.at(units * b + u))
                                dve.wait_ge(seen_ready.sem, seen_ready.at(units * b + u - 4))
                                dve.tensor_tensor_scan(hidden[:, u % 4, :], keep[:, u % 4, :], add[:, u % 4, :], 0.0, ALU.mult, ALU.add)\
                                   .then_inc(hidden_ready.sem, 1)
                            dve.wait_ge(seen_summed.sem, seen_summed.at(units * b + units - 1))
                            dve.wait_ge(o_ready.sem, o_ready.at(b - 1))
                            for h in range(2):
                                ins = dve.tensor_tensor(gated[:, h, 0:T], gates[:, h, b, :], y_ps[:, h, 0:T], ALU.mult)
                            ins.then_inc(gated_ready.sem, 1)
                            dve.wait_ge(o_ready.sem, o_ready.at(b))
                            dve.tensor_tensor(mix[:, b, :, :], mix[:, b, :, :], o_ps[:, 0:NT * D].rearrange("p (j d) -> p j d", d=D), ALU.add)\
                               .then_inc(mixed.sem, 1)

                    @block.gpsimd
                    def _(pool):
                        pool.sem_inc(seen_ready.sem, seen_ready.buffers)
                        with pool.Fori(0, B) as b:
                            for u in range(units):
                                pool.wait_ge(hidden_ready.sem, hidden_ready.at(units * b + u))
                                if u % 2 == 0:
                                    pool.wait_ge(c_copied.sem, c_copied.at(NS * b + u // 2))
                                pool.wait_ge(seen_summed.sem, seen_summed.at(units * b + u - 4))
                                pool.tensor_tensor(seen[:, u % 4, :], hidden[:, u % 4, :], c_all[:, (u // 2) % 2, :], ALU.mult)\
                                    .then_inc(seen_ready.sem, 1)

            for l in range(LAYERS):
                normalise(f"rms{l}", mix, normed, 1e-5, centre=False, gain=f"norm_w{l}")
                flip(f"a0_flip{l}", normed)
                project(l)
                softplus(l)
                scan(l)
            normalise("a0_normf", mix, normed, 1e-5, centre=False, gain="normf_w")
            normalise("a0_post", normed, mix, 1e-5, gain="post_g", shift="post_b", add_to=state)

        renew_semaphores()
        weights.append(sb("late_weights", [P, N_COLS[1]]))
        with ExitStack() as ctx:
            block = ctx.enter_context(nc.Block())

            @block.sync
            def _(sp):
                sp.dma_start(weights[1][:, :], w2_in).then_inc(late_loaded, 16)

        normalise("f0_ln", state, normed, 1e-5)
        flip("f0_flip", normed)
        with ExitStack() as ctx:
            score = sb("score", [P, 2, TP], F32, ctx)
            compared = sb("compared", [P, T], F32, ctx)
            count = sb("count", [P, 2, 3, NT], F32, ctx)
            factor = sb("factor", [P, 2, NT], F32, ctx)
            ffn_hidden = sb("ffn_hidden", [P, 2, 2, TP], F32, ctx)
            routed = sb("routed", [P, 2, NT, D], F32, ctx)
            score_ps = ctx.enter_context(nc.psum_tensor("score_ps", [P, 2, 512], F32))
            hidden_ps = ctx.enter_context(nc.psum_tensor("hidden_ps", [P, 2, 2, 512], F32))
            out_ps = ctx.enter_context(nc.psum_tensor("out_ps", [P, 2, 512], F32))
            score_sum, score_read = Signal(nc, ctx, "score_sum"), Signal(nc, ctx, "score_read")
            hidden_sum, hidden_done = Signal(nc, ctx, "hidden_sum"), Signal(nc, ctx, "hidden_done")
            out_sum, out_read = Signal(nc, ctx, "out_sum"), Signal(nc, ctx, "out_read")
            ranked = Signal(nc, ctx, "ranked")
            block = ctx.enter_context(nc.Block())

            @block.tensor
            def _(pe):
                for x in (score_sum, hidden_sum, out_sum):
                    pe.sem_inc(x.sem, x.buffers)
                with pe.Fori(0, B // 2) as c:
                    b = 2 * c
                    for s in range(2):
                        x = pairs(flipped)[0:D + 1, c, s, PADL:PADL + TP]
                        pe.wait_ge(score_read.sem, score_read.at(b + s - 2))
                        pe.sem_inc(bearer, 1)
                        pe.matmul(score_ps[:, s, 0:TP], W("route"), x, start=True, stop=True).then_inc(score_sum.sem, 1)
                        pe.wait_ge(hidden_done.sem, hidden_done.at(b + s - 2))
                        pe.sem_inc(bearer, 1)
                        for h in range(2):
                            mm = pe.matmul(hidden_ps[:, s, h, 0:TP], W("f0_w1", h * P, (h + 1) * P), x, start=True, stop=True)
                        mm.then_inc(hidden_sum.sem, 1)
                    for s in range(2):
                        pe.wait_ge(hidden_done.sem, hidden_done.at(b + s))
                        pe.sem_inc(bearer, 1)
                        pe.wait_ge(out_read.sem, out_read.at(b + s - 2))
                        pe.sem_inc(bearer, 1)
                        for j in range(NT):
                            o = out_ps[:, s, j * D:(j + 1) * D]
                            pe.matmul(o, W("ones_row"), W("f0_b2"), start=True, stop=False)
                            for h in range(2):
                                mm = pe.matmul(o, ffn_hidden[:, s, h, j * P:(j + 1) * P], W("f0_w2", h * D, (h + 1) * D), start=False, stop=(h == 1))
                        mm.then_inc(out_sum.sem, 1)

            @block.scalar
            def _(act):
                act.sem_inc(score_read.sem, score_read.buffers)
                act.sem_inc(hidden_done.sem, hidden_done.buffers)
                with act.Fori(0, B // 2) as c:
                    b = 2 * c
                    for s in range(2):
                        act.wait_ge(score_sum.sem, score_sum.at(b + s))
                        act.sem_inc(bearer, 1)
                        act.wait_ge(ranked.sem, ranked.at(b + s - 2))
                        act.sem_inc(bearer, 1)
                        act.activation(score[:, s, :], score_ps[:, s, 0:TP], ACT.Copy).then_inc(score_read.sem, 1)
                        act.wait_ge(hidden_sum.sem, hidden_sum.at(b + s))
                        act.sem_inc(bearer, 1)
                        act.wait_ge(out_sum.sem, out_sum.at(b + s - 2))
                        act.sem_inc(bearer, 1)
                        act.activation(ffn_hidden[:, s, :, :], hidden_ps[:, s, :, 0:TP], ACT.Gelu_apprx_tanh).then_inc(hidden_done.sem, 1)

            @block.vector
            def _(dve):
                chain = Chain(nc, ctx, dve, "route_chain")
                dve.sem_inc(ranked.sem, ranked.buffers)
                dve.sem_inc(out_read.sem, out_read.buffers)
                with dve.Fori(0, B // 2) as c:
                    b = 2 * c
                    chain.loop(c, 2 * (3 * NT + 2 + NT))
                    for s in range(2):
                        dve.wait_ge(score_read.sem, score_read.at(b + s))
                        for j in range(NT):
                            own = count[:, s, 2, j:j + 1]
                            chain.link(dve.scalar_tensor_tensor(compared[:, 0:P], score[:, s, j * P:(j + 1) * P], 1.0, ident, ALU.mult, ALU.mult,
                                                                accum_out=own))
                            chain.link(dve.tensor_scalar(compared[:, :], score[:, s, 0:T], own, None, ALU.is_gt, ALU.add,
                                                         accum_out=count[:, s, 0, j:j + 1]))
                            chain.link(dve.scalar_tensor_tensor(compared[:, :], score[:, s, 0:T], own, W("tri_lower", j * T, (j + 1) * T),
                                                                ALU.is_equal, ALU.mult, accum_out=count[:, s, 1, j:j + 1]))
                        chain.link(dve.tensor_tensor(count[:, s, 0, :], count[:, s, 0, :], count[:, s, 1, :], ALU.add))
                        chain.link(dve.scalar_tensor_tensor(factor[:, s, :], count[:, s, 0, :], KEEP - 0.5, count[:, s, 2, :], ALU.is_lt, ALU.mult))
                        dve.sem_inc(ranked.sem, 1)
                    for s in range(2):
                        dve.wait_ge(out_sum.sem, out_sum.at(b + s))
                        for j in range(NT):
                            chain.link(dve.scalar_tensor_tensor(routed[:, s, j, :], out_ps[:, s, j * D:(j + 1) * D], factor[:, s, j:j + 1],
                                                                pairs(normed)[:, c, s, j, :], ALU.mult, ALU.add))
                        dve.tensor_tensor(pairs(state)[:, c, s, :, :], pairs(state)[:, c, s, :, :], routed[:, s, :, :], ALU.add)\
                           .then_inc(out_read.sem, 1)
                    chain.close()

        def attention(name, units, causal, width, group, q_of, k_of, v_of, prepare, finish, ctx):
            o_banks = 2 if causal else 1
            tile = sb(f"{name}_tile", [P, NT, D], F32, ctx)
            probs = sb(f"{name}_probs", [P, 2, NT, T], F32, ctx)
            turned = sb(f"{name}_turned", [P, 2, NT * TP], F32, ctx)
            neg_max = sb(f"{name}_neg_max", [P, 2, NT], F32, ctx)
            s_ps = ctx.enter_context(nc.psum_tensor(f"{name}_s_ps", [P, NT, 512], F32))
            t_ps = ctx.enter_context(nc.psum_tensor(f"{name}_t_ps", [P, 2 if causal else 3, 512], F32))
            o_ps = ctx.enter_context(nc.psum_tensor(f"{name}_o_ps", [P, o_banks, 512], F32))
            x_ps = ctx.enter_context(nc.psum_tensor(f"{name}_x_ps", [P, 512], F32))

            def sig(n, buffers):
                return Signal(nc, ctx, f"{name}_{n}", buffers)

            staged, flipped_sum, ready_act, ready_dve = sig("staged", 1), sig("flipped_sum", 1), sig("ready_act", 1), sig("ready_dve", 1)
            scores_sum, max_ready, probs_ready = sig("scores_sum", 1), sig("max_ready", 1), sig("probs_ready", 2)
            turned_sum, act_turned, dve_turned = sig("turned_sum", 2), sig("act_turned", 2), sig("dve_turned", 2)
            product_sum, finished = sig("product_sum", 3), sig("finished", 2)
            block = ctx.enter_context(nc.Block())
            t_flat = t_ps[:, :, :].rearrange("p a n -> p (a n)")

            def keys(qt):
                return range(qt + 1) if causal else range(NT)

            def score_width(qt):
                return min((qt + 1) * P, T) if causal else T

            def place(kt, qt):
                if causal:
                    at = (0, 2 * P, 3 * P)[kt] + qt * P
                    return at, at + (P if kt > 0 else 0)
                return kt * TP + qt * P, kt * 512 + qt * P

            @block.gpsimd
            def _(pool):
                pool.sem_inc(staged.sem, staged.buffers)
                with pool.Fori(0, B) as b:
                    pool.wait_ge(flipped_sum.sem, flipped_sum.at(b - 1))
                    pool.tensor_copy(tile[:, :, :], normed[:, b, :, :]).then_inc(staged.sem, 1)

            @block.tensor
            def _(pe):
                for x in (flipped_sum, scores_sum, turned_sum, product_sum):
                    pe.sem_inc(x.sem, x.buffers)

                def scores(g, u):
                    for qt in range(NT):
                        w = score_width(qt)
                        if causal:
                            lo, n = qt * P, TK[qt]
                            pe.matmul(s_ps[:, qt, 0:w], q_of(u, qt), k_of(u, w), start=True, stop=False)
                            mm = pe.matmul(s_ps[:, qt, lo:lo + n], ident_bf[:, :], causal_bf[:, 0:n], start=False, stop=True)
                        else:
                            mm = pe.matmul(s_ps[:, qt, 0:w], q_of(u, qt), k_of(u, w), start=True, stop=True)
                    mm.then_inc(scores_sum.sem, 1)

                def turn(g, u):
                    pe.wait_ge(act_turned.sem, act_turned.at(g - 1))
                    pe.sem_inc(bearer, 1)
                    pe.wait_ge(dve_turned.sem, dve_turned.at(g - 1))
                    pe.sem_inc(bearer, 1)
                    for qt in range(NT):
                        for kt in keys(qt):
                            at = place(kt, qt)[1]
                            mm = pe.transpose(t_flat[0:TK[kt], at:at + P], probs[:, u % 2, qt, kt * P:kt * P + TK[kt]], ident)
                    mm.then_inc(turned_sum.sem, 1)

                def products(g, u):
                    pe.wait_ge(act_turned.sem, act_turned.at(g))
                    pe.sem_inc(bearer, 1)
                    pe.wait_ge(dve_turned.sem, dve_turned.at(g))
                    pe.sem_inc(bearer, 1)
                    if u % group == 0:
                        pe.wait_ge(finished.sem, finished.at((g_batch[0] * (units // group)) + u // group - o_banks))
                        pe.sem_inc(bearer, 1)
                    for qt in range(NT):
                        ks = keys(qt)
                        for kt in ks:
                            at = place(kt, qt)[0]
                            o = ((u % group) * NT + qt) * width
                            mm = pe.matmul(o_ps[:, (u // group) % o_banks, o:o + width], turned[0:TK[kt], u % 2, at:at + P], v_of(u, kt),
                                           start=(kt == 0), stop=(kt == ks[-1]))
                    mm.then_inc(product_sum.sem, 1)

                g_batch = [0]
                with pe.Fori(0, B) as b:
                    g_batch[0] = b
                    pe.wait_ge(staged.sem, staged.at(b))
                    pe.sem_inc(bearer, 1)
                    for j in range(NT):
                        mm = pe.transpose(x_ps[0:D, j * P:(j + 1) * P], tile[:, j, :], ident)
                    mm.then_inc(flipped_sum.sem, 1)
                    prepare["pe"](pe, b, s_ps, t_ps, x_ps, flipped_sum, ready_act, ready_dve)
                    scores(units * b, 0)
                    for u in range(units):
                        g = units * b + u
                        pe.wait_ge(probs_ready.sem, probs_ready.at(g))
                        pe.sem_inc(bearer, 1)
                        if u + 1 < units:
                            scores(g + 1, u + 1)
                        turn(g, u)
                        if u > 0:
                            products(g - 1, u - 1)
                    products(units * b + units - 1, units - 1)

            @block.scalar
            def _(act):
                for x in (ready_act, probs_ready, act_turned):
                    act.sem_inc(x.sem, x.buffers)

                def act_copy(g, u):
                    act.wait_ge(turned_sum.sem, turned_sum.at(g))
                    act.sem_inc(bearer, 1)
                    act.wait_ge(product_sum.sem, product_sum.at(g - 2))
                    act.sem_inc(bearer, 1)
                    kt = 0 if causal else NT - 1
                    (to, at), n = place(kt, 0), TP
                    act.activation(turned[0:TK[kt], u % 2, to:to + n], t_flat[0:TK[kt], at:at + n], ACT.Copy).then_inc(act_turned.sem, 1)

                with act.Fori(0, B) as b:
                    act.wait_ge(product_sum.sem, product_sum.at(units * b - 1))
                    act.sem_inc(bearer, 1)
                    prepare["act"](act, b, s_ps, t_ps, x_ps, flipped_sum, ready_act, ready_dve)
                    for u in range(units):
                        g = units * b + u
                        act.wait_ge(max_ready.sem, max_ready.at(g))
                        act.sem_inc(bearer, 1)
                        act.wait_ge(turned_sum.sem, turned_sum.at(g - 2))
                        act.sem_inc(bearer, 1)
                        for qt in range(NT):
                            w = score_width(qt)
                            ins = act.activation(probs[:, u % 2, qt, 0:w], s_ps[:, qt, 0:w], ACT.Exp, bias=neg_max[:, u % 2, qt:qt + 1],
                                                 scale=prepare["scale"])
                        ins.then_inc(probs_ready.sem, 1)
                        if u > 0:
                            act_copy(g - 1, u - 1)
                    act_copy(units * b + units - 1, units - 1)

            @block.vector
            def _(dve):
                for x in (ready_dve, max_ready, dve_turned, finished):
                    dve.sem_inc(x.sem, x.buffers)
                chain = Chain(nc, ctx, dve, f"{name}_chain")

                def dve_copy(g, u):
                    dve.wait_ge(turned_sum.sem, turned_sum.at(g))
                    dve.wait_ge(product_sum.sem, product_sum.at(g - 2))
                    if causal:
                        dve.tensor_copy(turned[:, u % 2, TP:TP + 2 * P], t_ps[:, 1, 0:2 * P])
                        out_, in_ = turned[0:LAST, u % 2, TP + 2 * P:2 * TP], t_ps[0:LAST, 1, 2 * P:TP]
                    else:
                        out_ = turned[:, u % 2, 0:2 * TP].rearrange("p (k n) -> p k n", n=TP)
                        in_ = t_ps[:, 0:2, 0:TP]
                    dve.tensor_copy(out_, in_).then_inc(dve_turned.sem, 1)

                def finish_group(g, b, u):
                    if u % group == group - 1:
                        dve.wait_ge(product_sum.sem, product_sum.at(g))
                        finish(dve, chain, b, u // group, o_ps[:, (u // group) % o_banks, 0:group * NT * width]).then_inc(finished.sem, 1)

                prepare["once"](dve)
                with dve.Fori(0, B) as b:
                    chain.loop(b, prepare["links"] + finish.links * (units // group))
                    prepare["dve"](dve, chain, b, s_ps, t_ps, x_ps, flipped_sum, ready_act, ready_dve)
                    for u in range(units):
                        g = units * b + u
                        dve.wait_ge(scores_sum.sem, scores_sum.at(g))
                        if causal:
                            for qt in range(NT):
                                ins = dve.tensor_reduce(neg_max[:, u % 2, qt:qt + 1], s_ps[:, qt, 0:score_width(qt)], AX.X, ALU.max, negate=True)
                        else:
                            ins = dve.tensor_reduce(neg_max[:, u % 2, :], s_ps[:, :, 0:T], AX.X, ALU.max, negate=True)
                        ins.then_inc(max_ready.sem, 1)
                        if u > 0:
                            dve_copy(g - 1, u - 1)
                        if u > 1:
                            finish_group(g - 2, b, u - 2)
                    dve_copy(units * b + units - 1, units - 1)
                    for u in range(max(units - 2, 0), units):
                        finish_group(units * b + u, b, u)
                    chain.close()

        normalise("a1_ln", state, normed, 1e-5)
        with ExitStack() as ctx:
            x_t = sb("a1_x", [D + 1, TP], F32, ctx)
            q_t = sb("a1_q", [D, TP], F32, ctx)
            k_t = sb("a1_k", [D, TP], F32, ctx)
            values = sb("a1_values", [P, NT, D + 1], F32, ctx)
            inverse = sb("a1_inverse", [D, 1], F32, ctx)
            sums = sb("a1_sums", [P, NT], F32, ctx)
            weighted = sb("a1_weighted", [P, NT, D], F32, ctx)

            def once(dve):
                dve.wait_ge(late_loaded, 16)
                dve.memset(x_t[D:D + 1, :], 1.0)
                dve.memset(values[:, :, D:D + 1], 1.0)
                dve.reciprocal(inverse[:, :], W("a1_scale"))

            def prepare_pe(pe, b, s_ps, t_ps, x_ps, flipped_sum, ready_act, ready_dve):
                pe.wait_ge(ready_dve.sem, ready_dve.at(2 * b))
                pe.sem_inc(bearer, 1)
                pe.matmul(s_ps[0:D, 0, 0:TP], W("a1_q"), x_t[:, :], start=True, stop=True)
                pe.matmul(s_ps[0:D, 1, 0:TP], W("a1_k"), x_t[:, :], start=True, stop=True)
                for j in range(NT):
                    mm = pe.matmul(s_ps[:, 2, j * D:(j + 1) * D], x_t[:, j * P:(j + 1) * P], W("a1_v"), start=True, stop=True)
                mm.then_inc(flipped_pe.sem, 1)
                pe.wait_ge(ready_dve.sem, ready_dve.at(2 * b + 1))
                pe.sem_inc(bearer, 1)
                pe.wait_ge(ready_act.sem, ready_act.at(b))
                pe.sem_inc(bearer, 1)

            def prepare_act(act, b, s_ps, t_ps, x_ps, flipped_sum, ready_act, ready_dve):
                act.wait_ge(flipped_pe.sem, flipped_pe.at(b))
                act.sem_inc(bearer, 1)
                act.activation(k_t[:, :], s_ps[0:D, 1, 0:TP], ACT.Copy)
                act.activation(values[:, :, 0:D], s_ps[:, 2, 0:NT * D].rearrange("p (j d) -> p j d", d=D), ACT.Copy)\
                   .then_inc(ready_act.sem, 1)

            def prepare_dve(dve, chain, b, s_ps, t_ps, x_ps, flipped_sum, ready_act, ready_dve):
                dve.wait_ge(flipped_sum.sem, flipped_sum.at(b))
                dve.tensor_copy(x_t[0:D, :], x_ps[0:D, 0:TP]).then_inc(ready_dve.sem, 1)
                dve.wait_ge(flipped_pe.sem, flipped_pe.at(b))
                dve.tensor_scalar(q_t[:, :], s_ps[0:D, 0, 0:TP], inverse[:, :], None, ALU.mult).then_inc(ready_dve.sem, 1)

            def finish(dve, chain, b, n, products):
                o = products.rearrange("p (j w) -> p j w", w=D + 1)
                chain.link(dve.reciprocal(sums[:, :], o[:, :, D]))
                chain.link(dve.tensor_tensor(weighted[:, :, :], o[:, :, 0:D], sums[:, :].unsqueeze(2).broadcast_to([P, NT, D]), ALU.mult))
                return dve.tensor_tensor(state[:, b, :, :], state[:, b, :, :], weighted[:, :, :], ALU.add)

            finish.links = 2
            flipped_pe = Signal(nc, ctx, "a1_projected", 1)
            with ExitStack() as opened:
                block = opened.enter_context(nc.Block())

                @block.tensor
                def _(pe):
                    pe.sem_inc(flipped_pe.sem, flipped_pe.buffers)

            attention("a1", 1, False, D + 1, 1, lambda u, qt: q_t[:, qt * P:(qt + 1) * P], lambda u, w: k_t[:, 0:w],
                      lambda u, kt: values[0:TK[kt], kt, :],
                      {"pe": prepare_pe, "act": prepare_act, "dve": prepare_dve, "once": once, "scale": 1.0, "links": 0}, finish, ctx)

        def small_softmax(name, logits, groups, n):
            with ExitStack() as ctx:
                top = sb(f"{name}_top", [P, groups], F32, ctx)
                total = sb(f"{name}_total", [P, groups], F32, ctx)
                shifted = ctx.enter_context(nc.semaphore(f"{name}_shifted"))
                exped = ctx.enter_context(nc.semaphore(f"{name}_exped"))
                block = ctx.enter_context(nc.Block())

                def wide(t):
                    return t[:, :].unsqueeze(2).broadcast_to([P, groups, n])

                @block.vector
                def _(dve):
                    chain = Chain(nc, ctx, dve, f"{name}_chain")
                    chain.link(dve.tensor_reduce(top[:, :], logits, AX.X, ALU.max))
                    dve.tensor_tensor(logits, logits, wide(top), ALU.subtract).then_inc(shifted, 1)
                    dve.wait_ge(exped, 1)
                    chain.link(dve.tensor_reduce(total[:, :], logits, AX.X, ALU.add))
                    chain.link(dve.reciprocal(total[:, :], total[:, :]))
                    chain.link(dve.tensor_tensor(logits, logits, wide(total), ALU.mult))

                @block.scalar
                def _(act):
                    act.wait_ge(shifted, 1)
                    act.activation(logits, logits, ACT.Exp).then_inc(exped, 1)

        renew_semaphores()

        normalise("f1_ln", state, normed, 1e-5)
        with ExitStack() as f1:
            inputs_tok = sb("f1_inputs", [P, B, NT, D], F32, f1)
            answers = sb("f1_answers", [P, B, NT, LH, LE * LD], F32, f1)
            mixed = sb("f1_mixed", [P, B, NT, D], F32, f1)
            with ExitStack() as ctx:
                x_t = sb("f1_x", [D + 1, TP], F32, ctx)
                wide_t = sb("f1_wide", [P, TP], F32, ctx)
                q_t = sb("f1_q", [P, LE, TP], F32, ctx)
                k_t = sb("f1_k", [P, TP], F32, ctx)
                values = sb("f1_values", [P, NT, LH, LD + 1], F32, ctx)
                present = sb("f1_present", [P, NT, LH, LD], F32, ctx)
                sums = sb("f1_sums", [P, LE * NT], F32, ctx)
                weighted = sb("f1_weighted", [P, LE * NT, LD], F32, ctx)
                projected = Signal(nc, ctx, "f1_projected", 2)
                with ExitStack() as opened:
                    block = opened.enter_context(nc.Block())

                    @block.tensor
                    def _(pe):
                        pe.sem_inc(projected.sem, projected.buffers)

                def once(dve):
                    dve.memset(x_t[D:D + 1, :], 1.0)
                    dve.memset(values[:, :, :, LD:LD + 1], 1.0)

                def prepare_pe(pe, b, s_ps, t_ps, x_ps, flipped_sum, ready_act, ready_dve):
                    pe.wait_ge(ready_dve.sem, ready_dve.at(3 * b))
                    pe.sem_inc(bearer, 1)
                    pe.matmul(s_ps[:, 0, 0:TP], W("hl_wide"), x_t[:, :], start=True, stop=True)
                    for j in range(NT):
                        mm = pe.matmul(s_ps[:, 1, j * D:(j + 1) * D], x_t[:, j * P:(j + 1) * P], W("hl_tok"), start=True, stop=True)
                    mm.then_inc(projected.sem, 1)
                    pe.wait_ge(ready_act.sem, ready_act.at(2 * b))
                    pe.sem_inc(bearer, 1)
                    pe.wait_ge(ready_dve.sem, ready_dve.at(3 * b + 1))
                    pe.sem_inc(bearer, 1)
                    for e, o in enumerate((s_ps[:, 0, 0:TP], s_ps[:, 1, 0:TP], s_ps[:, 2, 0:TP], x_ps[:, 0:TP])):
                        pe.matmul(o, W("wq_wide", e * P, (e + 1) * P), wide_t[:, :], start=True, stop=True)
                    pe.matmul(t_ps[:, 0, 0:TP], W("wk_wide"), wide_t[:, :], start=True, stop=True)
                    for j in range(NT):
                        mm = pe.matmul(t_ps[:, 1, j * D:(j + 1) * D], wide_t[:, j * P:(j + 1) * P], W("wv_wide"), start=True, stop=True)
                    mm.then_inc(projected.sem, 1)
                    pe.wait_ge(ready_act.sem, ready_act.at(2 * b + 1))
                    pe.sem_inc(bearer, 1)
                    pe.wait_ge(ready_dve.sem, ready_dve.at(3 * b + 2))
                    pe.sem_inc(bearer, 1)

                def prepare_act(act, b, s_ps, t_ps, x_ps, flipped_sum, ready_act, ready_dve):
                    act.wait_ge(projected.sem, projected.at(2 * b))
                    act.sem_inc(bearer, 1)
                    act.activation(wide_t[:, :], s_ps[:, 0, 0:TP], ACT.Copy).then_inc(ready_act.sem, 1)
                    act.wait_ge(projected.sem, projected.at(2 * b + 1))
                    act.sem_inc(bearer, 1)
                    act.activation(q_t[:, 0:2, :], s_ps[:, 0:2, 0:TP], ACT.Copy, scale=float(LD) ** 0.5)
                    act.activation(k_t[:, :], t_ps[:, 0, 0:TP], ACT.Copy).then_inc(ready_act.sem, 1)

                def prepare_dve(dve, chain, b, s_ps, t_ps, x_ps, flipped_sum, ready_act, ready_dve):
                    dve.wait_ge(flipped_sum.sem, flipped_sum.at(b))
                    dve.tensor_copy(x_t[0:D, :], x_ps[0:D, 0:TP]).then_inc(ready_dve.sem, 1)
                    dve.wait_ge(projected.sem, projected.at(2 * b))
                    heads = s_ps[:, 1, 0:NT * D]
                    dve.tensor_scalar(present[:, :, :, :].rearrange("p j n d -> p (j n d)"), heads, 0.0, None, ALU.not_equal)
                    dve.tensor_copy(inputs_tok[:, b, :, :], heads.rearrange("p (j d) -> p j d", d=D)).then_inc(ready_dve.sem, 1)
                    dve.wait_ge(projected.sem, projected.at(2 * b + 1))
                    dve.tensor_scalar(q_t[:, 2, :], s_ps[:, 2, 0:TP], float(LD) ** 0.5, None, ALU.mult)
                    dve.tensor_scalar(q_t[:, 3, :], x_ps[:, 0:TP], float(LD) ** 0.5, None, ALU.mult)
                    dve.tensor_copy(values[:, :, :, 0:LD], t_ps[:, 1, 0:NT * D].rearrange("p (j n d) -> p j n d", n=LH, d=LD))\
                       .then_inc(ready_dve.sem, 1)

                def finish(dve, chain, b, n, products):
                    o = products.rearrange("p (g w) -> p g w", w=LD + 1)
                    chain.link(dve.reciprocal(sums[:, :], o[:, :, LD]))
                    chain.link(dve.tensor_tensor(weighted[:, :, :], o[:, :, 0:LD], sums[:, :].unsqueeze(2).broadcast_to([P, LE * NT, LD]), ALU.mult))
                    return dve.tensor_tensor(answers[:, b, :, n, :].rearrange("p j (e d) -> p e j d", e=LE),
                                             weighted[:, :, :].rearrange("p (e j) d -> p e j d", e=LE),
                                             present[:, :, n, :].unsqueeze(1).broadcast_to([P, LE, NT, LD]), ALU.mult)

                finish.links = 2
                attention("f1", LH * LE, True, LD + 1, LE,
                          lambda u, qt: q_t[32 * (u // LE):32 * (u // LE) + LD, u % LE, qt * P:(qt + 1) * P],
                          lambda u, w: k_t[32 * (u // LE):32 * (u // LE) + LD, 0:w],
                          lambda u, kt: values[0:TK[kt], kt, u // LE, :],
                          {"pe": prepare_pe, "act": prepare_act, "dve": prepare_dve, "once": once, "scale": 1.0, "links": 0}, finish, ctx)

            gates1 = sb("f1_gates", [P, B, NT, LH * LE], F32, f1)
            with ExitStack() as ctx:
                tile = sb("g1_tile", [P, NT, LH * D], F32, ctx)
                turned = sb("g1_turned", [P, 2, TP], F32, ctx)
                turned_ps = ctx.enter_context(nc.psum_tensor("g1_turned_ps", [P, 2, 512], F32))
                logit_ps = ctx.enter_context(nc.psum_tensor("g1_logit_ps", [P, 512], F32))
                staged, turned_sum, copied = Signal(nc, ctx, "g1_staged", 1), Signal(nc, ctx, "g1_turned_sum", 1), Signal(nc, ctx, "g1_copied", 1)
                logit_sum, logit_read = Signal(nc, ctx, "g1_logit_sum", 1), Signal(nc, ctx, "g1_logit_read", 1)
                block = ctx.enter_context(nc.Block())

                @block.gpsimd
                def _(pool):
                    pool.sem_inc(staged.sem, staged.buffers)
                    with pool.Fori(0, B) as b:
                        pool.wait_ge(turned_sum.sem, turned_sum.at(b - 1))
                        pool.tensor_copy(tile[:, :, :], answers[:, b, :, :, :].rearrange("p j n f -> p j (n f)")).then_inc(staged.sem, 1)

                @block.tensor
                def _(pe):
                    pe.sem_inc(turned_sum.sem, turned_sum.buffers)
                    pe.sem_inc(logit_sum.sem, logit_sum.buffers)
                    with pe.Fori(0, B) as b:
                        pe.wait_ge(staged.sem, staged.at(b))
                        pe.sem_inc(bearer, 1)
                        pe.wait_ge(copied.sem, copied.at(b - 1))
                        pe.sem_inc(bearer, 1)
                        for h in range(2):
                            for j in range(NT):
                                mm = pe.transpose(turned_ps[:, h, j * P:(j + 1) * P], tile[:, j, h * P:(h + 1) * P], ident)
                        mm.then_inc(turned_sum.sem, 1)
                        pe.wait_ge(copied.sem, copied.at(b))
                        pe.sem_inc(bearer, 1)
                        pe.wait_ge(logit_read.sem, logit_read.at(b - 1))
                        pe.sem_inc(bearer, 1)
                        for j in range(NT):
                            for h in range(2):
                                at = j * 16 + h * 8
                                mm = pe.matmul(logit_ps[:, at:at + 8], turned[:, h, j * P:(j + 1) * P], W("gate_w", h * 8, h * 8 + 8),
                                               start=True, stop=True)
                        mm.then_inc(logit_sum.sem, 1)

                @block.scalar
                def _(act):
                    act.sem_inc(copied.sem, copied.buffers)
                    with act.Fori(0, B) as b:
                        act.wait_ge(turned_sum.sem, turned_sum.at(b))
                        act.sem_inc(bearer, 1)
                        act.wait_ge(logit_sum.sem, logit_sum.at(b - 1))
                        act.sem_inc(bearer, 1)
                        act.activation(turned[:, :, :], turned_ps[:, :, 0:TP], ACT.Copy).then_inc(copied.sem, 1)

                @block.vector
                def _(dve):
                    dve.sem_inc(logit_read.sem, logit_read.buffers)
                    with dve.Fori(0, B) as b:
                        dve.wait_ge(logit_sum.sem, logit_sum.at(b))
                        dve.tensor_tensor(gates1[:, b, :, :], logit_ps[:, 0:NT * 16].rearrange("p (j g) -> p j g", g=16),
                                          R("gate_b").unsqueeze(1).broadcast_to([P, NT, 16]), ALU.add).then_inc(logit_read.sem, 1)

            small_softmax("g1", gates1[:, :, :, :].rearrange("p b j (n e) -> p (b j n) e", e=LE), B * NT * LH, LE)
            with ExitStack() as ctx:
                residual = sb("f1_residual", [P, NT, LH, LD], F32, ctx)
                block = ctx.enter_context(nc.Block())

                @block.vector
                def _(dve):
                    chain = Chain(nc, ctx, dve, "mix_chain")
                    for n in range(LH):
                        dve.tensor_copy(residual[:, :, n, :], inputs_tok[:, n, :, n * LD:(n + 1) * LD])
                    a = answers[:, :, :, :, :].rearrange("p b j n (e d) -> p (b j n e) d", d=LD)
                    g = gates1[:, :, :, :].rearrange("p b j g -> p (b j g)").unsqueeze(2).broadcast_to([P, B * NT * LH * LE, LD])
                    chain.link(dve.tensor_tensor(a, a, g, ALU.mult))
                    chain.link(dve.tensor_reduce(normed[:, :, :, :].rearrange("p b j (n d) -> p (b j n) d", d=LD),
                                                 answers[:, :, :, :, :].rearrange("p b j n (e d) -> p (b j n) d e", d=LD), AX.X, ALU.add))
                    flat = normed[:, :, :, :].rearrange("p b j d -> p b (j d)")
                    r = residual[:, :, :, :].rearrange("p j n d -> p (j n d)").unsqueeze(1).broadcast_to([P, B, NT * D])
                    chain.link(dve.tensor_tensor(flat, flat, r, ALU.add))

            normalise("f1_ln1", normed, mixed, 1e-8, gain="ln_g", shift="ln_b", width=LD)
            with ExitStack() as ctx:
                tile = sb("fc_tile", [P, NT, D], F32, ctx)
                x_t = sb("fc_x", [D + 1, TP], F32, ctx)
                nonzero = sb("fc_nonzero", [D, TP], F32, ctx)
                middle = sb("fc_middle", [D + 1, TP], F32, ctx)
                result = sb("fc_result", [P, NT, D], F32, ctx)
                x_ps = ctx.enter_context(nc.psum_tensor("fc_x_ps", [P, 512], F32))
                m_ps = ctx.enter_context(nc.psum_tensor("fc_m_ps", [P, 512], F32))
                y_ps = ctx.enter_context(nc.psum_tensor("fc_y_ps", [P, 512], F32))
                names = ("staged", "x_sum", "x_ready", "m_sum", "m_ready", "y_sum", "y_read")
                staged, x_sum, x_ready, m_sum, m_ready, y_sum, y_read = (Signal(nc, ctx, f"fc_{n}", 1) for n in names)
                block = ctx.enter_context(nc.Block())

                @block.gpsimd
                def _(pool):
                    pool.sem_inc(staged.sem, staged.buffers)
                    with pool.Fori(0, B) as b:
                        pool.wait_ge(y_read.sem, y_read.at(b - 1))
                        pool.tensor_copy(tile[:, :, :], mixed[:, b, :, :]).then_inc(staged.sem, 1)

                @block.tensor
                def _(pe):
                    for x in (x_sum, m_sum, y_sum):
                        pe.sem_inc(x.sem, x.buffers)
                    with pe.Fori(0, B) as b:
                        pe.wait_ge(staged.sem, staged.at(b))
                        pe.sem_inc(bearer, 1)
                        pe.wait_ge(x_ready.sem, x_ready.at(b - 1))
                        pe.sem_inc(bearer, 1)
                        for j in range(NT):
                            mm = pe.transpose(x_ps[0:D, j * P:(j + 1) * P], tile[:, j, :], ident)
                        mm.then_inc(x_sum.sem, 1)
                        pe.wait_ge(x_ready.sem, x_ready.at(b))
                        pe.sem_inc(bearer, 1)
                        pe.wait_ge(m_ready.sem, m_ready.at(b - 1))
                        pe.sem_inc(bearer, 1)
                        pe.matmul(m_ps[0:D, 0:TP], W("fc1"), x_t[:, :], start=True, stop=True).then_inc(m_sum.sem, 1)
                        pe.wait_ge(m_ready.sem, m_ready.at(b))
                        pe.sem_inc(bearer, 1)
                        pe.wait_ge(y_read.sem, y_read.at(b - 1))
                        pe.sem_inc(bearer, 1)
                        for j in range(NT):
                            mm = pe.matmul(y_ps[:, j * D:(j + 1) * D], middle[:, j * P:(j + 1) * P], W("fc2"), start=True, stop=True)
                        mm.then_inc(y_sum.sem, 1)

                @block.scalar
                def _(act):
                    act.sem_inc(x_ready.sem, x_ready.buffers)
                    with act.Fori(0, B) as b:
                        act.wait_ge(x_sum.sem, x_sum.at(b))
                        act.sem_inc(bearer, 1)
                        act.wait_ge(m_ready.sem, m_ready.at(b - 1))
                        act.sem_inc(bearer, 1)
                        act.activation(x_t[0:D, :], x_ps[0:D, 0:TP], ACT.Copy).then_inc(x_ready.sem, 1)

                @block.vector
                def _(dve):
                    chain = Chain(nc, ctx, dve, "fc_chain")
                    chain.link(dve.memset(x_t[D:D + 1, :], 1.0))
                    chain.link(dve.memset(middle[D:D + 1, :], 1.0))
                    dve.sem_inc(m_ready.sem, m_ready.buffers)
                    dve.sem_inc(y_read.sem, y_read.buffers)
                    first = chain.count
                    with dve.Fori(0, B) as b:
                        chain.loop(b, 3)
                        chain.base = chain.base + first
                        dve.wait_ge(x_ready.sem, x_ready.at(b))
                        chain.link(dve.tensor_scalar(nonzero[:, :], x_t[0:D, :], 0.0, None, ALU.not_equal))
                        dve.wait_ge(m_sum.sem, m_sum.at(b))
                        dve.scalar_tensor_tensor(middle[0:D, :], m_ps[0:D, 0:TP], 0.0, nonzero[:, :], ALU.max, ALU.mult).then_inc(m_ready.sem, 1)
                        dve.wait_ge(staged.sem, staged.at(b))
                        chain.link(dve.tensor_scalar(result[:, :, :], tile[:, :, :], 0.0, None, ALU.not_equal))
                        dve.wait_ge(y_sum.sem, y_sum.at(b))
                        chain.link(dve.tensor_tensor(result[:, :, :], result[:, :, :], y_ps[:, 0:NT * D].rearrange("p (j d) -> p j d", d=D), ALU.mult))
                        dve.tensor_tensor(normed[:, b, :, :], result[:, :, :], tile[:, :, :], ALU.add).then_inc(y_read.sem, 1)
                        chain.close()

            normalise("f1_ln2", normed, mixed, 1e-8, gain="fnorm_g", shift="fnorm_b", width=LD)
            head_gates = sb("f1_head_gates", [P, B * NT, LH], F32, f1)
            with ExitStack() as ctx:
                block = ctx.enter_context(nc.Block())

                @block.vector
                def _(dve):
                    chain = Chain(nc, ctx, dve, "fgate_chain")
                    for n in range(LH):
                        row = R("fgate")[:, n * D:(n + 1) * D].unsqueeze(1).broadcast_to([P, B * NT, D])
                        s = scratch[:, :, :, :].rearrange("p b j d -> p (b j) d")
                        chain.link(dve.tensor_tensor(s, mixed[:, :, :, :].rearrange("p b j d -> p (b j) d"), row, ALU.mult))
                        chain.link(dve.tensor_reduce(head_gates[:, :, n], s, AX.X, ALU.add))

            small_softmax("g2", head_gates[:, :, :], B * NT, LH)
            with ExitStack() as ctx:
                block = ctx.enter_context(nc.Block())

                @block.vector
                def _(dve):
                    chain = Chain(nc, ctx, dve, "f1_chain")
                    m = mixed[:, :, :, :].rearrange("p b j (n d) -> p (b j n) d", d=LD)
                    chain.link(dve.tensor_tensor(m, m, head_gates[:, :, :].rearrange("p g n -> p (g n)").unsqueeze(2)
                                                 .broadcast_to([P, B * NT * LH, LD]), ALU.mult))
                    chain.link(dve.tensor_tensor(state[:, :, :, :], state[:, :, :, :], mixed[:, :, :, :], ALU.add))

        renew_semaphores()

        normalise("a2_ln", state, normed, 1e-5)
        with ExitStack() as ctx:
            x_t = sb("a2_x", [D, TP], F32, ctx)
            q_t = sb("a2_q", [P, 2, TP], F32, ctx)
            k_t = sb("a2_k", [P, 2, TP], F32, ctx)
            values = sb("a2_values", [P, NT, AH, D + 1], F32, ctx)
            sums = sb("a2_sums", [P, NT], F32, ctx)
            weighted = sb("a2_weighted", [P, NT, D], F32, ctx)
            projected = Signal(nc, ctx, "a2_projected", 1)
            with ExitStack() as opened:
                block = opened.enter_context(nc.Block())

                @block.tensor
                def _(pe):
                    pe.sem_inc(projected.sem, projected.buffers)

            def once(dve):
                dve.memset(values[:, :, :, D:D + 1], 1.0)

            def prepare_pe(pe, b, s_ps, t_ps, x_ps, flipped_sum, ready_act, ready_dve):
                pe.wait_ge(ready_dve.sem, ready_dve.at(2 * b))
                pe.sem_inc(bearer, 1)
                for h in range(2):
                    pe.matmul(s_ps[:, h, 0:TP], W("a2_q", h * P, (h + 1) * P), x_t[:, :], start=True, stop=True)
                pe.matmul(s_ps[:, 2, 0:TP], W("a2_k", 0, P), x_t[:, :], start=True, stop=True)
                pe.matmul(x_ps[:, 0:TP], W("a2_k", P, 2 * P), x_t[:, :], start=True, stop=True)
                for j in range(NT):
                    mm = pe.matmul(t_ps[:, j, 0:AH * D], x_t[:, j * P:(j + 1) * P], W("a2_vo"), start=True, stop=True)
                mm.then_inc(projected.sem, 1)
                pe.wait_ge(ready_dve.sem, ready_dve.at(2 * b + 1))
                pe.sem_inc(bearer, 1)
                pe.wait_ge(ready_act.sem, ready_act.at(b))
                pe.sem_inc(bearer, 1)

            def prepare_act(act, b, s_ps, t_ps, x_ps, flipped_sum, ready_act, ready_dve):
                act.wait_ge(projected.sem, projected.at(b))
                act.sem_inc(bearer, 1)
                act.activation(q_t[:, :, :], s_ps[:, 0:2, 0:TP], ACT.Copy, scale=float(D) ** -0.5)
                act.activation(values[:, 0, :, 0:D], t_ps[:, 0, :].rearrange("p (n d) -> p n d", d=D), ACT.Copy)\
                   .then_inc(ready_act.sem, 1)

            def prepare_dve(dve, chain, b, s_ps, t_ps, x_ps, flipped_sum, ready_act, ready_dve):
                dve.wait_ge(flipped_sum.sem, flipped_sum.at(b))
                dve.tensor_copy(x_t[:, :], x_ps[0:D, 0:TP]).then_inc(ready_dve.sem, 1)
                dve.wait_ge(projected.sem, projected.at(b))
                dve.tensor_copy(k_t[:, 0, :], s_ps[:, 2, 0:TP])
                dve.tensor_copy(k_t[:, 1, :], x_ps[:, 0:TP])
                for j in range(1, NT):
                    ins = dve.tensor_copy(values[:, j, :, 0:D], t_ps[:, j, :].rearrange("p (n d) -> p n d", d=D))
                ins.then_inc(ready_dve.sem, 1)

            def finish(dve, chain, b, n, products):
                o = products.rearrange("p (j w) -> p j w", w=D + 1)
                chain.link(dve.reciprocal(sums[:, :], o[:, :, D]))
                chain.link(dve.tensor_tensor(weighted[:, :, :], o[:, :, 0:D], sums[:, :].unsqueeze(2).broadcast_to([P, NT, D]), ALU.mult))
                ins = dve.tensor_tensor(state[:, b, :, :], state[:, b, :, :], weighted[:, :, :], ALU.add)
                return ins

            finish.links = 2
            attention("a2", AH, False, D + 1, 1,
                      lambda u, qt: q_t[AR * (u % 4):AR * (u % 4) + AR, u // 4, qt * P:(qt + 1) * P],
                      lambda u, w: k_t[AR * (u % 4):AR * (u % 4) + AR, u // 4, 0:w],
                      lambda u, kt: values[0:TK[kt], kt, u, :],
                      {"pe": prepare_pe, "act": prepare_act, "dve": prepare_dve, "once": once, "scale": 1.0, "links": 0}, finish, ctx)

        def experts(name, gate, bias, function):
            with ExitStack() as whole_mix:
                logits = sb(f"{name}_logits", [P, B, NT, NE], F32, whole_mix)
                combine = sb(f"{name}_combine", [P, B, NT, NE], F32, whole_mix)
                flip(f"{name}_flip", normed, logits, gate)
                groups = B * NT
                with ExitStack() as ctx:
                    first = sb(f"{name}_first", [P, groups, NE], F32, ctx)
                    work = sb(f"{name}_work", [P, groups, NE], F32, ctx)
                    value = sb(f"{name}_value", [P, 4, groups], F32, ctx)
                    apart = ctx.enter_context(nc.semaphore(f"{name}_apart"))
                    exped = ctx.enter_context(nc.semaphore(f"{name}_exped"))
                    block = ctx.enter_context(nc.Block())
                    g = logits[:, :, :, :].rearrange("p b j e -> p (b j) e")
                    second = combine[:, :, :, :].rearrange("p b j e -> p (b j) e")

                    def wide(t):
                        return t.unsqueeze(2).broadcast_to([P, groups, NE])

                    @block.vector
                    def _(dve):
                        chain = Chain(nc, ctx, dve, f"{name}_route_chain")
                        countdown = R("countdown").unsqueeze(1).broadcast_to([P, groups, NE])

                        def pick(best, mark):
                            chain.link(dve.tensor_reduce(best, g, AX.X, ALU.max))
                            chain.link(dve.tensor_tensor(work[:, :, :], g, wide(best), ALU.is_equal))
                            chain.link(dve.tensor_tensor(work[:, :, :], work[:, :, :], countdown, ALU.mult))
                            chain.link(dve.tensor_reduce(value[:, 2, :], work[:, :, :], AX.X, ALU.max))
                            chain.link(dve.tensor_tensor(mark, work[:, :, :], wide(value[:, 2, :]), ALU.is_equal))

                        if bias is not None:
                            chain.link(dve.tensor_tensor(g, g, R(bias).unsqueeze(1).broadcast_to([P, groups, NE]), ALU.add))
                        pick(value[:, 0, :], first[:, :, :])
                        chain.link(dve.scalar_tensor_tensor(g, first[:, :, :], -BIG, g, ALU.mult, ALU.add))
                        pick(value[:, 1, :], second)
                        dve.tensor_tensor(value[:, 3, :], value[:, 1, :], value[:, 0, :], ALU.subtract).then_inc(apart, 1)
                        dve.wait_ge(exped, 1)
                        chain.link(dve.tensor_scalar(value[:, 0, :], value[:, 3, :], 1.0, None, ALU.add))
                        chain.link(dve.reciprocal(value[:, 0, :], value[:, 0, :]))
                        chain.link(dve.tensor_tensor(value[:, 1, :], value[:, 0, :], value[:, 3, :], ALU.mult))
                        chain.link(dve.tensor_tensor(first[:, :, :], first[:, :, :], wide(value[:, 0, :]), ALU.mult))
                        chain.link(dve.tensor_tensor(second, second, wide(value[:, 1, :]), ALU.mult))
                        chain.link(dve.tensor_tensor(second, second, first[:, :, :], ALU.add))

                    @block.scalar
                    def _(act):
                        act.wait_ge(apart, 1)
                        act.activation(value[:, 3, :], value[:, 3, :], ACT.Exp).then_inc(exped, 1)

                with ExitStack() as ctx:
                    hidden = sb(f"{name}_hidden", [P, 3, TP], F32, ctx)
                    weighted = sb(f"{name}_weighted", [P, 2, NE * D], F32, ctx)
                    total = sb(f"{name}_total", [P, NT, D], F32, ctx)
                    h_ps = ctx.enter_context(nc.psum_tensor(f"{name}_h_ps", [P, 2, 512], F32))
                    y_ps = ctx.enter_context(nc.psum_tensor(f"{name}_y_ps", [P, 2, NT, 512], F32))
                    hidden_sum, hidden_ready, used = Signal(nc, ctx, f"{name}_hidden_sum", 2), Signal(nc, ctx, f"{name}_hidden_ready", 2), Signal(nc, ctx, f"{name}_used", 2)
                    y_sum, y_read = Signal(nc, ctx, f"{name}_y_sum", 2), Signal(nc, ctx, f"{name}_y_read", 2)
                    block = ctx.enter_context(nc.Block())

                    @block.tensor
                    def _(pe):
                        for x in (hidden_sum, used, y_sum):
                            pe.sem_inc(x.sem, x.buffers)
                        with pe.Fori(0, B // 2) as c:
                            def up(s, e):
                                pe.wait_ge(hidden_ready.sem, hidden_ready.at(NE * (2 * c + s) + e - 2))
                                pe.sem_inc(bearer, 1)
                                pe.matmul(h_ps[:, e % 2, 0:TP], W(f"{name}_w1", e * EH, (e + 1) * EH),
                                          pairs(flipped)[0:D + 1, c, s, PADL:PADL + TP], start=True, stop=True).then_inc(hidden_sum.sem, 1)

                            for s in range(2):
                                up(s, 0)
                                pe.wait_ge(y_read.sem, y_read.at(2 * c + s - 2))
                                pe.sem_inc(bearer, 1)
                                for j in range(NT):
                                    pe.matmul(y_ps[:, s, j, 0:NE * D], W("ones_row"), W(f"{name}_b2"), start=True, stop=False)
                                for e in range(NE):
                                    if e + 1 < NE:
                                        up(s, e + 1)
                                    pe.wait_ge(hidden_ready.sem, hidden_ready.at(NE * (2 * c + s) + e))
                                    pe.sem_inc(bearer, 1)
                                    for j in range(NT):
                                        mm = pe.matmul(y_ps[:, s, j, e * D:(e + 1) * D], hidden[:, e % 2, j * P:(j + 1) * P],
                                                       W(f"{name}_w2", e * D, (e + 1) * D), start=False, stop=(e == NE - 1))
                                    mm.then_inc(used.sem, 1)
                                pe.sem_inc(bearer, 1)
                                pe.wait_ge(used.sem, used.at(NE * (2 * c + s) + NE - 1))
                                pe.sem_inc(y_sum.sem, 1)

                    @block.scalar
                    def _(act):
                        act.sem_inc(hidden_ready.sem, hidden_ready.buffers)
                        with act.Fori(0, B) as b:
                            for e in range(NE):
                                act.wait_ge(hidden_sum.sem, hidden_sum.at(NE * b + e))
                                act.sem_inc(bearer, 1)
                                act.wait_ge(used.sem, used.at(NE * b + e - 2))
                                act.sem_inc(bearer, 1)
                                act.activation(hidden[:, e % 2, :], h_ps[:, e % 2, 0:TP], function).then_inc(hidden_ready.sem, 1)

                    @block.vector
                    def _(dve):
                        dve.sem_inc(y_read.sem, y_read.buffers)
                        chain = Chain(nc, ctx, dve, f"{name}_chain")
                        with dve.Fori(0, B // 2) as c:
                            chain.loop(c, 2 * 2 * NT)
                            for s in range(2):
                                dve.wait_ge(y_sum.sem, y_sum.at(2 * c + s))
                                for j in range(NT):
                                    w = weighted[:, j % 2, :].rearrange("p (e d) -> p e d", e=NE)
                                    chain.link(dve.tensor_tensor(w, y_ps[:, s, j, 0:NE * D].rearrange("p (e d) -> p e d", e=NE),
                                                                 pairs(combine)[:, c, s, j, :].unsqueeze(2).broadcast_to([P, NE, D]), ALU.mult))
                                    chain.link(dve.tensor_reduce(total[:, j, :], weighted[:, j % 2, :].rearrange("p (e d) -> p d e", e=NE), AX.X, ALU.add))
                                dve.tensor_tensor(pairs(state)[:, c, s, :, :], pairs(state)[:, c, s, :, :], total[:, :, :], ALU.add)\
                                   .then_inc(y_read.sem, 1)
                            chain.close()

        normalise("m2_ln", state, normed, 1e-5)
        experts("m2", "m2_gate", "m2_bias", ACT.Relu)
        renew_semaphores()

        normalise("a3_ln", state, normed, 1e-5)
        flip("a3_flip", normed)
        with ExitStack() as ctx:
            x_t = sb("a3_x", [D, TP], F32, ctx)
            k_exp = sb("a3_k_exp", [D, TP], F32, ctx)
            v_t = sb("a3_v", [D, TP], F32, ctx)
            q_tok = sb("a3_q_tok", [P, NT, D], F32, ctx)
            k_tok = sb("a3_k_tok", [P, NT, D], F32, ctx)
            mass = sb("a3_mass", [D, 4], F32, ctx)
            pair = sb("a3_pair", [D, D], F32, ctx)
            o_t = sb("a3_o", [D, T], F32, ctx)
            in_line = sb("a3_in_line", [8, 8 * T], F32, ctx)
            k_ps = ctx.enter_context(nc.psum_tensor("a3_k_ps", [P, 512], F32))
            v_ps = ctx.enter_context(nc.psum_tensor("a3_v_ps", [P, 512], F32))
            q_ps = ctx.enter_context(nc.psum_tensor("a3_q_ps", [P, 512], F32))
            kt_ps = ctx.enter_context(nc.psum_tensor("a3_kt_ps", [P, 512], F32))
            pair_ps = ctx.enter_context(nc.psum_tensor("a3_pair_ps", [P, 512], F32))
            o_ps = ctx.enter_context(nc.psum_tensor("a3_o_ps", [P, 512], F32))
            y_ps = ctx.enter_context(nc.psum_tensor("a3_y_ps", [P, 512], F32))
            lined_up = ctx.enter_context(nc.semaphore("a3_lined_up"))
            names = ("staged", "k_sum", "v_sum", "q_sum", "top", "exped", "v_ready", "q_ready", "kt_sum", "kt_ready", "pair_sum", "pair_ready",
                     "o_sum", "o_ready", "y_sum", "y_read")
            (staged, k_sum, v_sum, q_sum, top, exped, v_ready, q_ready, kt_sum, kt_ready, pair_sum, pair_ready,
             o_sum, o_ready, y_sum, y_read) = (Signal(nc, ctx, f"a3_{n}", 1) for n in names)
            block = ctx.enter_context(nc.Block())

            @block.sync
            def _(sp):
                with sp.Fori(0, B) as b:
                    sp.wait_ge(o_ready.sem, o_ready.at(b))
                    sp.sem_inc(bearer, 1)
                    sp.wait_ge(y_sum.sem, y_sum.at(b - 1))
                    sp.sem_inc(bearer, 1)
                    for h in range(8):
                        sp.dma_start(in_line[:, h * T:(h + 1) * T], o_t[8 * h:8 * h + 8, :]).then_inc(lined_up, 16)

            @block.gpsimd
            def _(pool):
                pool.sem_inc(staged.sem, staged.buffers)
                with pool.Fori(0, B) as b:
                    pool.wait_ge(q_sum.sem, q_sum.at(b - 1))
                    pool.tensor_copy(x_t[:, :], flipped[0:D, b, PADL:PADL + TP]).then_inc(staged.sem, 1)

            @block.tensor
            def _(pe):
                for x in (k_sum, v_sum, q_sum, kt_sum, pair_sum, o_sum, y_sum):
                    pe.sem_inc(x.sem, x.buffers)
                with pe.Fori(0, B) as b:
                    pe.wait_ge(staged.sem, staged.at(b))
                    pe.sem_inc(bearer, 1)
                    pe.wait_ge(exped.sem, exped.at(b - 1))
                    pe.sem_inc(bearer, 1)
                    pe.matmul(k_ps[0:D, 0:TP], W("a3_qkv", D, 2 * D), x_t[:, :], start=True, stop=True).then_inc(k_sum.sem, 1)
                    pe.wait_ge(v_ready.sem, v_ready.at(b - 1))
                    pe.sem_inc(bearer, 1)
                    pe.matmul(v_ps[0:D, 0:TP], W("a3_qkv", 2 * D, 3 * D), x_t[:, :], start=True, stop=True).then_inc(v_sum.sem, 1)
                    pe.wait_ge(q_ready.sem, q_ready.at(b - 1))
                    pe.sem_inc(bearer, 1)
                    for j in range(NT):
                        mm = pe.matmul(q_ps[:, j * D:(j + 1) * D], x_t[:, j * P:(j + 1) * P], W("a3_qkv", 0, D), start=True, stop=True)
                    mm.then_inc(q_sum.sem, 1)
                    pe.wait_ge(exped.sem, exped.at(b))
                    pe.sem_inc(bearer, 1)
                    pe.wait_ge(kt_ready.sem, kt_ready.at(b - 1))
                    pe.sem_inc(bearer, 1)
                    for j in range(NT):
                        mm = pe.transpose(kt_ps[:, j * D:(j + 1) * D], k_exp[:, j * P:(j + 1) * P], ident[0:D, 0:D])
                    mm.then_inc(kt_sum.sem, 1)
                    pe.wait_ge(kt_ready.sem, kt_ready.at(b))
                    pe.sem_inc(bearer, 1)
                    pe.wait_ge(q_ready.sem, q_ready.at(b))
                    pe.sem_inc(bearer, 1)
                    pe.wait_ge(pair_ready.sem, pair_ready.at(b - 1))
                    pe.sem_inc(bearer, 1)
                    for j in range(NT):
                        mm = pe.matmul(pair_ps[0:D, 0:D], k_tok[0:TK[j], j, :], q_tok[0:TK[j], j, :], start=(j == 0), stop=(j == NT - 1))
                    mm.then_inc(pair_sum.sem, 1)
                    pe.wait_ge(pair_ready.sem, pair_ready.at(b))
                    pe.sem_inc(bearer, 1)
                    pe.wait_ge(v_ready.sem, v_ready.at(b))
                    pe.sem_inc(bearer, 1)
                    pe.wait_ge(o_ready.sem, o_ready.at(b - 1))
                    pe.sem_inc(bearer, 1)
                    pe.matmul(o_ps[0:D, 0:TP], pair[:, :], v_t[:, :], start=True, stop=True).then_inc(o_sum.sem, 1)
                    pe.wait_ge(y_read.sem, y_read.at(b - 1))
                    pe.sem_inc(bearer, 1)
                    pe.wait_ge(lined_up, b * (8 * 16) + (8 * 16 + 1))
                    pe.sem_inc(bearer, 1)
                    for j in range(NT):
                        y = y_ps[0:TK[j], j * D:(j + 1) * D]
                        pe.matmul(y, W("ones_row", 0, TK[j]), W("a3_bias"), start=True, stop=False)
                        for g in range(8):
                            at = 8 * P * j + g
                            mm = pe.matmul(y, in_line[:, at:at + 8 * (TK[j] - 1) + 1:8], W("a3_out", g * D, (g + 1) * D), start=False, stop=(g == 7))
                    mm.then_inc(y_sum.sem, 1)

            @block.scalar
            def _(act):
                act.sem_inc(exped.sem, exped.buffers)
                act.sem_inc(q_ready.sem, q_ready.buffers)
                act.sem_inc(kt_ready.sem, kt_ready.buffers)
                with act.Fori(0, B) as b:
                    act.wait_ge(top.sem, top.at(b))
                    act.sem_inc(bearer, 1)
                    act.wait_ge(kt_sum.sem, kt_sum.at(b - 1))
                    act.sem_inc(bearer, 1)
                    act.wait_ge(pair_ready.sem, pair_ready.at(b - 1))
                    act.sem_inc(bearer, 1)
                    act.activation(k_exp[:, 0:T], k_ps[0:D, 0:T], ACT.Exp, bias=mass[:, 0:1], accum_out=mass[:, 1:2]).then_inc(exped.sem, 1)
                    act.wait_ge(q_sum.sem, q_sum.at(b))
                    act.sem_inc(bearer, 1)
                    act.wait_ge(pair_sum.sem, pair_sum.at(b - 1))
                    act.sem_inc(bearer, 1)
                    act.activation(q_tok[:, :, :], q_ps[:, 0:NT * D].rearrange("p (j d) -> p j d", d=D), ACT.Copy).then_inc(q_ready.sem, 1)
                    act.wait_ge(kt_sum.sem, kt_sum.at(b))
                    act.sem_inc(bearer, 1)
                    act.activation(k_tok[:, :, :], kt_ps[:, 0:NT * D].rearrange("p (j d) -> p j d", d=D), ACT.Copy).then_inc(kt_ready.sem, 1)

            @block.vector
            def _(dve):
                chain = Chain(nc, ctx, dve, "a3_chain")
                chain.link(dve.memset(k_exp[:, T:TP], 0.0))
                first = chain.count
                for x in (top, v_ready, pair_ready, o_ready, y_read):
                    dve.sem_inc(x.sem, x.buffers)
                dve.sem_inc(lined_up, 1)
                with dve.Fori(0, B) as b:
                    chain.loop(b, 1)
                    chain.base = chain.base + first
                    dve.wait_ge(k_sum.sem, k_sum.at(b))
                    dve.tensor_reduce(mass[:, 0:1], k_ps[0:D, 0:T], AX.X, ALU.max, negate=True).then_inc(top.sem, 1)
                    dve.wait_ge(v_sum.sem, v_sum.at(b))
                    dve.wait_ge(o_sum.sem, o_sum.at(b - 1))
                    dve.tensor_copy(v_t[:, :], v_ps[0:D, 0:TP]).then_inc(v_ready.sem, 1)
                    dve.wait_ge(exped.sem, exped.at(b))
                    chain.link(dve.reciprocal(mass[:, 2:3], mass[:, 1:2]))
                    dve.wait_ge(pair_sum.sem, pair_sum.at(b))
                    dve.scalar_tensor_tensor(pair[:, :], pair_ps[0:D, 0:D], mass[:, 2:3], W("head_mask"), ALU.mult, ALU.mult).then_inc(pair_ready.sem, 1)
                    dve.wait_ge(o_sum.sem, o_sum.at(b))
                    dve.wait_ge(lined_up, b * (8 * 16) + 1)
                    dve.tensor_copy(o_t[:, :], o_ps[0:D, 0:T]).then_inc(o_ready.sem, 1)
                    dve.wait_ge(y_sum.sem, y_sum.at(b))
                    dve.tensor_copy(normed[:, b, 0:2, :], y_ps[:, 0:2 * D].rearrange("p (j d) -> p j d", d=D))
                    dve.tensor_copy(normed[0:LAST, b, 2, :], y_ps[0:LAST, 2 * D:3 * D]).then_inc(y_read.sem, 1)
                    chain.close()

        with ExitStack() as ctx:
            attended = sb("a3_attended", [P, B, NT, D], F32, ctx)
            normalise("a3_out_ln", normed, attended, 1e-5, gain="a3_gamma", shift="a3_beta", add_to=state)

        with ExitStack() as ctx:
            plain = sb("m3_plain", [P, B, NT, D], F32, ctx)
            normalise("m3_ln", state, plain, 1e-5)
            normalise("m3_own_ln", plain, normed, 1e-5, gain="m3_gamma", shift="m3_beta")
        experts("m3", "m3_gate", None, ACT.Gelu)


        store()


def pack(inputs):
    w = [np.zeros((P, n), np.float32) for n in N_COLS]
    r = np.zeros((N_ROWS,), np.float32)
    a = {k: np.ascontiguousarray(v) for k, v in inputs.items()}

    def put(name, m):
        part, rows_, at, cols = COLS[name]
        m = np.ascontiguousarray(m)
        assert m.shape == (rows_, cols), (name, m.shape)
        w[part][0:rows_, at:at + cols] = m

    def row(name, v):
        at, cols = ROWS[name]
        r[at:at + cols] = np.ascontiguousarray(v).reshape(-1)

    def with_bias(m, bias):
        return np.concatenate([m, bias.reshape(1, -1)], 0)

    def halves(m):
        return np.concatenate([m[0:P], m[P:2 * P]], 1)

    idx = np.arange(P)
    put("ident", np.eye(P, dtype=np.float32))
    put("tri_lower", np.concatenate([(np.arange(T)[None, :] < (idx[:, None] + j * P)).astype(np.float32) for j in range(NT)], 1))
    put("causal", np.where(idx[None, :] > idx[:, None], np.float32(-BIG), np.float32(0)))
    head = np.arange(D) // 8
    put("head_mask", np.where(head[:, None] == head[None, :], np.float32(D ** -0.5), np.float32(0)))
    put("ones_row", np.ones((1, P), np.float32))
    put("tok_kernel", a["L0_tok_kernel"].transpose(1, 0, 2).reshape(C_IN, TAPS * D))
    for n in ("bias", "beta"):
        row(f"tok_{n}", a[f"L0_tok_{n}"])
    row("tok_mean", a["L0_tok_moving_mean"])
    row("tok_var", a["L0_tok_moving_var"])
    for n in ("pre_g", "pre_b", "post_g", "post_b", "normf_w"):
        row(n, a[f"L0_attn_{n}"])
    for l in range(LAYERS):
        row(f"norm_w{l}", a["L0_attn_norm_w"][l])
        row(f"conv_w{l}", a["L0_attn_conv_w"][l][:, 0, :].T)
        put(f"in_u{l}", a["L0_attn_inproj_w"][l][0:DI].T)
        put(f"in_g{l}", a["L0_attn_inproj_w"][l][DI:].T)
        put(f"conv_b{l}", halves(a["L0_attn_conv_b"][l][:, None]))
        xp = a["L0_attn_xproj_w"][l].T
        put(f"x_bc{l}", halves(np.concatenate([xp[:, RK:]] * 3, 1)))
        put(f"x_dt{l}", halves(xp[:, 0:RK]))
        put(f"dt_w{l}", a["L0_attn_dtproj_w"][l].T)
        put(f"dt_b{l}", halves(a["L0_attn_dtproj_b"][l][:, None]))
        put(f"a_log{l}", halves(a["L0_attn_A_log"][l]))
        put(f"skip{l}", halves(a["L0_attn_D_param"][l][:, None]))
        put(f"out_w{l}", halves(a["L0_attn_outproj_w"][l].T))
    put("route", np.repeat(with_bias(a["L0_ffn_wr"], a["L0_ffn_br"]), P, 1))
    put("f0_w1", with_bias(a["L0_ffn_w1"], a["L0_ffn_b1"]))
    put("f0_w2", halves(a["L0_ffn_w2"]))
    put("f0_b2", a["L0_ffn_b2"].reshape(1, D))
    for n in "qkv":
        put(f"a1_{n}", with_bias(a[f"L1_attn_W{n}"].T, a[f"L1_attn_b{n}"]))
    put("a1_scale", np.repeat(a["L1_attn_scale"].reshape(1, 1), D, 0))
    hl, hb = a["L1_ffn_hl_w"], a["L1_ffn_hl_b"]
    put("hl_tok", with_bias(hl.reshape(D, D).T, hb.reshape(-1)))
    wide = np.zeros((D + 1, P), np.float32)
    wq, wk, wv = (np.zeros((P, n), np.float32) for n in (LE * P, P, D))
    gw = np.zeros((P, 16), np.float32)
    fc1, fc2 = np.zeros((D + 1, D), np.float32), np.zeros((D + 1, D), np.float32)
    for n in range(LH):
        c, d = slice(32 * n, 32 * n + LD), slice(LD * n, LD * n + LD)
        wide[0:D, c], wide[D, c] = hl[n].T, hb[n]
        for e in range(LE):
            wq[c, e * P + 32 * n:e * P + 32 * n + LD] = a["L1_ffn_wq"][n, e].T
        wk[c, c] = a["L1_ffn_wk"][n].T
        wv[c, d] = a["L1_ffn_wv"][n].T
        gw[(n % 2) * D:(n % 2) * D + D, (n // 2) * 8 + (n % 2) * 4:(n // 2) * 8 + (n % 2) * 4 + 4] = a["L1_ffn_gate_w"][n].T
        for m, k in ((fc1, "fc1"), (fc2, "fc2")):
            m[d, d], m[D, d] = a[f"L1_ffn_{k}_w"].T, a[f"L1_ffn_{k}_b"]
    for name, m in (("hl_wide", wide), ("wq_wide", wq), ("wk_wide", wk), ("wv_wide", wv), ("gate_w", gw), ("fc1", fc1), ("fc2", fc2)):
        put(name, m)
    row("gate_b", a["L1_ffn_gate_b"])
    for n in ("ln_g", "ln_b", "fnorm_g", "fnorm_b"):
        row(n, a[f"L1_ffn_{n}"])
    row("fgate", a["L1_ffn_fgate_w"])
    put("a2_q", a["L2_attn_Q"].reshape(AH * AR, D).T)
    put("a2_k", a["L2_attn_K"].reshape(AH * AR, D).T)
    put("a2_vo", a["L2_attn_VO"].transpose(1, 0, 2).reshape(D, AH * D))
    for m, s, gate, gb in (("m2", "L2_ffn", "Wg", "bg"), ("m3", "L3_ffn", "Wr", "br")):
        put(f"{m}_gate", with_bias(a[f"{s}_{gate}"], a[f"{s}_{gb}"]))
        put(f"{m}_w1", with_bias(a[f"{s}_W1"].transpose(1, 0, 2).reshape(D, NE * EH), a[f"{s}_b1"].reshape(-1)))
        put(f"{m}_w2", a[f"{s}_W2"].transpose(1, 0, 2).reshape(EH, NE * D))
        put(f"{m}_b2", a[f"{s}_b2"].reshape(1, -1))
    row("m2_bias", a["L2_ffn_bias"])
    put("a3_qkv", a["L3_attn_Wqkv"])
    put("a3_out", a["L3_attn_Wout"].reshape(8, 8, D).transpose(1, 0, 2).reshape(8, 8 * D))
    put("a3_bias", a["L3_attn_bout"].reshape(1, D))
    row("a3_gamma", a["L3_attn_gamma"])
    row("a3_beta", a["L3_attn_beta"])
    row("m3_gamma", a["L3_ffn_gamma"])
    row("m3_beta", a["L3_ffn_beta"])
    row("countdown", np.arange(NE, 0, -1, dtype=np.float32))
    sel = (np.arange(96)[:, None, None] % 32 == np.arange(32)[None, :, None]) * np.ones((1, 1, P))
    x = np.pad(a["x"].transpose(2, 0, 1), ((0, 0), (0, 0), (0, TP + TAPS - 1 - T_IN)))
    return {"x": np.ascontiguousarray(x), "w": w[0], "w2": w[1], "r": r, "sel": np.ascontiguousarray(sel.astype(np.float32))}


def kernel(**inputs):
    import concourse.bacc as bacc
    from concourse.bass_utils import run_bass_kernel_spmd

    nc = bacc.Bacc("TRN2", target_bir_lowering=False, num_devices=1)
    arrays = pack(inputs)
    args = [nc.dram_tensor(n, v.shape, mybir.dt.from_np(v.dtype), kind="ExternalInput").ap() for n, v in arrays.items()]
    out = nc.dram_tensor("y", (B, T, D), F32, kind="ExternalOutput").ap()
    tower(nc, *args, out)
    r = run_bass_kernel_spmd(nc, [arrays], core_ids=[0])
    return r.results[0]["y"]
```

```python
from contextlib import ExitStack

import numpy as np
import concourse.bass as bass
from concourse import mybir

ALU = mybir.AluOpType
ACT = mybir.ActivationFunctionType
AX = mybir.AxisListType
F32 = mybir.dt.float32
BF16 = mybir.dt.bfloat16

P = 128
B, T_IN, C_IN = 8, 375, 128
TAPS = 3
T = T_IN - TAPS + 1
D = 64
NT = 3
TP = NT * P
LAST = T - 2 * P
TK = [P, P, LAST]
DI, NS, RK, KC, LAYERS = 256, 16, 16, 4, 2
KEEP = max(1, int(0.5 * T)) - 1
LH, LE, LD = 4, 4, 16
AH, AR = 8, 32
NE, EH = 8, 128
PADL = 4
BIG = 1.0e30
N_SEMAPHORES = 256


class Signal:

    def __init__(self, nc, ctx, name, buffers=2):
        self.sem = ctx.enter_context(nc.semaphore(name))
        self.buffers = buffers

    def at(self, step):
        return step + (self.buffers + 1)


class Chain:

    def __init__(self, nc, ctx, eng, name):
        self.sem = ctx.enter_context(nc.semaphore(name))
        self.eng, self.base, self.count = eng, 0, 0

    def loop(self, step, links):
        self.base, self.count, self.links = step * links, 0, links

    def close(self):
        assert self.count == self.links, self.count

    def link(self, ins):
        self.count += 1
        ins.then_inc(self.sem, 1)
        self.eng.wait_ge(self.sem, self.base + self.count)


def column_table():
    names = [("ident", P, P), ("tri_lower", P, NT * T), ("causal", P, P), ("head_mask", D, D), ("ones_row", 1, P)]
    names += [("tok_kernel", C_IN, TAPS * D)]
    for l in range(LAYERS):
        names += [(f"in_u{l}", D, DI), (f"in_g{l}", D, DI), (f"conv_b{l}", P, 2), (f"x_bc{l}", P, 2 * 96), (f"x_dt{l}", P, 2 * RK),
                  (f"dt_w{l}", RK, DI), (f"dt_b{l}", P, 2), (f"a_log{l}", P, 2 * NS), (f"skip{l}", P, 2), (f"out_w{l}", P, 2 * D)]
    names += [("route", D + 1, P), ("f0_w1", D + 1, 4 * D), ("f0_w2", P, 2 * D), ("f0_b2", 1, D)]
    late = len(names)
    names += [("a1_q", D + 1, D), ("a1_k", D + 1, D), ("a1_v", D + 1, D), ("a1_scale", D, 1)]
    names += [("hl_tok", D + 1, D), ("hl_wide", D + 1, P), ("wq_wide", P, LE * P), ("wk_wide", P, P), ("wv_wide", P, D)]
    names += [("gate_w", P, 2 * 8), ("fc1", D + 1, D), ("fc2", D + 1, D)]
    names += [("a2_q", D, AH * AR), ("a2_k", D, AH * AR), ("a2_vo", D, AH * D)]
    for m in ("m2", "m3"):
        names += [(f"{m}_gate", D + 1, NE), (f"{m}_w1", D + 1, NE * EH), (f"{m}_w2", EH, NE * D), (f"{m}_b2", 1, NE * D)]
    names += [("a3_qkv", D, 3 * D), ("a3_out", 8, 8 * D), ("a3_bias", 1, D)]
    table, at = {}, [0, 0]
    for i, (name, rows, cols) in enumerate(names):
        part = int(i >= late)
        table[name] = (part, rows, at[part], cols)
        at[part] += cols
    return table, at


def row_table():
    names = [("tok_bias", D), ("tok_beta", D), ("tok_mean", D), ("tok_var", D), ("pre_g", D), ("pre_b", D), ("post_g", D),
             ("post_b", D), ("norm_w0", D), ("norm_w1", D), ("normf_w", D), ("conv_w0", KC * DI), ("conv_w1", KC * DI),
             ("gate_b", LH * LE), ("ln_g", LD), ("ln_b", LD), ("fnorm_g", LD), ("fnorm_b", LD), ("fgate", LH * D),
             ("m2_bias", NE), ("a3_gamma", D), ("a3_beta", D), ("m3_gamma", D), ("m3_beta", D), ("countdown", NE)]
    table, at = {}, 0
    for name, cols in names:
        table[name] = (at, cols)
        at += cols
    return table, at


COLS, N_COLS = column_table()
ROWS, N_ROWS = row_table()


def tower(nc, x_in, w_in, w2_in, r_in, sel_in, out):
    with ExitStack() as whole:
        def sb(name, shape, dt=F32, ctx=whole):
            return ctx.enter_context(nc.sbuf_tensor(name, shape, dt))

        bearer = whole.enter_context(nc.semaphore("wait_bearer"))
        late_loaded = whole.enter_context(nc.semaphore("late_loaded"))

        def renew_semaphores():
            with ExitStack() as ctx:
                block = ctx.enter_context(nc.Block())

                @block.sync
                def _(sp):
                    sp.sem_clear(range(late_loaded.num + 1, N_SEMAPHORES))

        weights = [sb("early_weights", [P, N_COLS[0]])]
        rows = sb("rows", [P, N_ROWS])
        state = sb("state", [P, B, NT, D])
        normed = sb("normed", [P, B, NT, D])
        scratch = sb("scratch", [P, B, NT, D])
        stat = sb("stat", [P, 4, B * NT * LH])
        flipped = sb("flipped", [D + 1, B, PADL + TP])
        ident_bf = sb("ident_bf", [P, P], BF16)
        causal_bf = sb("causal_bf", [P, P], BF16)

        def pairs(t):
            rest = " ".join("xyz"[0:len(t.shape) - 2])
            return t[tuple([slice(None)] * len(t.shape))].rearrange(f"p (c s) {rest} -> p c s {rest}", s=2)

        def W(name, lo=0, hi=None, rows_=None):
            part, r, at, cols = COLS[name]
            return weights[part][0:(rows_ or r), at + lo:at + (cols if hi is None else hi)]

        def R(name, parts=P):
            at, cols = ROWS[name]
            return rows[0:parts, at:at + cols]

        ident = W("ident")

        with ExitStack() as ctx:
            x_sb = sb("x_sb", [C_IN, B, TP + TAPS - 1], F32, ctx)
            x_sign = sb("x_sign", [C_IN, B, TP + TAPS - 1], BF16, ctx)
            k_sign = sb("k_sign", [C_IN, TAPS * D], BF16, ctx)
            affine = sb("affine", [P, 4, D], F32, ctx)
            conv_ps = ctx.enter_context(nc.psum_tensor("conv_ps", [P, 2, 512], F32))
            loaded = ctx.enter_context(nc.semaphore("tok_loaded"))
            signs = ctx.enter_context(nc.semaphore("tok_signs"))
            root = ctx.enter_context(nc.semaphore("tok_root"))
            var_ready = ctx.enter_context(nc.semaphore("tok_var_ready"))
            conv_done = Signal(nc, ctx, "tok_conv_done")
            placed = Signal(nc, ctx, "tok_placed")
            block = ctx.enter_context(nc.Block())

            @block.sync
            def _(sp):
                sp.dma_start(x_sb[:, :, :], x_in).then_inc(loaded, 16)
                sp.dma_start(weights[0][:, :], w_in).then_inc(loaded, 16)
                sp.dma_start(rows[:, :], r_in.rearrange("(a n) -> a n", a=1).broadcast_to([P, N_ROWS])).then_inc(loaded, 16)

            @block.scalar
            def _(act):
                act.wait_ge(var_ready, 1)
                act.activation(affine[:, 1, :], affine[:, 0, :], ACT.Sqrt).then_inc(root, 1)

            @block.vector
            def _(dve):
                chain = Chain(nc, ctx, dve, "tok_chain")
                dve.sem_inc(placed.sem, placed.buffers)
                dve.wait_ge(loaded, 48)
                dve.tensor_scalar(affine[:, 0, :], R("tok_var"), 1e-3, None, ALU.add).then_inc(var_ready, 1)
                dve.tensor_scalar(k_sign[:, :], W("tok_kernel"), 0.0, 0.5, ALU.is_ge, ALU.subtract).then_inc(signs, 1)
                dve.tensor_scalar(x_sign[:, :, :], x_sb[:, :, :], 0.0, 0.5, ALU.is_ge, ALU.subtract).then_inc(signs, 1)
                dve.tensor_copy(ident_bf[:, :], ident)
                dve.tensor_copy(causal_bf[:, :], W("causal"))
                dve.memset(flipped[D:D + 1, :, :], 1.0)
                dve.memset(flipped[0:D, :, 0:PADL], 0.0)
                chain.link(dve.tensor_tensor(affine[:, 3, :], R("tok_bias"), R("tok_mean"), ALU.subtract))
                dve.wait_ge(root, 1)
                chain.link(dve.reciprocal(affine[:, 2, :], affine[:, 1, :]))
                chain.link(dve.tensor_tensor(affine[:, 3, :], affine[:, 3, :], affine[:, 2, :], ALU.mult))
                chain.link(dve.tensor_tensor(affine[:, 3, :], affine[:, 3, :], R("tok_beta"), ALU.add))
                chain.link(dve.tensor_scalar(affine[:, 2, :], affine[:, 2, :], 4.0, None, ALU.mult))
                scale = affine[:, 2:3, :].broadcast_to([P, NT, D])
                shift = affine[:, 3:4, :].broadcast_to([P, NT, D])
                mul_sem = Chain(nc, ctx, dve, "tok_scaled")
                with dve.Fori(0, B // 2) as c:
                    b = 2 * c
                    mul_sem.loop(c, 2)
                    for s in range(2):
                        dve.wait_ge(conv_done.sem, conv_done.at(b + s))
                        ps = conv_ps[:, s, 0:NT * D].rearrange("p (j d) -> p j d", d=D)
                        mul_sem.link(dve.tensor_tensor(pairs(state)[:, c, s, :, :], ps, scale, ALU.mult))
                        dve.tensor_tensor(pairs(state)[:, c, s, :, :], pairs(state)[:, c, s, :, :], shift, ALU.add).then_inc(placed.sem, 1)
                    mul_sem.close()

            @block.tensor
            def _(pe):
                pe.sem_inc(conv_done.sem, conv_done.buffers)
                pe.wait_ge(signs, 2)
                with pe.Fori(0, B // 2) as c:
                    b = 2 * c
                    for s in range(2):
                        pe.wait_ge(placed.sem, placed.at(b + s - 2))
                        pe.sem_inc(bearer, 1)
                        for j in range(NT):
                            for k in range(TAPS):
                                mm = pe.matmul(conv_ps[:, s, j * D:(j + 1) * D], pairs(x_sign)[:, c, s, j * P + k:j * P + k + P],
                                               k_sign[:, k * D:(k + 1) * D], start=(k == 0), stop=(k == TAPS - 1))
                        mm.then_inc(conv_done.sem, 1)

        def normalise(name, src, dst, eps, centre=True, gain=None, shift=None, add_to=None, width=D):
            with ExitStack() as ctx:
                group = B * NT * D // width
                root = ctx.enter_context(nc.semaphore(f"{name}_root"))
                spread = ctx.enter_context(nc.semaphore(f"{name}_spread"))
                block = ctx.enter_context(nc.Block())

                def v(t):
                    return t[:, :, :, :].rearrange("p b j (g w) -> p (b j g) w", w=width)

                def wide(k):
                    return stat[:, k, 0:group].unsqueeze(2).broadcast_to([P, group, width])

                @block.vector
                def _(dve):
                    chain = Chain(nc, ctx, dve, f"{name}_chain")
                    centred = src
                    if centre:
                        chain.link(dve.tensor_reduce(stat[:, 0, 0:group], v(src), AX.X, ALU.add))
                        chain.link(dve.tensor_scalar(stat[:, 0, 0:group], stat[:, 0, 0:group], 1.0 / width, None, ALU.mult))
                        chain.link(dve.tensor_tensor(v(dst), v(src), wide(0), ALU.subtract))
                        centred = dst
                    chain.link(dve.tensor_tensor(v(scratch), v(centred), v(centred), ALU.mult))
                    chain.link(dve.tensor_reduce(stat[:, 1, 0:group], v(scratch), AX.X, ALU.add))
                    dve.tensor_scalar(stat[:, 1, 0:group], stat[:, 1, 0:group], 1.0 / width, eps, ALU.mult, ALU.add).then_inc(spread, 1)
                    dve.wait_ge(root, 1)
                    chain.link(dve.reciprocal(stat[:, 3, 0:group], stat[:, 2, 0:group]))
                    chain.link(dve.tensor_tensor(v(dst), v(centred), wide(3), ALU.mult))
                    for vec, op in ((gain, ALU.mult), (shift, ALU.add)):
                        if vec is not None:
                            chain.link(dve.tensor_tensor(v(dst), v(dst), R(vec).unsqueeze(1).broadcast_to([P, group, width]), op))
                    if add_to is not None:
                        chain.link(dve.tensor_tensor(v(add_to), v(add_to), v(dst), ALU.add))

                @block.scalar
                def _(act):
                    act.wait_ge(spread, 1)
                    act.activation(stat[:, 2, 0:group], stat[:, 1, 0:group], ACT.Sqrt).then_inc(root, 1)

        def flip(name, src, logits=None, gate=None):
            with ExitStack() as ctx:
                tile = sb(f"{name}_tile", [P, 2, NT, D], F32, ctx)
                turned = sb(f"{name}_turned", [D + 1, 2, TP], F32, ctx)
                ps = ctx.enter_context(nc.psum_tensor(f"{name}_ps", [P, 2, 512], F32))
                lps = ctx.enter_context(nc.psum_tensor(f"{name}_lps", [P, 2, 512], F32))
                staged = Signal(nc, ctx, f"{name}_staged")
                turned_ps = Signal(nc, ctx, f"{name}_turned_ps")
                turned_sb = Signal(nc, ctx, f"{name}_turned_sb")
                kept = Signal(nc, ctx, f"{name}_kept")
                logit_ps = Signal(nc, ctx, f"{name}_logit_ps")
                logit_sb = Signal(nc, ctx, f"{name}_logit_sb")
                ones = ctx.enter_context(nc.semaphore(f"{name}_ones"))
                block = ctx.enter_context(nc.Block())

                @block.gpsimd
                def _(pool):
                    pool.sem_inc(staged.sem, staged.buffers)
                    pool.memset(turned[D:D + 1, :, :], 1.0).then_inc(ones, 1)
                    pool.wait_ge(ones, 1)
                    with pool.Fori(0, B // 2) as c:
                        b = 2 * c
                        for s in range(2):
                            pool.wait_ge(turned_ps.sem, turned_ps.at(b + s - 2))
                            pool.tensor_copy(tile[:, s, :, :], pairs(src)[:, c, s, :, :]).then_inc(staged.sem, 1)

                @block.tensor
                def _(pe):
                    pe.sem_inc(turned_ps.sem, turned_ps.buffers)
                    pe.sem_inc(logit_ps.sem, logit_ps.buffers)
                    pe.wait_ge(ones, 1)
                    with pe.Fori(0, B // 2) as c:
                        b = 2 * c
                        for s in range(2):
                            pe.wait_ge(staged.sem, staged.at(b + s))
                            pe.sem_inc(bearer, 1)
                            pe.wait_ge(turned_sb.sem, turned_sb.at(b + s - 2))
                            pe.sem_inc(bearer, 1)
                            for j in range(NT):
                                mm = pe.transpose(ps[0:D, s, j * P:(j + 1) * P], tile[:, s, j, :], ident)
                            mm.then_inc(turned_ps.sem, 1)
                        for s in range(2):
                            pe.wait_ge(turned_sb.sem, turned_sb.at(b + s))
                            pe.sem_inc(bearer, 1)
                            if logits is not None:
                                pe.wait_ge(logit_sb.sem, logit_sb.at(b + s - 2))
                                pe.sem_inc(bearer, 1)
                                for j in range(NT):
                                    mm = pe.matmul(lps[:, s, j * NE:(j + 1) * NE], turned[:, s, j * P:(j + 1) * P], W(gate),
                                                   start=True, stop=True)
                                mm.then_inc(logit_ps.sem, 1)

                @block.scalar
                def _(act):
                    act.sem_inc(turned_sb.sem, turned_sb.buffers)
                    with act.Fori(0, B // 2) as c:
                        b = 2 * c
                        for s in range(2):
                            act.wait_ge(turned_ps.sem, turned_ps.at(b + s))
                            act.sem_inc(bearer, 1)
                            act.wait_ge(kept.sem, kept.at(b + s - 2))
                            act.sem_inc(bearer, 1)
                            if logits is not None:
                                act.wait_ge(logit_ps.sem, logit_ps.at(b + s - 2))
                                act.sem_inc(bearer, 1)
                            act.activation(turned[0:D, s, :], ps[0:D, s, 0:TP], ACT.Copy).then_inc(turned_sb.sem, 1)

                @block.vector
                def _(dve):
                    dve.sem_inc(kept.sem, kept.buffers)
                    dve.sem_inc(logit_sb.sem, logit_sb.buffers)
                    with dve.Fori(0, B // 2) as c:
                        b = 2 * c
                        for s in range(2):
                            dve.wait_ge(turned_sb.sem, turned_sb.at(b + s))
                            dve.tensor_copy(pairs(flipped)[0:D, c, s, PADL:PADL + TP], turned[0:D, s, :]).then_inc(kept.sem, 1)
                        for s in range(2):
                            if logits is not None:
                                dve.wait_ge(logit_ps.sem, logit_ps.at(b + s))
                                dve.tensor_copy(pairs(logits)[:, c, s, :, :], lps[:, s, 0:NT * NE].rearrange("p (j e) -> p j e", e=NE))\
                                   .then_inc(logit_sb.sem, 1)

        def store():
            with ExitStack() as ctx:
                stored = ctx.enter_context(nc.semaphore("stored"))
                block = ctx.enter_context(nc.Block())

                @block.sync
                def _(sp):
                    for j in range(NT):
                        sp.dma_start(out[:, j * P:j * P + TK[j], :].rearrange("b p d -> p b d"), state[0:TK[j], :, j, :]).then_inc(stored, 16)
                    sp.wait_ge(stored, 16 * NT)

        normalise("a0_ln", state, normed, 1e-5)
        with ExitStack() as mamba:
            mix = sb("mix", [P, B, NT, D], F32, mamba)
            conv_in = sb("conv_in", [P, 2, B, T], F32, mamba)
            gates = sb("gates", [P, 2, B, T], F32, mamba)
            steps = sb("steps", [P, 2, B, T], F32, mamba)
            drive = sb("drive", [P, 2, B, T], F32, mamba)
            bc_parts = sb("bc_parts", [96, B, T], BF16, mamba)
            spread = sb("spread", [96, 2 * NS, P], BF16, mamba)
            tap_w = sb("tap_w", [D, KC, DI], F32, mamba)
            decay = sb("decay", [P, 2, 2 * NS], F32, mamba)
            skip = sb("skip", [P, 2, P], F32, mamba)
            normalise("a0_pre", normed, mix, 1e-5, gain="pre_g", shift="pre_b")

            with ExitStack() as ctx:
                sel_loaded = ctx.enter_context(nc.semaphore("sel_loaded"))
                block = ctx.enter_context(nc.Block())
                sel_f32 = drive[0:96, :, :, :].rearrange("p a b t -> p (a b t)")[:, 0:2 * NS * P]

                @block.sync
                def _(sp):
                    sp.dma_start(sel_f32, sel_in.rearrange("k c m -> k (c m)")).then_inc(sel_loaded, 16)

                @block.vector
                def _(dve):
                    dve.wait_ge(sel_loaded, 16)
                    dve.tensor_copy(spread[:, :, :].rearrange("k c m -> k (c m)"), sel_f32)

            def project(l):
                with ExitStack() as ctx:
                    low_rank = sb(f"low_rank{l}", [RK, T], F32, ctx)
                    rest = sb(f"rest{l}", [96, T], F32, ctx)
                    middle = sb(f"middle{l}", [96, T], BF16, ctx)
                    u_ps = ctx.enter_context(nc.psum_tensor(f"u_ps{l}", [P, 2, 512], F32))
                    g_ps = ctx.enter_context(nc.psum_tensor(f"g_ps{l}", [P, 2, 512], F32))
                    bc_ps = ctx.enter_context(nc.psum_tensor(f"bc_ps{l}", [P, 512], F32))
                    low_ps = ctx.enter_context(nc.psum_tensor(f"low_ps{l}", [P, 512], F32))
                    dt_ps = ctx.enter_context(nc.psum_tensor(f"dt_ps{l}", [P, 2, 512], F32))
                    exps = ctx.enter_context(nc.semaphore(f"decay_exp{l}"))
                    taps = ctx.enter_context(nc.semaphore(f"tap_weights{l}"))

                    def sig(n):
                        return Signal(nc, ctx, f"{n}{l}", 1)

                    u_sum, g_sum, u_done, g_done = sig("u_sum"), sig("g_sum"), sig("u_done"), sig("g_done")
                    bc_sum, low_sum, low_done, dt_sum = sig("bc_sum"), sig("low_sum"), sig("low_done"), sig("dt_sum")
                    bc_read, bc_done, dt_done = sig("bc_read"), sig("bc_done"), sig("dt_done")
                    block = ctx.enter_context(nc.Block())

                    @block.tensor
                    def _(pe):
                        for x in (u_sum, g_sum, bc_sum, low_sum, dt_sum):
                            pe.sem_inc(x.sem, x.buffers)
                        pe.wait_ge(taps, 1)
                        with pe.Fori(0, B) as b:
                            pe.wait_ge(u_done.sem, u_done.at(b - 1))
                            pe.sem_inc(bearer, 1)
                            for h in range(2):
                                for k in range(KC):
                                    at = PADL - (KC - 1) + k
                                    mm = pe.matmul(u_ps[:, h, 0:T], tap_w[:, k, h * P:(h + 1) * P], flipped[0:D, b, at:at + T],
                                                   start=(k == 0), stop=(k == KC - 1))
                            mm.then_inc(u_sum.sem, 1)
                            pe.wait_ge(g_done.sem, g_done.at(b - 1))
                            pe.sem_inc(bearer, 1)
                            for h in range(2):
                                mm = pe.matmul(g_ps[:, h, 0:T], W(f"in_g{l}", h * P, (h + 1) * P), flipped[0:D, b, PADL:PADL + T],
                                               start=True, stop=True)
                            mm.then_inc(g_sum.sem, 1)
                            pe.wait_ge(u_done.sem, u_done.at(b))
                            pe.sem_inc(bearer, 1)
                            pe.wait_ge(low_done.sem, low_done.at(b - 1))
                            pe.sem_inc(bearer, 1)
                            for h in range(2):
                                mm = pe.matmul(low_ps[0:RK, 0:T], W(f"x_dt{l}", h * RK, (h + 1) * RK), conv_in[:, h, b, :],
                                               start=(h == 0), stop=(h == 1))
                            mm.then_inc(low_sum.sem, 1)
                            pe.wait_ge(bc_read.sem, bc_read.at(b - 1))
                            pe.sem_inc(bearer, 1)
                            for h in range(2):
                                mm = pe.matmul(bc_ps[0:96, 0:T], W(f"x_bc{l}", h * 96, (h + 1) * 96), conv_in[:, h, b, :],
                                               start=(h == 0), stop=(h == 1))
                            mm.then_inc(bc_sum.sem, 1)
                            pe.wait_ge(low_done.sem, low_done.at(b))
                            pe.sem_inc(bearer, 1)
                            pe.wait_ge(dt_done.sem, dt_done.at(b - 1))
                            pe.sem_inc(bearer, 1)
                            for h in range(2):
                                mm = pe.matmul(dt_ps[:, h, 0:T], W(f"dt_w{l}", h * P, (h + 1) * P), low_rank[:, :], start=True, stop=True)
                            mm.then_inc(dt_sum.sem, 1)

                    @block.scalar
                    def _(act):
                        for x in (u_done, g_done, low_done):
                            act.sem_inc(x.sem, x.buffers)
                        act.activation(decay[:, 0, :], W(f"a_log{l}"), ACT.Exp).then_inc(exps, 1)
                        with act.Fori(0, B) as b:
                            act.wait_ge(u_sum.sem, u_sum.at(b))
                            act.sem_inc(bearer, 1)
                            for h in range(2):
                                ins = act.activation(conv_in[:, h, b, :], u_ps[:, h, 0:T], ACT.Silu, bias=W(f"conv_b{l}", h, h + 1))
                            ins.then_inc(u_done.sem, 1)
                            act.wait_ge(g_sum.sem, g_sum.at(b))
                            act.sem_inc(bearer, 1)
                            for h in range(2):
                                ins = act.activation(gates[:, h, b, :], g_ps[:, h, 0:T], ACT.Silu)
                            ins.then_inc(g_done.sem, 1)
                            act.wait_ge(low_sum.sem, low_sum.at(b))
                            act.sem_inc(bearer, 1)
                            act.wait_ge(dt_sum.sem, dt_sum.at(b - 1))
                            act.sem_inc(bearer, 1)
                            act.activation(low_rank[:, :], low_ps[0:RK, 0:T], ACT.Copy).then_inc(low_done.sem, 1)

                    @block.vector
                    def _(dve):
                        chain = Chain(nc, ctx, dve, f"project_chain{l}")
                        for x in (bc_read, bc_done, dt_done):
                            dve.sem_inc(x.sem, x.buffers)
                        taps_row = R(f"conv_w{l}", D).rearrange("p (k d) -> p k d", k=KC)
                        dve.tensor_tensor(tap_w[:, :, :], taps_row, W(f"in_u{l}").unsqueeze(1).broadcast_to([D, KC, DI]), ALU.mult)\
                           .then_inc(taps, 1)
                        for h in range(2):
                            dve.tensor_scalar(skip[:, h, :], ident, W(f"skip{l}", h, h + 1), None, ALU.mult)
                        dve.wait_ge(exps, 1)
                        dve.tensor_scalar(decay[:, 1, :], decay[:, 0, :], -1.0, None, ALU.mult)
                        with dve.Fori(0, B) as b:
                            chain.loop(b, 4)
                            dve.wait_ge(bc_sum.sem, bc_sum.at(b))
                            chain.link(dve.tensor_copy(bc_parts[:, b, :], bc_ps[0:96, 0:T]))
                            chain.link(dve.tensor_tensor(rest[:, :], bc_ps[0:96, 0:T], bc_parts[:, b, :], ALU.subtract))
                            dve.tensor_copy(bc_parts[32:64, b, :], rest[32:64, :])
                            chain.link(dve.tensor_copy(middle[64:96, :], rest[64:96, :]))
                            chain.link(dve.tensor_tensor(bc_parts[64:96, b, :], rest[64:96, :], middle[64:96, :], ALU.subtract))
                            chain.close()
                            dve.sem_inc(bc_read.sem, 1)
                            dve.wait_ge(dt_sum.sem, dt_sum.at(b))
                            for h in range(2):
                                ins = dve.tensor_scalar(steps[:, h, b, :], dt_ps[:, h, 0:T], W(f"dt_b{l}", h, h + 1), None, ALU.add)
                            ins.then_inc(dt_done.sem, 1)

            def softplus(l):
                batches = B // 2
                with ExitStack() as ctx:
                    def flat(t):
                        return t[:, :, :, :].rearrange("p b j d -> p (b j d)")[:, 0:batches * T].rearrange("p (b t) -> p b t", b=batches)

                    one_plus, logs = flat(scratch), flat(normed)
                    log_ready = ctx.enter_context(nc.semaphore(f"log_ready{l}"))
                    log_used = ctx.enter_context(nc.semaphore(f"log_used{l}"))
                    block = ctx.enter_context(nc.Block())
                    chunks = [(h, slice(batches * k, batches * k + batches)) for h in range(2) for k in range(2)]

                    @block.scalar
                    def _(act):
                        chain = Chain(nc, ctx, act, f"softplus_chain{l}")
                        for i, (h, bs) in enumerate(chunks):
                            chain.link(act.activation(drive[:, h, bs, :], steps[:, h, bs, :], ACT.Abs))
                            chain.link(act.activation(drive[:, h, bs, :], drive[:, h, bs, :], ACT.Exp, scale=-1.0))
                            if i > 0:
                                act.wait_ge(log_used, i)
                            chain.link(act.activation(one_plus, drive[:, h, bs, :], ACT.Identity, bias=1.0))
                            act.activation(logs, one_plus, ACT.Ln).then_inc(log_ready, 1)

                    @block.vector
                    def _(dve):
                        chain = Chain(nc, ctx, dve, f"steps_chain{l}")
                        for i, (h, bs) in enumerate(chunks):
                            dve.wait_ge(log_ready, i + 1)
                            chain.link(dve.scalar_tensor_tensor(one_plus, one_plus, 1.0, drive[:, h, bs, :], ALU.subtract, ALU.subtract))
                            chain.link(dve.scalar_tensor_tensor(steps[:, h, bs, :], steps[:, h, bs, :], 0.0, logs, ALU.max, ALU.add))
                            dve.tensor_tensor(steps[:, h, bs, :], steps[:, h, bs, :], one_plus, ALU.subtract).then_inc(log_used, 1)
                            dve.wait_ge(log_used, i + 1)
                            dve.tensor_tensor(drive[:, h, bs, :], steps[:, h, bs, :], conv_in[:, h, bs, :], ALU.mult)

            def scan(l):
                units = 2 * NS
                with ExitStack() as ctx:
                    c_all = sb(f"c_all{l}", [P, 2, T], F32, ctx)
                    keep = sb(f"keep{l}", [P, 4, T], F32, ctx)
                    add = scratch[:, :, :, :].rearrange("p b j d -> p (b j d)")[:, 0:4 * T].rearrange("p (s t) -> p s t", s=4)
                    seen = normed[:, :, :, :].rearrange("p b j d -> p (b j d)")[:, 0:4 * T].rearrange("p (s t) -> p s t", s=4)
                    hidden = sb(f"hidden{l}", [P, 4, T], F32, ctx)
                    gated = sb(f"gated{l}", [P, 2, TP], F32, ctx)
                    b_ps = ctx.enter_context(nc.psum_tensor(f"b_ps{l}", [P, 2, 512], F32))
                    c_ps = ctx.enter_context(nc.psum_tensor(f"c_ps{l}", [P, 2, 512], F32))
                    y_ps = ctx.enter_context(nc.psum_tensor(f"y_ps{l}", [P, 2, 512], F32))
                    o_ps = ctx.enter_context(nc.psum_tensor(f"o_ps{l}", [P, 512], F32))

                    def sig(n, buffers):
                        return Signal(nc, ctx, f"{n}{l}", buffers)

                    b_spread, c_spread, c_copied = sig("b_spread", 2), sig("c_spread", 2), sig("c_copied", 2)
                    keep_ready, add_ready, hidden_ready = sig("keep_ready", 4), sig("add_ready", 4), sig("hidden_ready", 4)
                    seen_ready, seen_summed = sig("seen_ready", 4), sig("seen_summed", 4)
                    gated_ready, o_ready, mixed = sig("gated_ready", 1), sig("o_ready", 1), sig("mixed", 1)
                    block = ctx.enter_context(nc.Block())

                    @block.tensor
                    def _(pe):
                        for x in (b_spread, c_spread, seen_summed, o_ready):
                            pe.sem_inc(x.sem, x.buffers)

                        def spread_out(b, n):
                            pe.wait_ge(add_ready.sem, add_ready.at(units * b + 2 * (n - 2) + 1))
                            pe.sem_inc(bearer, 1)
                            pe.matmul(b_ps[:, n % 2, 0:T], spread[:, n, :], bc_parts[:, b, :], start=True, stop=True).then_inc(b_spread.sem, 1)
                            pe.wait_ge(c_copied.sem, c_copied.at(NS * b + n - 2))
                            pe.sem_inc(bearer, 1)
                            pe.matmul(c_ps[:, n % 2, 0:T], spread[:, NS + n, :], bc_parts[:, b, :], start=True, stop=True).then_inc(c_spread.sem, 1)

                        def output(b):
                            pe.wait_ge(gated_ready.sem, gated_ready.at(b))
                            pe.wait_ge(mixed.sem, mixed.at(b - 1))
                            for j in range(NT):
                                for h in range(2):
                                    mm = pe.matmul(o_ps[:, j * D:(j + 1) * D], gated[:, h, j * P:(j + 1) * P], W(f"out_w{l}", h * D, (h + 1) * D),
                                                   start=(h == 0), stop=(h == 1))
                            mm.then_inc(o_ready.sem, 1)

                        def sums(b, follows):
                            spread_out(b, 0)
                            spread_out(b, 1)
                            pe.wait_ge(gated_ready.sem, gated_ready.at(b - 1))
                            pe.sem_inc(bearer, 1)
                            for h in range(2):
                                pe.matmul(y_ps[:, h, 0:T], skip[:, h, :], conv_in[:, h, b, :], start=True, stop=False)
                            for n in range(NS):
                                if n + 2 < NS:
                                    spread_out(b, n + 2)
                                for h in range(2):
                                    pe.wait_ge(seen_ready.sem, seen_ready.at(units * b + 2 * n + h))
                                    pe.matmul(y_ps[:, h, 0:T], ident, seen[:, (2 * n + h) % 4, :], start=False, stop=(n == NS - 1))\
                                      .then_inc(seen_summed.sem, 1)
                                if follows and n == 0:
                                    output(b - 1)

                        sums(0, False)
                        with pe.Fori(1, B) as b:
                            sums(b, True)
                        output(B - 1)

                    @block.scalar
                    def _(act):
                        for x in (c_copied, keep_ready):
                            act.sem_inc(x.sem, x.buffers)
                        with act.Fori(0, B) as b:
                            for n in range(NS):
                                act.wait_ge(c_spread.sem, c_spread.at(NS * b + n))
                                act.wait_ge(seen_ready.sem, seen_ready.at(units * b + 2 * (n - 2) + 1))
                                act.activation(c_all[:, n % 2, :], c_ps[:, n % 2, 0:T], ACT.Copy).then_inc(c_copied.sem, 1)
                                for h in range(2):
                                    u = 2 * n + h
                                    act.wait_ge(hidden_ready.sem, hidden_ready.at(units * b + u - 4))
                                    act.sem_inc(bearer, 1)
                                    act.activation(keep[:, u % 4, :], steps[:, h, b, :], ACT.Exp, scale=decay[:, 1, h * NS + n:h * NS + n + 1])\
                                       .then_inc(keep_ready.sem, 1)

                    @block.vector
                    def _(dve):
                        for x in (add_ready, hidden_ready, gated_ready, mixed):
                            dve.sem_inc(x.sem, x.buffers)
                        dve.memset(gated[:, :, T:TP], 0.0)

                        def inputs(b, u):
                            n, h = u // 2, u % 2
                            dve.wait_ge(b_spread.sem, b_spread.at(NS * b + n))
                            dve.wait_ge(hidden_ready.sem, hidden_ready.at(units * b + u - 4))
                            dve.tensor_tensor(add[:, u % 4, :], drive[:, h, b, :], b_ps[:, n % 2, 0:T], ALU.mult).then_inc(add_ready.sem, 1)

                        def gate(b):
                            dve.wait_ge(seen_summed.sem, seen_summed.at(units * b + units - 1))
                            dve.wait_ge(o_ready.sem, o_ready.at(b - 1))
                            for h in range(2):
                                ins = dve.tensor_tensor(gated[:, h, 0:T], gates[:, h, b, :], y_ps[:, h, 0:T], ALU.mult)
                            ins.then_inc(gated_ready.sem, 1)

                        def add_output(b):
                            dve.wait_ge(o_ready.sem, o_ready.at(b))
                            dve.tensor_tensor(mix[:, b, :, :], mix[:, b, :, :], o_ps[:, 0:NT * D].rearrange("p (j d) -> p j d", d=D), ALU.add)\
                               .then_inc(mixed.sem, 1)

                        def recur(b, follows):
                            inputs(b, 0)
                            for u in range(units):
                                if u + 1 < units:
                                    inputs(b, u + 1)
                                dve.wait_ge(keep_ready.sem, keep_ready.at(units * b + u))
                                dve.wait_ge(add_ready.sem, add_ready.at(units * b + u))
                                dve.wait_ge(seen_ready.sem, seen_ready.at(units * b + u - 4))
                                dve.tensor_tensor_scan(hidden[:, u % 4, :], keep[:, u % 4, :], add[:, u % 4, :], 0.0, ALU.mult, ALU.add)\
                                   .then_inc(hidden_ready.sem, 1)
                                if follows and u == 1:
                                    gate(b - 1)
                                if follows and u == 6:
                                    add_output(b - 1)

                        recur(0, False)
                        with dve.Fori(1, B) as b:
                            recur(b, True)
                        gate(B - 1)
                        add_output(B - 1)

                    @block.gpsimd
                    def _(pool):
                        pool.sem_inc(seen_ready.sem, seen_ready.buffers)
                        with pool.Fori(0, B) as b:
                            for u in range(units):
                                pool.wait_ge(hidden_ready.sem, hidden_ready.at(units * b + u))
                                if u % 2 == 0:
                                    pool.wait_ge(c_copied.sem, c_copied.at(NS * b + u // 2))
                                pool.wait_ge(seen_summed.sem, seen_summed.at(units * b + u - 4))
                                pool.tensor_tensor(seen[:, u % 4, :], hidden[:, u % 4, :], c_all[:, (u // 2) % 2, :], ALU.mult)\
                                    .then_inc(seen_ready.sem, 1)

            for l in range(LAYERS):
                normalise(f"rms{l}", mix, normed, 1e-5, centre=False, gain=f"norm_w{l}")
                flip(f"a0_flip{l}", normed)
                project(l)
                softplus(l)
                scan(l)
            normalise("a0_normf", mix, normed, 1e-5, centre=False, gain="normf_w")
            normalise("a0_post", normed, mix, 1e-5, gain="post_g", shift="post_b", add_to=state)

        renew_semaphores()
        weights.append(sb("late_weights", [P, N_COLS[1]]))
        with ExitStack() as ctx:
            block = ctx.enter_context(nc.Block())

            @block.sync
            def _(sp):
                sp.dma_start(weights[1][:, :], w2_in).then_inc(late_loaded, 16)

        normalise("f0_ln", state, normed, 1e-5)
        flip("f0_flip", normed)
        with ExitStack() as ctx:
            score = sb("score", [P, 2, TP], F32, ctx)
            compared = sb("compared", [P, T], F32, ctx)
            count = sb("count", [P, 2, 3, NT], F32, ctx)
            factor = sb("factor", [P, 2, NT], F32, ctx)
            ffn_hidden = sb("ffn_hidden", [P, 2, 2, TP], F32, ctx)
            routed = sb("routed", [P, 2, NT, D], F32, ctx)
            score_ps = ctx.enter_context(nc.psum_tensor("score_ps", [P, 2, 512], F32))
            hidden_ps = ctx.enter_context(nc.psum_tensor("hidden_ps", [P, 2, 2, 512], F32))
            out_ps = ctx.enter_context(nc.psum_tensor("out_ps", [P, 2, 512], F32))
            score_sum, score_read = Signal(nc, ctx, "score_sum"), Signal(nc, ctx, "score_read")
            hidden_sum, hidden_done = Signal(nc, ctx, "hidden_sum"), Signal(nc, ctx, "hidden_done")
            out_sum, out_read = Signal(nc, ctx, "out_sum"), Signal(nc, ctx, "out_read")
            ranked = Signal(nc, ctx, "ranked")
            block = ctx.enter_context(nc.Block())

            @block.tensor
            def _(pe):
                for x in (score_sum, hidden_sum, out_sum):
                    pe.sem_inc(x.sem, x.buffers)
                with pe.Fori(0, B // 2) as c:
                    b = 2 * c
                    for s in range(2):
                        x = pairs(flipped)[0:D + 1, c, s, PADL:PADL + TP]
                        pe.wait_ge(score_read.sem, score_read.at(b + s - 2))
                        pe.sem_inc(bearer, 1)
                        pe.matmul(score_ps[:, s, 0:TP], W("route"), x, start=True, stop=True).then_inc(score_sum.sem, 1)
                        pe.wait_ge(hidden_done.sem, hidden_done.at(b + s - 2))
                        pe.sem_inc(bearer, 1)
                        for h in range(2):
                            mm = pe.matmul(hidden_ps[:, s, h, 0:TP], W("f0_w1", h * P, (h + 1) * P), x, start=True, stop=True)
                        mm.then_inc(hidden_sum.sem, 1)
                    for s in range(2):
                        pe.wait_ge(hidden_done.sem, hidden_done.at(b + s))
                        pe.sem_inc(bearer, 1)
                        pe.wait_ge(out_read.sem, out_read.at(b + s - 2))
                        pe.sem_inc(bearer, 1)
                        for j in range(NT):
                            o = out_ps[:, s, j * D:(j + 1) * D]
                            pe.matmul(o, W("ones_row"), W("f0_b2"), start=True, stop=False)
                            for h in range(2):
                                mm = pe.matmul(o, ffn_hidden[:, s, h, j * P:(j + 1) * P], W("f0_w2", h * D, (h + 1) * D), start=False, stop=(h == 1))
                        mm.then_inc(out_sum.sem, 1)

            @block.scalar
            def _(act):
                act.sem_inc(score_read.sem, score_read.buffers)
                act.sem_inc(hidden_done.sem, hidden_done.buffers)
                with act.Fori(0, B // 2) as c:
                    b = 2 * c
                    for s in range(2):
                        act.wait_ge(score_sum.sem, score_sum.at(b + s))
                        act.sem_inc(bearer, 1)
                        act.wait_ge(ranked.sem, ranked.at(b + s - 2))
                        act.sem_inc(bearer, 1)
                        act.activation(score[:, s, :], score_ps[:, s, 0:TP], ACT.Copy).then_inc(score_read.sem, 1)
                        act.wait_ge(hidden_sum.sem, hidden_sum.at(b + s))
                        act.sem_inc(bearer, 1)
                        act.wait_ge(out_sum.sem, out_sum.at(b + s - 2))
                        act.sem_inc(bearer, 1)
                        act.activation(ffn_hidden[:, s, :, :], hidden_ps[:, s, :, 0:TP], ACT.Gelu_apprx_tanh).then_inc(hidden_done.sem, 1)

            @block.vector
            def _(dve):
                chain = Chain(nc, ctx, dve, "route_chain")
                dve.sem_inc(ranked.sem, ranked.buffers)
                dve.sem_inc(out_read.sem, out_read.buffers)
                with dve.Fori(0, B // 2) as c:
                    b = 2 * c
                    chain.loop(c, 2 * (3 * NT + 2 + NT))
                    for s in range(2):
                        dve.wait_ge(score_read.sem, score_read.at(b + s))
                        for j in range(NT):
                            own = count[:, s, 2, j:j + 1]
                            chain.link(dve.scalar_tensor_tensor(compared[:, 0:P], score[:, s, j * P:(j + 1) * P], 1.0, ident, ALU.mult, ALU.mult,
                                                                accum_out=own))
                            chain.link(dve.tensor_scalar(compared[:, :], score[:, s, 0:T], own, None, ALU.is_gt, ALU.add,
                                                         accum_out=count[:, s, 0, j:j + 1]))
                            chain.link(dve.scalar_tensor_tensor(compared[:, :], score[:, s, 0:T], own, W("tri_lower", j * T, (j + 1) * T),
                                                                ALU.is_equal, ALU.mult, accum_out=count[:, s, 1, j:j + 1]))
                        chain.link(dve.tensor_tensor(count[:, s, 0, :], count[:, s, 0, :], count[:, s, 1, :], ALU.add))
                        chain.link(dve.scalar_tensor_tensor(factor[:, s, :], count[:, s, 0, :], KEEP - 0.5, count[:, s, 2, :], ALU.is_lt, ALU.mult))
                        dve.sem_inc(ranked.sem, 1)
                    for s in range(2):
                        dve.wait_ge(out_sum.sem, out_sum.at(b + s))
                        for j in range(NT):
                            chain.link(dve.scalar_tensor_tensor(routed[:, s, j, :], out_ps[:, s, j * D:(j + 1) * D], factor[:, s, j:j + 1],
                                                                pairs(normed)[:, c, s, j, :], ALU.mult, ALU.add))
                        dve.tensor_tensor(pairs(state)[:, c, s, :, :], pairs(state)[:, c, s, :, :], routed[:, s, :, :], ALU.add)\
                           .then_inc(out_read.sem, 1)
                    chain.close()

        def attention(name, iterations, units, causal, width, group, q_of, k_of, v_of, prepare, finish, ctx):
            steps, batches = units * NT, B // iterations
            tile = sb(f"{name}_tile", [P, batches, NT, D], F32, ctx)
            probs = sb(f"{name}_probs", [P, 3, TP], F32, ctx)
            turned = sb(f"{name}_turned", [P, 2, TP], F32, ctx)
            neg_max = sb(f"{name}_neg_max", [P, 3], F32, ctx)
            s_ps = ctx.enter_context(nc.psum_tensor(f"{name}_s_ps", [P, NT, 512], F32))
            t_ps = ctx.enter_context(nc.psum_tensor(f"{name}_t_ps", [P, 2, 512], F32))
            o_ps = ctx.enter_context(nc.psum_tensor(f"{name}_o_ps", [P, 2, 512], F32))
            x_ps = ctx.enter_context(nc.psum_tensor(f"{name}_x_ps", [P, 512], F32))

            def sig(n, buffers):
                return Signal(nc, ctx, f"{name}_{n}", buffers)

            staged, flipped_sum, projected = sig("staged", 1), sig("flipped_sum", 1), sig("projected", 2)
            ready_act, ready_dve = sig("ready_act", 1), sig("ready_dve", 1)
            scores_sum, max_ready, probs_ready = sig("scores_sum", 3), sig("max_ready", 3), sig("probs_ready", 3)
            turned_sum, turned_dve, turned_act = sig("turned_sum", 3), sig("turned_dve", 1), sig("turned_act", 1)
            product_sum, finished = sig("product_sum", 3), sig("finished", 2)
            block = ctx.enter_context(nc.Block())
            used = (s_ps, t_ps, o_ps, x_ps, flipped_sum, projected, ready_act, ready_dve, finished)

            def keys(qt):
                return range(qt + 1) if causal else range(NT)

            def score_width(qt):
                return min((qt + 1) * P, T) if causal else T

            @block.gpsimd
            def _(pool):
                pool.sem_inc(staged.sem, staged.buffers)
                with pool.Fori(0, iterations) as c:
                    pool.wait_ge(flipped_sum.sem, flipped_sum.at(c - 1))
                    for s in range(batches):
                        source = pairs(normed)[:, c, s, :, :] if batches == 2 else normed[:, c, :, :]
                        ins = pool.tensor_copy(tile[:, s, :, :], source)
                    ins.then_inc(staged.sem, 1)

            @block.tensor
            def _(pe):
                for x in (flipped_sum, projected, scores_sum, turned_sum, product_sum):
                    pe.sem_inc(x.sem, x.buffers)

                def scores(c, i):
                    u, qt = i // NT, i % NT
                    w = score_width(qt)
                    pe.wait_ge(probs_ready.sem, probs_ready.at(steps * c + i - 3))
                    mm = pe.matmul(s_ps[:, i % 3, 0:w], q_of(u, qt), k_of(u, w), start=True, stop=not causal)
                    if causal:
                        lo, n = qt * P, TK[qt]
                        mm = pe.matmul(s_ps[:, i % 3, lo:lo + n], ident_bf[:, :], causal_bf[:, 0:n], start=False, stop=True)
                    mm.then_inc(scores_sum.sem, 1)

                def turn(c, i):
                    pe.wait_ge(probs_ready.sem, probs_ready.at(steps * c + i))
                    copied = (turned_dve, turned_act)[i % 2]
                    pe.wait_ge(copied.sem, copied.at(steps // 2 * c + i // 2 - 1))
                    for kt in keys(i % NT):
                        mm = pe.transpose(t_ps[:, i % 2, kt * P:(kt + 1) * P], probs[:, i % 3, kt * P:(kt + 1) * P], ident)
                    mm.then_inc(turned_sum.sem, 1)

                def products(c, i):
                    u, qt = i // NT, i % NT
                    copied = (turned_dve, turned_act)[i % 2]
                    if u % group == 0 and qt == 0:
                        pe.wait_ge(finished.sem, finished.at(units // group * c + u // group - 2))
                    pe.wait_ge(copied.sem, copied.at(steps // 2 * c + i // 2))
                    o = ((u % group) * NT + qt) * width
                    for kt in keys(qt):
                        mm = pe.matmul(o_ps[:, (u // group) % 2, o:o + width], turned[:, i % 2, kt * P:(kt + 1) * P], v_of(u, kt),
                                       start=(kt == 0), stop=(kt == keys(qt)[-1]))
                    mm.then_inc(product_sum.sem, 1)

                with pe.Fori(0, iterations) as c:
                    pe.wait_ge(staged.sem, staged.at(c))
                    pe.sem_inc(bearer, 1)
                    for s in range(batches):
                        for j in range(NT):
                            to = (x_ps, t_ps[:, 0, :])[s]
                            mm = pe.transpose(to[0:D, j * P:(j + 1) * P], tile[:, s, j, :], ident)
                    mm.then_inc(flipped_sum.sem, 1)
                    prepare["pe"](pe, c, *used)
                    scores(c, 0)
                    scores(c, 1)
                    for i in range(steps):
                        if i + 2 < steps:
                            scores(c, i + 2)
                        turn(c, i)
                        if i > 0:
                            products(c, i - 1)
                    products(c, steps - 1)

            @block.scalar
            def _(act):
                for x in (ready_act, probs_ready, turned_act):
                    act.sem_inc(x.sem, x.buffers)

                def exp(c, i):
                    w = score_width(i % NT)
                    act.wait_ge(turned_sum.sem, turned_sum.at(steps * c + i - 3))
                    act.wait_ge(max_ready.sem, max_ready.at(steps * c + i))
                    act.activation(probs[:, i % 3, 0:w], s_ps[:, i % 3, 0:w], ACT.Exp, bias=neg_max[:, i % 3:i % 3 + 1])\
                       .then_inc(probs_ready.sem, 1)

                with act.Fori(0, iterations) as c:
                    act.wait_ge(product_sum.sem, product_sum.at(steps * c - 1))
                    prepare["act"](act, c, *used)
                    exp(c, 0)
                    for i in range(steps):
                        if i + 1 < steps:
                            exp(c, i + 1)
                        if i % 2 == 1:
                            n = P * len(keys(i % NT))
                            act.wait_ge(product_sum.sem, product_sum.at(steps * c + i - 2))
                            act.wait_ge(turned_sum.sem, turned_sum.at(steps * c + i))
                            act.activation(turned[:, 1, 0:n], t_ps[:, 1, 0:n], ACT.Copy).then_inc(turned_act.sem, 1)

            @block.vector
            def _(dve):
                chain = Chain(nc, ctx, dve, f"{name}_chain")
                prepare["once"](dve)
                chain.link(dve.memset(probs[:, :, :], 0.0))
                first = chain.count
                for x in (ready_dve, max_ready, turned_dve, finished):
                    dve.sem_inc(x.sem, x.buffers)

                def maximum(c, i):
                    dve.wait_ge(scores_sum.sem, scores_sum.at(steps * c + i))
                    dve.tensor_reduce(neg_max[:, i % 3:i % 3 + 1], s_ps[:, i % 3, 0:score_width(i % NT)], AX.X, ALU.max, negate=True)\
                       .then_inc(max_ready.sem, 1)

                def finish_group(c, i):
                    u = i // NT
                    if i % NT == NT - 1 and u % group == group - 1:
                        dve.wait_ge(product_sum.sem, product_sum.at(steps * c + i))
                        finish(dve, chain, c, u // group, o_ps[:, (u // group) % 2, 0:group * NT * width]).then_inc(finished.sem, 1)

                with dve.Fori(0, iterations) as c:
                    chain.loop(c, finish.links * (units // group))
                    chain.base = chain.base + first
                    prepare["dve"](dve, c, *used)
                    maximum(c, 0)
                    maximum(c, 1)
                    for i in range(steps):
                        if i + 2 < steps:
                            maximum(c, i + 2)
                        if i % 2 == 0:
                            n = P * len(keys(i % NT))
                            dve.wait_ge(product_sum.sem, product_sum.at(steps * c + i - 2))
                            dve.wait_ge(turned_sum.sem, turned_sum.at(steps * c + i))
                            dve.tensor_copy(turned[:, 0, 0:n], t_ps[:, 0, 0:n]).then_inc(turned_dve.sem, 1)
                        if i > 1:
                            finish_group(c, i - 2)
                    for i in range(steps - 2, steps):
                        finish_group(c, i)
                    chain.close()

        normalise("a1_ln", state, normed, 1e-5)
        with ExitStack() as ctx:
            x_t = sb("a1_x", [D + 1, 2, TP], F32, ctx)
            q_t = sb("a1_q", [D, 2, TP], F32, ctx)
            k_t = sb("a1_k", [D, 2, TP], F32, ctx)
            values = sb("a1_values", [P, 2, NT, D + 1], F32, ctx)
            inverse = sb("a1_inverse", [D, 1], F32, ctx)
            sums = sb("a1_sums", [P, NT], F32, ctx)
            weighted = sb("a1_weighted", [P, NT, D], F32, ctx)

            def once(dve):
                dve.wait_ge(late_loaded, 16)
                dve.memset(x_t[D:D + 1, :, :], 1.0)
                dve.memset(values[:, :, :, D:D + 1], 1.0)
                dve.reciprocal(inverse[:, :], W("a1_scale"))

            def prepare_pe(pe, c, s_ps, t_ps, o_ps, x_ps, flipped_sum, projected, ready_act, ready_dve, finished):
                pe.wait_ge(finished.sem, finished.at(2 * c - 1))
                pe.wait_ge(ready_dve.sem, ready_dve.at(2 * c))
                pe.sem_inc(bearer, 1)
                q_banks, k_banks, v_banks = (s_ps[:, 0, :], s_ps[:, 1, :]), (s_ps[:, 2, :], x_ps), (o_ps[:, 0, :], o_ps[:, 1, :])
                for s in range(2):
                    pe.matmul(q_banks[s][0:D, 0:TP], W("a1_q"), x_t[:, s, :], start=True, stop=True)
                    pe.matmul(k_banks[s][0:D, 0:TP], W("a1_k"), x_t[:, s, :], start=True, stop=True)
                    for j in range(NT):
                        mm = pe.matmul(v_banks[s][:, j * D:(j + 1) * D], x_t[:, s, j * P:(j + 1) * P], W("a1_v"), start=True, stop=True)
                mm.then_inc(projected.sem, 1)
                pe.wait_ge(ready_dve.sem, ready_dve.at(2 * c + 1))
                pe.wait_ge(ready_act.sem, ready_act.at(c))
                pe.sem_inc(bearer, 1)

            def prepare_act(act, c, s_ps, t_ps, o_ps, x_ps, flipped_sum, projected, ready_act, ready_dve, finished):
                act.wait_ge(projected.sem, projected.at(c))
                act.activation(values[:, 0, :, 0:D], o_ps[:, 0, 0:NT * D].rearrange("p (j d) -> p j d", d=D), ACT.Copy)
                act.activation(values[:, 1, :, 0:D], o_ps[:, 1, 0:NT * D].rearrange("p (j d) -> p j d", d=D), ACT.Copy)
                act.activation(k_t[:, 1, :], x_ps[0:D, 0:TP], ACT.Copy).then_inc(ready_act.sem, 1)

            def prepare_dve(dve, c, s_ps, t_ps, o_ps, x_ps, flipped_sum, projected, ready_act, ready_dve, finished):
                dve.wait_ge(flipped_sum.sem, flipped_sum.at(c))
                dve.tensor_copy(x_t[0:D, 0, :], x_ps[0:D, 0:TP])
                dve.tensor_copy(x_t[0:D, 1, :], t_ps[0:D, 0, 0:TP]).then_inc(ready_dve.sem, 1)
                dve.wait_ge(projected.sem, projected.at(c))
                dve.tensor_scalar(q_t[:, :, :], s_ps[0:D, 0:2, 0:TP], inverse[:, :], None, ALU.mult)
                dve.tensor_copy(k_t[:, 0, :], s_ps[0:D, 2, 0:TP]).then_inc(ready_dve.sem, 1)

            def finish(dve, chain, c, n, products):
                o = products.rearrange("p (j w) -> p j w", w=D + 1)
                chain.link(dve.reciprocal(sums[:, :], o[:, :, D]))
                chain.link(dve.tensor_tensor(weighted[:, :, :], o[:, :, 0:D], sums[:, :].unsqueeze(2).broadcast_to([P, NT, D]), ALU.mult))
                return dve.tensor_tensor(pairs(state)[:, c, n, :, :], pairs(state)[:, c, n, :, :], weighted[:, :, :], ALU.add)

            finish.links = 2
            attention("a1", B // 2, 2, False, D + 1, 1, lambda u, qt: q_t[:, u, qt * P:(qt + 1) * P], lambda u, w: k_t[:, u, 0:w],
                      lambda u, kt: values[:, u, kt, :],
                      {"pe": prepare_pe, "act": prepare_act, "dve": prepare_dve, "once": once}, finish, ctx)

        def small_softmax(name, logits, groups, n):
            with ExitStack() as ctx:
                top = sb(f"{name}_top", [P, groups], F32, ctx)
                total = sb(f"{name}_total", [P, groups], F32, ctx)
                shifted = ctx.enter_context(nc.semaphore(f"{name}_shifted"))
                exped = ctx.enter_context(nc.semaphore(f"{name}_exped"))
                block = ctx.enter_context(nc.Block())

                def wide(t):
                    return t[:, :].unsqueeze(2).broadcast_to([P, groups, n])

                @block.vector
                def _(dve):
                    chain = Chain(nc, ctx, dve, f"{name}_chain")
                    chain.link(dve.tensor_reduce(top[:, :], logits, AX.X, ALU.max))
                    dve.tensor_tensor(logits, logits, wide(top), ALU.subtract).then_inc(shifted, 1)
                    dve.wait_ge(exped, 1)
                    chain.link(dve.tensor_reduce(total[:, :], logits, AX.X, ALU.add))
                    chain.link(dve.reciprocal(total[:, :], total[:, :]))
                    chain.link(dve.tensor_tensor(logits, logits, wide(total), ALU.mult))

                @block.scalar
                def _(act):
                    act.wait_ge(shifted, 1)
                    act.activation(logits, logits, ACT.Exp).then_inc(exped, 1)

        renew_semaphores()

        normalise("f1_ln", state, normed, 1e-5)
        with ExitStack() as f1:
            inputs_tok = sb("f1_inputs", [P, B, NT, D], F32, f1)
            answers = sb("f1_answers", [P, B, NT, LH, LE * LD], F32, f1)
            mixed = sb("f1_mixed", [P, B, NT, D], F32, f1)
            with ExitStack() as ctx:
                x_t = sb("f1_x", [D + 1, TP], F32, ctx)
                wide_t = sb("f1_wide", [P, TP], F32, ctx)
                q_t = sb("f1_q", [P, LE, TP], F32, ctx)
                k_t = sb("f1_k", [P, LH, TP], F32, ctx)
                values = sb("f1_values", [P, NT, LH, LD + 1], F32, ctx)
                present = sb("f1_present", [P, NT, LH, LD], F32, ctx)
                sums = sb("f1_sums", [P, LE * NT], F32, ctx)
                weighted = sb("f1_weighted", [P, LE * NT, LD], F32, ctx)

                def once(dve):
                    dve.memset(k_t[:, :, :], 0.0)
                    dve.memset(x_t[D:D + 1, :], 1.0)
                    dve.memset(values[:, :, :, LD:LD + 1], 1.0)

                def prepare_pe(pe, b, s_ps, t_ps, o_ps, x_ps, flipped_sum, projected, ready_act, ready_dve, finished):
                    pe.wait_ge(ready_dve.sem, ready_dve.at(3 * b))
                    pe.sem_inc(bearer, 1)
                    pe.matmul(s_ps[:, 0, 0:TP], W("hl_wide"), x_t[:, :], start=True, stop=True)
                    for j in range(NT):
                        mm = pe.matmul(s_ps[:, 1, j * D:(j + 1) * D], x_t[:, j * P:(j + 1) * P], W("hl_tok"), start=True, stop=True)
                    mm.then_inc(projected.sem, 1)
                    pe.wait_ge(ready_act.sem, ready_act.at(2 * b))
                    pe.sem_inc(bearer, 1)
                    pe.wait_ge(ready_dve.sem, ready_dve.at(3 * b + 1))
                    pe.sem_inc(bearer, 1)
                    for e, o in enumerate((s_ps[:, 0, 0:TP], s_ps[:, 1, 0:TP], s_ps[:, 2, 0:TP], x_ps[:, 0:TP])):
                        pe.matmul(o, W("wq_wide", e * P, (e + 1) * P), wide_t[:, :], start=True, stop=True)
                    pe.matmul(t_ps[:, 0, 0:TP], W("wk_wide"), wide_t[:, :], start=True, stop=True)
                    for j in range(NT):
                        mm = pe.matmul(t_ps[:, 1, j * D:(j + 1) * D], wide_t[:, j * P:(j + 1) * P], W("wv_wide"), start=True, stop=True)
                    mm.then_inc(projected.sem, 1)
                    pe.wait_ge(ready_act.sem, ready_act.at(2 * b + 1))
                    pe.sem_inc(bearer, 1)
                    pe.wait_ge(ready_dve.sem, ready_dve.at(3 * b + 2))
                    pe.sem_inc(bearer, 1)

                def prepare_act(act, b, s_ps, t_ps, o_ps, x_ps, flipped_sum, projected, ready_act, ready_dve, finished):
                    act.wait_ge(projected.sem, projected.at(2 * b))
                    act.sem_inc(bearer, 1)
                    act.activation(wide_t[:, :], s_ps[:, 0, 0:TP], ACT.Copy).then_inc(ready_act.sem, 1)
                    act.wait_ge(projected.sem, projected.at(2 * b + 1))
                    act.sem_inc(bearer, 1)
                    for n in range(LH):
                        rows_n = slice(32 * n, 32 * n + 32)
                        ins = act.activation(k_t[rows_n, n, :], t_ps[rows_n, 0, 0:TP], ACT.Copy)
                    ins.then_inc(ready_act.sem, 1)

                def prepare_dve(dve, b, s_ps, t_ps, o_ps, x_ps, flipped_sum, projected, ready_act, ready_dve, finished):
                    dve.wait_ge(flipped_sum.sem, flipped_sum.at(b))
                    dve.tensor_copy(x_t[0:D, :], x_ps[0:D, 0:TP]).then_inc(ready_dve.sem, 1)
                    dve.wait_ge(projected.sem, projected.at(2 * b))
                    heads = s_ps[:, 1, 0:NT * D]
                    dve.tensor_scalar(present[:, :, :, :].rearrange("p j n d -> p (j n d)"), heads, 0.0, None, ALU.not_equal)
                    dve.tensor_copy(inputs_tok[:, b, :, :], heads.rearrange("p (j d) -> p j d", d=D)).then_inc(ready_dve.sem, 1)
                    dve.wait_ge(projected.sem, projected.at(2 * b + 1))
                    dve.tensor_scalar(q_t[:, 0:3, :], s_ps[:, :, 0:TP], float(LD) ** 0.5, None, ALU.mult)
                    dve.tensor_scalar(q_t[:, 3, :], x_ps[:, 0:TP], float(LD) ** 0.5, None, ALU.mult)
                    dve.tensor_copy(values[:, :, :, 0:LD], t_ps[:, 1, 0:NT * D].rearrange("p (j n d) -> p j n d", n=LH, d=LD))\
                       .then_inc(ready_dve.sem, 1)

                def finish(dve, chain, b, n, products):
                    o = products.rearrange("p (g w) -> p g w", w=LD + 1)
                    chain.link(dve.reciprocal(sums[:, :], o[:, :, LD]))
                    chain.link(dve.tensor_tensor(weighted[:, :, :], o[:, :, 0:LD], sums[:, :].unsqueeze(2).broadcast_to([P, LE * NT, LD]), ALU.mult))
                    return dve.tensor_tensor(answers[:, b, :, n, :].rearrange("p j (e d) -> p e j d", e=LE),
                                             weighted[:, :, :].rearrange("p (e j) d -> p e j d", e=LE),
                                             present[:, :, n, :].unsqueeze(1).broadcast_to([P, LE, NT, LD]), ALU.mult)

                finish.links = 2
                attention("f1", B, LH * LE, True, LD + 1, LE,
                          lambda u, qt: q_t[:, u % LE, qt * P:(qt + 1) * P],
                          lambda u, w: k_t[:, u // LE, 0:w],
                          lambda u, kt: values[:, kt, u // LE, :],
                          {"pe": prepare_pe, "act": prepare_act, "dve": prepare_dve, "once": once}, finish, ctx)

            gates1 = sb("f1_gates", [P, B, NT, LH * LE], F32, f1)
            with ExitStack() as ctx:
                tile = sb("g1_tile", [P, NT, LH * D], F32, ctx)
                turned = sb("g1_turned", [P, 2, TP], F32, ctx)
                turned_ps = ctx.enter_context(nc.psum_tensor("g1_turned_ps", [P, 2, 512], F32))
                logit_ps = ctx.enter_context(nc.psum_tensor("g1_logit_ps", [P, 512], F32))
                staged, turned_sum, copied = Signal(nc, ctx, "g1_staged", 1), Signal(nc, ctx, "g1_turned_sum", 1), Signal(nc, ctx, "g1_copied", 1)
                logit_sum, logit_read = Signal(nc, ctx, "g1_logit_sum", 1), Signal(nc, ctx, "g1_logit_read", 1)
                block = ctx.enter_context(nc.Block())

                @block.gpsimd
                def _(pool):
                    pool.sem_inc(staged.sem, staged.buffers)
                    with pool.Fori(0, B) as b:
                        pool.wait_ge(turned_sum.sem, turned_sum.at(b - 1))
                        pool.tensor_copy(tile[:, :, :], answers[:, b, :, :, :].rearrange("p j n f -> p j (n f)")).then_inc(staged.sem, 1)

                @block.tensor
                def _(pe):
                    pe.sem_inc(turned_sum.sem, turned_sum.buffers)
                    pe.sem_inc(logit_sum.sem, logit_sum.buffers)
                    with pe.Fori(0, B) as b:
                        pe.wait_ge(staged.sem, staged.at(b))
                        pe.sem_inc(bearer, 1)
                        pe.wait_ge(copied.sem, copied.at(b - 1))
                        pe.sem_inc(bearer, 1)
                        for h in range(2):
                            for j in range(NT):
                                mm = pe.transpose(turned_ps[:, h, j * P:(j + 1) * P], tile[:, j, h * P:(h + 1) * P], ident)
                        mm.then_inc(turned_sum.sem, 1)
                        pe.wait_ge(copied.sem, copied.at(b))
                        pe.sem_inc(bearer, 1)
                        pe.wait_ge(logit_read.sem, logit_read.at(b - 1))
                        pe.sem_inc(bearer, 1)
                        for j in range(NT):
                            for h in range(2):
                                at = j * 16 + h * 8
                                mm = pe.matmul(logit_ps[:, at:at + 8], turned[:, h, j * P:(j + 1) * P], W("gate_w", h * 8, h * 8 + 8),
                                               start=True, stop=True)
                        mm.then_inc(logit_sum.sem, 1)

                @block.scalar
                def _(act):
                    act.sem_inc(copied.sem, copied.buffers)
                    with act.Fori(0, B) as b:
                        act.wait_ge(turned_sum.sem, turned_sum.at(b))
                        act.sem_inc(bearer, 1)
                        act.wait_ge(logit_sum.sem, logit_sum.at(b - 1))
                        act.sem_inc(bearer, 1)
                        act.activation(turned[:, :, :], turned_ps[:, :, 0:TP], ACT.Copy).then_inc(copied.sem, 1)

                @block.vector
                def _(dve):
                    dve.sem_inc(logit_read.sem, logit_read.buffers)
                    with dve.Fori(0, B) as b:
                        dve.wait_ge(logit_sum.sem, logit_sum.at(b))
                        dve.tensor_tensor(gates1[:, b, :, :], logit_ps[:, 0:NT * 16].rearrange("p (j g) -> p j g", g=16),
                                          R("gate_b").unsqueeze(1).broadcast_to([P, NT, 16]), ALU.add).then_inc(logit_read.sem, 1)

            small_softmax("g1", gates1[:, :, :, :].rearrange("p b j (n e) -> p (b j n) e", e=LE), B * NT * LH, LE)
            with ExitStack() as ctx:
                residual = sb("f1_residual", [P, NT, LH, LD], F32, ctx)
                block = ctx.enter_context(nc.Block())

                @block.vector
                def _(dve):
                    chain = Chain(nc, ctx, dve, "mix_chain")
                    for n in range(LH):
                        dve.tensor_copy(residual[:, :, n, :], inputs_tok[:, n, :, n * LD:(n + 1) * LD])
                    a = answers[:, :, :, :, :].rearrange("p b j n (e d) -> p (b j n e) d", d=LD)
                    g = gates1[:, :, :, :].rearrange("p b j g -> p (b j g)").unsqueeze(2).broadcast_to([P, B * NT * LH * LE, LD])
                    chain.link(dve.tensor_tensor(a, a, g, ALU.mult))
                    chain.link(dve.tensor_reduce(normed[:, :, :, :].rearrange("p b j (n d) -> p (b j n) d", d=LD),
                                                 answers[:, :, :, :, :].rearrange("p b j n (e d) -> p (b j n) d e", d=LD), AX.X, ALU.add))
                    flat = normed[:, :, :, :].rearrange("p b j d -> p b (j d)")
                    r = residual[:, :, :, :].rearrange("p j n d -> p (j n d)").unsqueeze(1).broadcast_to([P, B, NT * D])
                    chain.link(dve.tensor_tensor(flat, flat, r, ALU.add))

            normalise("f1_ln1", normed, mixed, 1e-8, gain="ln_g", shift="ln_b", width=LD)
            with ExitStack() as ctx:
                tile = sb("fc_tile", [P, NT, D], F32, ctx)
                x_t = sb("fc_x", [D + 1, TP], F32, ctx)
                nonzero = sb("fc_nonzero", [D, TP], F32, ctx)
                middle = sb("fc_middle", [D + 1, TP], F32, ctx)
                result = sb("fc_result", [P, NT, D], F32, ctx)
                x_ps = ctx.enter_context(nc.psum_tensor("fc_x_ps", [P, 512], F32))
                m_ps = ctx.enter_context(nc.psum_tensor("fc_m_ps", [P, 512], F32))
                y_ps = ctx.enter_context(nc.psum_tensor("fc_y_ps", [P, 512], F32))
                names = ("staged", "x_sum", "x_ready", "m_sum", "m_ready", "y_sum", "y_read")
                staged, x_sum, x_ready, m_sum, m_ready, y_sum, y_read = (Signal(nc, ctx, f"fc_{n}", 1) for n in names)
                block = ctx.enter_context(nc.Block())

                @block.gpsimd
                def _(pool):
                    pool.sem_inc(staged.sem, staged.buffers)
                    with pool.Fori(0, B) as b:
                        pool.wait_ge(y_read.sem, y_read.at(b - 1))
                        pool.tensor_copy(tile[:, :, :], mixed[:, b, :, :]).then_inc(staged.sem, 1)

                @block.tensor
                def _(pe):
                    for x in (x_sum, m_sum, y_sum):
                        pe.sem_inc(x.sem, x.buffers)
                    with pe.Fori(0, B) as b:
                        pe.wait_ge(staged.sem, staged.at(b))
                        pe.sem_inc(bearer, 1)
                        pe.wait_ge(x_ready.sem, x_ready.at(b - 1))
                        pe.sem_inc(bearer, 1)
                        for j in range(NT):
                            mm = pe.transpose(x_ps[0:D, j * P:(j + 1) * P], tile[:, j, :], ident)
                        mm.then_inc(x_sum.sem, 1)
                        pe.wait_ge(x_ready.sem, x_ready.at(b))
                        pe.sem_inc(bearer, 1)
                        pe.wait_ge(m_ready.sem, m_ready.at(b - 1))
                        pe.sem_inc(bearer, 1)
                        pe.matmul(m_ps[0:D, 0:TP], W("fc1"), x_t[:, :], start=True, stop=True).then_inc(m_sum.sem, 1)
                        pe.wait_ge(m_ready.sem, m_ready.at(b))
                        pe.sem_inc(bearer, 1)
                        pe.wait_ge(y_read.sem, y_read.at(b - 1))
                        pe.sem_inc(bearer, 1)
                        for j in range(NT):
                            mm = pe.matmul(y_ps[:, j * D:(j + 1) * D], middle[:, j * P:(j + 1) * P], W("fc2"), start=True, stop=True)
                        mm.then_inc(y_sum.sem, 1)

                @block.scalar
                def _(act):
                    act.sem_inc(x_ready.sem, x_ready.buffers)
                    with act.Fori(0, B) as b:
                        act.wait_ge(x_sum.sem, x_sum.at(b))
                        act.sem_inc(bearer, 1)
                        act.wait_ge(m_ready.sem, m_ready.at(b - 1))
                        act.sem_inc(bearer, 1)
                        act.activation(x_t[0:D, :], x_ps[0:D, 0:TP], ACT.Copy).then_inc(x_ready.sem, 1)

                @block.vector
                def _(dve):
                    chain = Chain(nc, ctx, dve, "fc_chain")
                    chain.link(dve.memset(x_t[D:D + 1, :], 1.0))
                    chain.link(dve.memset(middle[D:D + 1, :], 1.0))
                    dve.sem_inc(m_ready.sem, m_ready.buffers)
                    dve.sem_inc(y_read.sem, y_read.buffers)
                    first = chain.count
                    with dve.Fori(0, B) as b:
                        chain.loop(b, 3)
                        chain.base = chain.base + first
                        dve.wait_ge(x_ready.sem, x_ready.at(b))
                        chain.link(dve.tensor_scalar(nonzero[:, :], x_t[0:D, :], 0.0, None, ALU.not_equal))
                        dve.wait_ge(m_sum.sem, m_sum.at(b))
                        dve.scalar_tensor_tensor(middle[0:D, :], m_ps[0:D, 0:TP], 0.0, nonzero[:, :], ALU.max, ALU.mult).then_inc(m_ready.sem, 1)
                        dve.wait_ge(staged.sem, staged.at(b))
                        chain.link(dve.tensor_scalar(result[:, :, :], tile[:, :, :], 0.0, None, ALU.not_equal))
                        dve.wait_ge(y_sum.sem, y_sum.at(b))
                        chain.link(dve.tensor_tensor(result[:, :, :], result[:, :, :], y_ps[:, 0:NT * D].rearrange("p (j d) -> p j d", d=D), ALU.mult))
                        dve.tensor_tensor(normed[:, b, :, :], result[:, :, :], tile[:, :, :], ALU.add).then_inc(y_read.sem, 1)
                        chain.close()

            normalise("f1_ln2", normed, mixed, 1e-8, gain="fnorm_g", shift="fnorm_b", width=LD)
            head_gates = sb("f1_head_gates", [P, B * NT, LH], F32, f1)
            with ExitStack() as ctx:
                block = ctx.enter_context(nc.Block())

                @block.vector
                def _(dve):
                    chain = Chain(nc, ctx, dve, "fgate_chain")
                    for n in range(LH):
                        row = R("fgate")[:, n * D:(n + 1) * D].unsqueeze(1).broadcast_to([P, B * NT, D])
                        s = scratch[:, :, :, :].rearrange("p b j d -> p (b j) d")
                        chain.link(dve.tensor_tensor(s, mixed[:, :, :, :].rearrange("p b j d -> p (b j) d"), row, ALU.mult))
                        chain.link(dve.tensor_reduce(head_gates[:, :, n], s, AX.X, ALU.add))

            small_softmax("g2", head_gates[:, :, :], B * NT, LH)
            with ExitStack() as ctx:
                block = ctx.enter_context(nc.Block())

                @block.vector
                def _(dve):
                    chain = Chain(nc, ctx, dve, "f1_chain")
                    m = mixed[:, :, :, :].rearrange("p b j (n d) -> p (b j n) d", d=LD)
                    chain.link(dve.tensor_tensor(m, m, head_gates[:, :, :].rearrange("p g n -> p (g n)").unsqueeze(2)
                                                 .broadcast_to([P, B * NT * LH, LD]), ALU.mult))
                    chain.link(dve.tensor_tensor(state[:, :, :, :], state[:, :, :, :], mixed[:, :, :, :], ALU.add))

        renew_semaphores()

        normalise("a2_ln", state, normed, 1e-5)
        with ExitStack() as ctx:
            x_t = sb("a2_x", [D, TP], F32, ctx)
            q_t = sb("a2_q", [P, 2, TP], F32, ctx)
            k_t = sb("a2_k", [P, AH, TP], F32, ctx)
            values = sb("a2_values", [P, NT, AH, D + 1], F32, ctx)
            sums = sb("a2_sums", [P, NT], F32, ctx)
            weighted = sb("a2_weighted", [P, NT, D], F32, ctx)

            def once(dve):
                dve.memset(k_t[:, :, :], 0.0)
                dve.memset(values[:, :, :, D:D + 1], 1.0)

            def prepare_pe(pe, b, s_ps, t_ps, o_ps, x_ps, flipped_sum, projected, ready_act, ready_dve, finished):
                pe.wait_ge(ready_dve.sem, ready_dve.at(2 * b))
                pe.sem_inc(bearer, 1)
                pe.wait_ge(finished.sem, finished.at(AH * b - 1))
                pe.sem_inc(bearer, 1)
                for h in range(2):
                    pe.matmul(s_ps[:, h, 0:TP], W("a2_q", h * P, (h + 1) * P), x_t[:, :], start=True, stop=True)
                pe.matmul(s_ps[:, 2, 0:TP], W("a2_k", 0, P), x_t[:, :], start=True, stop=True)
                pe.matmul(x_ps[:, 0:TP], W("a2_k", P, 2 * P), x_t[:, :], start=True, stop=True)
                for j in range(NT):
                    mm = pe.matmul((t_ps[:, 0, :], t_ps[:, 1, :], o_ps[:, 0, :])[j], x_t[:, j * P:(j + 1) * P], W("a2_vo"), start=True, stop=True)
                mm.then_inc(projected.sem, 1)
                pe.wait_ge(ready_dve.sem, ready_dve.at(2 * b + 1))
                pe.sem_inc(bearer, 1)
                pe.wait_ge(ready_act.sem, ready_act.at(b))
                pe.sem_inc(bearer, 1)

            def prepare_act(act, b, s_ps, t_ps, o_ps, x_ps, flipped_sum, projected, ready_act, ready_dve, finished):
                act.wait_ge(projected.sem, projected.at(b))
                act.sem_inc(bearer, 1)
                act.activation(q_t[:, :, :], s_ps[:, 0:2, 0:TP], ACT.Copy, scale=float(D) ** -0.5)
                for j in range(2):
                    ins = act.activation(values[:, j, :, 0:D], t_ps[:, j, :].rearrange("p (n d) -> p n d", d=D), ACT.Copy)
                ins.then_inc(ready_act.sem, 1)

            def prepare_dve(dve, b, s_ps, t_ps, o_ps, x_ps, flipped_sum, projected, ready_act, ready_dve, finished):
                dve.wait_ge(flipped_sum.sem, flipped_sum.at(b))
                dve.tensor_copy(x_t[:, :], x_ps[0:D, 0:TP]).then_inc(ready_dve.sem, 1)
                dve.wait_ge(projected.sem, projected.at(b))
                for u in range(AH):
                    rows_u = slice(AR * (u % 4), AR * (u % 4) + AR)
                    dve.tensor_copy(k_t[rows_u, u, :], (s_ps[:, 2, :], x_ps)[u // 4][rows_u, 0:TP])
                dve.tensor_copy(values[:, 2, :, 0:D], o_ps[:, 0, :].rearrange("p (n d) -> p n d", d=D)).then_inc(ready_dve.sem, 1)

            def finish(dve, chain, b, n, products):
                o = products.rearrange("p (j w) -> p j w", w=D + 1)
                chain.link(dve.reciprocal(sums[:, :], o[:, :, D]))
                chain.link(dve.tensor_tensor(weighted[:, :, :], o[:, :, 0:D], sums[:, :].unsqueeze(2).broadcast_to([P, NT, D]), ALU.mult))
                ins = dve.tensor_tensor(state[:, b, :, :], state[:, b, :, :], weighted[:, :, :], ALU.add)
                return ins

            finish.links = 2
            attention("a2", B, AH, False, D + 1, 1,
                      lambda u, qt: q_t[:, u // 4, qt * P:(qt + 1) * P],
                      lambda u, w: k_t[:, u, 0:w],
                      lambda u, kt: values[:, kt, u, :],
                      {"pe": prepare_pe, "act": prepare_act, "dve": prepare_dve, "once": once}, finish, ctx)

        def experts(name, gate, bias, function):
            with ExitStack() as whole_mix:
                logits = sb(f"{name}_logits", [P, B, NT, NE], F32, whole_mix)
                combine = sb(f"{name}_combine", [P, B, NT, NE], F32, whole_mix)
                flip(f"{name}_flip", normed, logits, gate)
                groups = B * NT
                with ExitStack() as ctx:
                    first = sb(f"{name}_first", [P, groups, NE], F32, ctx)
                    work = sb(f"{name}_work", [P, groups, NE], F32, ctx)
                    value = sb(f"{name}_value", [P, 4, groups], F32, ctx)
                    apart = ctx.enter_context(nc.semaphore(f"{name}_apart"))
                    exped = ctx.enter_context(nc.semaphore(f"{name}_exped"))
                    block = ctx.enter_context(nc.Block())
                    g = logits[:, :, :, :].rearrange("p b j e -> p (b j) e")
                    second = combine[:, :, :, :].rearrange("p b j e -> p (b j) e")

                    def wide(t):
                        return t.unsqueeze(2).broadcast_to([P, groups, NE])

                    @block.vector
                    def _(dve):
                        chain = Chain(nc, ctx, dve, f"{name}_route_chain")
                        countdown = R("countdown").unsqueeze(1).broadcast_to([P, groups, NE])

                        def pick(best, mark):
                            chain.link(dve.tensor_reduce(best, g, AX.X, ALU.max))
                            chain.link(dve.tensor_tensor(work[:, :, :], g, wide(best), ALU.is_equal))
                            chain.link(dve.tensor_tensor(work[:, :, :], work[:, :, :], countdown, ALU.mult))
                            chain.link(dve.tensor_reduce(value[:, 2, :], work[:, :, :], AX.X, ALU.max))
                            chain.link(dve.tensor_tensor(mark, work[:, :, :], wide(value[:, 2, :]), ALU.is_equal))

                        if bias is not None:
                            chain.link(dve.tensor_tensor(g, g, R(bias).unsqueeze(1).broadcast_to([P, groups, NE]), ALU.add))
                        pick(value[:, 0, :], first[:, :, :])
                        chain.link(dve.scalar_tensor_tensor(g, first[:, :, :], -BIG, g, ALU.mult, ALU.add))
                        pick(value[:, 1, :], second)
                        dve.tensor_tensor(value[:, 3, :], value[:, 1, :], value[:, 0, :], ALU.subtract).then_inc(apart, 1)
                        dve.wait_ge(exped, 1)
                        chain.link(dve.tensor_scalar(value[:, 0, :], value[:, 3, :], 1.0, None, ALU.add))
                        chain.link(dve.reciprocal(value[:, 0, :], value[:, 0, :]))
                        chain.link(dve.tensor_tensor(value[:, 1, :], value[:, 0, :], value[:, 3, :], ALU.mult))
                        chain.link(dve.tensor_tensor(first[:, :, :], first[:, :, :], wide(value[:, 0, :]), ALU.mult))
                        chain.link(dve.tensor_tensor(second, second, wide(value[:, 1, :]), ALU.mult))
                        chain.link(dve.tensor_tensor(second, second, first[:, :, :], ALU.add))

                    @block.scalar
                    def _(act):
                        act.wait_ge(apart, 1)
                        act.activation(value[:, 3, :], value[:, 3, :], ACT.Exp).then_inc(exped, 1)

                with ExitStack() as ctx:
                    hidden = sb(f"{name}_hidden", [P, 3, TP], F32, ctx)
                    weighted = sb(f"{name}_weighted", [P, 2, NE * D], F32, ctx)
                    total = sb(f"{name}_total", [P, NT, D], F32, ctx)
                    h_ps = ctx.enter_context(nc.psum_tensor(f"{name}_h_ps", [P, 2, 512], F32))
                    y_ps = ctx.enter_context(nc.psum_tensor(f"{name}_y_ps", [P, 2, NT, 512], F32))
                    hidden_sum, hidden_ready, used = Signal(nc, ctx, f"{name}_hidden_sum", 2), Signal(nc, ctx, f"{name}_hidden_ready", 2), Signal(nc, ctx, f"{name}_used", 2)
                    y_sum, y_read = Signal(nc, ctx, f"{name}_y_sum", 2), Signal(nc, ctx, f"{name}_y_read", 2)
                    block = ctx.enter_context(nc.Block())

                    @block.tensor
                    def _(pe):
                        for x in (hidden_sum, used, y_sum):
                            pe.sem_inc(x.sem, x.buffers)
                        with pe.Fori(0, B // 2) as c:
                            def up(s, e):
                                pe.wait_ge(hidden_ready.sem, hidden_ready.at(NE * (2 * c + s) + e - 2))
                                pe.sem_inc(bearer, 1)
                                pe.matmul(h_ps[:, e % 2, 0:TP], W(f"{name}_w1", e * EH, (e + 1) * EH),
                                          pairs(flipped)[0:D + 1, c, s, PADL:PADL + TP], start=True, stop=True).then_inc(hidden_sum.sem, 1)

                            for s in range(2):
                                up(s, 0)
                                pe.wait_ge(y_read.sem, y_read.at(2 * c + s - 2))
                                pe.sem_inc(bearer, 1)
                                for j in range(NT):
                                    pe.matmul(y_ps[:, s, j, 0:NE * D], W("ones_row"), W(f"{name}_b2"), start=True, stop=False)
                                for e in range(NE):
                                    if e + 1 < NE:
                                        up(s, e + 1)
                                    pe.wait_ge(hidden_ready.sem, hidden_ready.at(NE * (2 * c + s) + e))
                                    pe.sem_inc(bearer, 1)
                                    for j in range(NT):
                                        mm = pe.matmul(y_ps[:, s, j, e * D:(e + 1) * D], hidden[:, e % 2, j * P:(j + 1) * P],
                                                       W(f"{name}_w2", e * D, (e + 1) * D), start=False, stop=(e == NE - 1))
                                    mm.then_inc(used.sem, 1)
                                pe.sem_inc(bearer, 1)
                                pe.wait_ge(used.sem, used.at(NE * (2 * c + s) + NE - 1))
                                pe.sem_inc(y_sum.sem, 1)

                    @block.scalar
                    def _(act):
                        act.sem_inc(hidden_ready.sem, hidden_ready.buffers)
                        with act.Fori(0, B) as b:
                            for e in range(NE):
                                act.wait_ge(hidden_sum.sem, hidden_sum.at(NE * b + e))
                                act.sem_inc(bearer, 1)
                                act.wait_ge(used.sem, used.at(NE * b + e - 2))
                                act.sem_inc(bearer, 1)
                                act.activation(hidden[:, e % 2, :], h_ps[:, e % 2, 0:TP], function).then_inc(hidden_ready.sem, 1)

                    @block.vector
                    def _(dve):
                        dve.sem_inc(y_read.sem, y_read.buffers)
                        chain = Chain(nc, ctx, dve, f"{name}_chain")
                        with dve.Fori(0, B // 2) as c:
                            chain.loop(c, 2 * 2 * NT)
                            for s in range(2):
                                dve.wait_ge(y_sum.sem, y_sum.at(2 * c + s))
                                for j in range(NT):
                                    w = weighted[:, j % 2, :].rearrange("p (e d) -> p e d", e=NE)
                                    chain.link(dve.tensor_tensor(w, y_ps[:, s, j, 0:NE * D].rearrange("p (e d) -> p e d", e=NE),
                                                                 pairs(combine)[:, c, s, j, :].unsqueeze(2).broadcast_to([P, NE, D]), ALU.mult))
                                    chain.link(dve.tensor_reduce(total[:, j, :], weighted[:, j % 2, :].rearrange("p (e d) -> p d e", e=NE), AX.X, ALU.add))
                                dve.tensor_tensor(pairs(state)[:, c, s, :, :], pairs(state)[:, c, s, :, :], total[:, :, :], ALU.add)\
                                   .then_inc(y_read.sem, 1)
                            chain.close()

        normalise("m2_ln", state, normed, 1e-5)
        experts("m2", "m2_gate", "m2_bias", ACT.Relu)
        renew_semaphores()

        normalise("a3_ln", state, normed, 1e-5)
        flip("a3_flip", normed)
        with ExitStack() as ctx:
            x_t = sb("a3_x", [D, TP], F32, ctx)
            k_exp = sb("a3_k_exp", [D, TP], F32, ctx)
            v_t = sb("a3_v", [D, TP], F32, ctx)
            q_tok = sb("a3_q_tok", [P, NT, D], F32, ctx)
            k_tok = sb("a3_k_tok", [P, NT, D], F32, ctx)
            mass = sb("a3_mass", [D, 4], F32, ctx)
            pair = sb("a3_pair", [D, D], F32, ctx)
            o_t = sb("a3_o", [D, T], F32, ctx)
            in_line = sb("a3_in_line", [8, 8 * T], F32, ctx)
            k_ps = ctx.enter_context(nc.psum_tensor("a3_k_ps", [P, 512], F32))
            v_ps = ctx.enter_context(nc.psum_tensor("a3_v_ps", [P, 512], F32))
            q_ps = ctx.enter_context(nc.psum_tensor("a3_q_ps", [P, 512], F32))
            kt_ps = ctx.enter_context(nc.psum_tensor("a3_kt_ps", [P, 512], F32))
            pair_ps = ctx.enter_context(nc.psum_tensor("a3_pair_ps", [P, 512], F32))
            o_ps = ctx.enter_context(nc.psum_tensor("a3_o_ps", [P, 512], F32))
            y_ps = ctx.enter_context(nc.psum_tensor("a3_y_ps", [P, 512], F32))
            lined_up = ctx.enter_context(nc.semaphore("a3_lined_up"))
            names = ("staged", "k_sum", "v_sum", "q_sum", "top", "exped", "v_ready", "q_ready", "kt_sum", "kt_ready", "pair_sum", "pair_ready",
                     "o_sum", "o_ready", "y_sum", "y_read")
            (staged, k_sum, v_sum, q_sum, top, exped, v_ready, q_ready, kt_sum, kt_ready, pair_sum, pair_ready,
             o_sum, o_ready, y_sum, y_read) = (Signal(nc, ctx, f"a3_{n}", 1) for n in names)
            block = ctx.enter_context(nc.Block())

            @block.sync
            def _(sp):
                with sp.Fori(0, B) as b:
                    sp.wait_ge(o_ready.sem, o_ready.at(b))
                    sp.sem_inc(bearer, 1)
                    sp.wait_ge(y_sum.sem, y_sum.at(b - 1))
                    sp.sem_inc(bearer, 1)
                    for h in range(8):
                        sp.dma_start(in_line[:, h * T:(h + 1) * T], o_t[8 * h:8 * h + 8, :]).then_inc(lined_up, 16)

            @block.gpsimd
            def _(pool):
                pool.sem_inc(staged.sem, staged.buffers)
                with pool.Fori(0, B) as b:
                    pool.wait_ge(q_sum.sem, q_sum.at(b - 1))
                    pool.tensor_copy(x_t[:, :], flipped[0:D, b, PADL:PADL + TP]).then_inc(staged.sem, 1)

            @block.tensor
            def _(pe):
                for x in (k_sum, v_sum, q_sum, kt_sum, pair_sum, o_sum, y_sum):
                    pe.sem_inc(x.sem, x.buffers)
                with pe.Fori(0, B) as b:
                    pe.wait_ge(staged.sem, staged.at(b))
                    pe.sem_inc(bearer, 1)
                    pe.wait_ge(exped.sem, exped.at(b - 1))
                    pe.sem_inc(bearer, 1)
                    pe.matmul(k_ps[0:D, 0:TP], W("a3_qkv", D, 2 * D), x_t[:, :], start=True, stop=True).then_inc(k_sum.sem, 1)
                    pe.wait_ge(v_ready.sem, v_ready.at(b - 1))
                    pe.sem_inc(bearer, 1)
                    pe.matmul(v_ps[0:D, 0:TP], W("a3_qkv", 2 * D, 3 * D), x_t[:, :], start=True, stop=True).then_inc(v_sum.sem, 1)
                    pe.wait_ge(q_ready.sem, q_ready.at(b - 1))
                    pe.sem_inc(bearer, 1)
                    for j in range(NT):
                        mm = pe.matmul(q_ps[:, j * D:(j + 1) * D], x_t[:, j * P:(j + 1) * P], W("a3_qkv", 0, D), start=True, stop=True)
                    mm.then_inc(q_sum.sem, 1)
                    pe.wait_ge(exped.sem, exped.at(b))
                    pe.sem_inc(bearer, 1)
                    pe.wait_ge(kt_ready.sem, kt_ready.at(b - 1))
                    pe.sem_inc(bearer, 1)
                    for j in range(NT):
                        mm = pe.transpose(kt_ps[:, j * D:(j + 1) * D], k_exp[:, j * P:(j + 1) * P], ident[0:D, 0:D])
                    mm.then_inc(kt_sum.sem, 1)
                    pe.wait_ge(kt_ready.sem, kt_ready.at(b))
                    pe.sem_inc(bearer, 1)
                    pe.wait_ge(q_ready.sem, q_ready.at(b))
                    pe.sem_inc(bearer, 1)
                    pe.wait_ge(pair_ready.sem, pair_ready.at(b - 1))
                    pe.sem_inc(bearer, 1)
                    for j in range(NT):
                        mm = pe.matmul(pair_ps[0:D, 0:D], k_tok[0:TK[j], j, :], q_tok[0:TK[j], j, :], start=(j == 0), stop=(j == NT - 1))
                    mm.then_inc(pair_sum.sem, 1)
                    pe.wait_ge(pair_ready.sem, pair_ready.at(b))
                    pe.sem_inc(bearer, 1)
                    pe.wait_ge(v_ready.sem, v_ready.at(b))
                    pe.sem_inc(bearer, 1)
                    pe.wait_ge(o_ready.sem, o_ready.at(b - 1))
                    pe.sem_inc(bearer, 1)
                    pe.matmul(o_ps[0:D, 0:TP], pair[:, :], v_t[:, :], start=True, stop=True).then_inc(o_sum.sem, 1)
                    pe.wait_ge(y_read.sem, y_read.at(b - 1))
                    pe.sem_inc(bearer, 1)
                    pe.wait_ge(lined_up, b * (8 * 16) + (8 * 16 + 1))
                    pe.sem_inc(bearer, 1)
                    for j in range(NT):
                        y = y_ps[0:TK[j], j * D:(j + 1) * D]
                        pe.matmul(y, W("ones_row", 0, TK[j]), W("a3_bias"), start=True, stop=False)
                        for g in range(8):
                            at = 8 * P * j + g
                            mm = pe.matmul(y, in_line[:, at:at + 8 * (TK[j] - 1) + 1:8], W("a3_out", g * D, (g + 1) * D), start=False, stop=(g == 7))
                    mm.then_inc(y_sum.sem, 1)

            @block.scalar
            def _(act):
                act.sem_inc(exped.sem, exped.buffers)
                act.sem_inc(q_ready.sem, q_ready.buffers)
                act.sem_inc(kt_ready.sem, kt_ready.buffers)
                with act.Fori(0, B) as b:
                    act.wait_ge(top.sem, top.at(b))
                    act.sem_inc(bearer, 1)
                    act.wait_ge(kt_sum.sem, kt_sum.at(b - 1))
                    act.sem_inc(bearer, 1)
                    act.wait_ge(pair_ready.sem, pair_ready.at(b - 1))
                    act.sem_inc(bearer, 1)
                    act.activation(k_exp[:, 0:T], k_ps[0:D, 0:T], ACT.Exp, bias=mass[:, 0:1], accum_out=mass[:, 1:2]).then_inc(exped.sem, 1)
                    act.wait_ge(q_sum.sem, q_sum.at(b))
                    act.sem_inc(bearer, 1)
                    act.wait_ge(pair_sum.sem, pair_sum.at(b - 1))
                    act.sem_inc(bearer, 1)
                    act.activation(q_tok[:, :, :], q_ps[:, 0:NT * D].rearrange("p (j d) -> p j d", d=D), ACT.Copy).then_inc(q_ready.sem, 1)
                    act.wait_ge(kt_sum.sem, kt_sum.at(b))
                    act.sem_inc(bearer, 1)
                    act.activation(k_tok[:, :, :], kt_ps[:, 0:NT * D].rearrange("p (j d) -> p j d", d=D), ACT.Copy).then_inc(kt_ready.sem, 1)

            @block.vector
            def _(dve):
                chain = Chain(nc, ctx, dve, "a3_chain")
                chain.link(dve.memset(k_exp[:, T:TP], 0.0))
                first = chain.count
                for x in (top, v_ready, pair_ready, o_ready, y_read):
                    dve.sem_inc(x.sem, x.buffers)
                dve.sem_inc(lined_up, 1)
                with dve.Fori(0, B) as b:
                    chain.loop(b, 1)
                    chain.base = chain.base + first
                    dve.wait_ge(k_sum.sem, k_sum.at(b))
                    dve.tensor_reduce(mass[:, 0:1], k_ps[0:D, 0:T], AX.X, ALU.max, negate=True).then_inc(top.sem, 1)
                    dve.wait_ge(v_sum.sem, v_sum.at(b))
                    dve.wait_ge(o_sum.sem, o_sum.at(b - 1))
                    dve.tensor_copy(v_t[:, :], v_ps[0:D, 0:TP]).then_inc(v_ready.sem, 1)
                    dve.wait_ge(exped.sem, exped.at(b))
                    chain.link(dve.reciprocal(mass[:, 2:3], mass[:, 1:2]))
                    dve.wait_ge(pair_sum.sem, pair_sum.at(b))
                    dve.scalar_tensor_tensor(pair[:, :], pair_ps[0:D, 0:D], mass[:, 2:3], W("head_mask"), ALU.mult, ALU.mult).then_inc(pair_ready.sem, 1)
                    dve.wait_ge(o_sum.sem, o_sum.at(b))
                    dve.wait_ge(lined_up, b * (8 * 16) + 1)
                    dve.tensor_copy(o_t[:, :], o_ps[0:D, 0:T]).then_inc(o_ready.sem, 1)
                    dve.wait_ge(y_sum.sem, y_sum.at(b))
                    dve.tensor_copy(normed[:, b, 0:2, :], y_ps[:, 0:2 * D].rearrange("p (j d) -> p j d", d=D))
                    dve.tensor_copy(normed[0:LAST, b, 2, :], y_ps[0:LAST, 2 * D:3 * D]).then_inc(y_read.sem, 1)
                    chain.close()

        with ExitStack() as ctx:
            attended = sb("a3_attended", [P, B, NT, D], F32, ctx)
            normalise("a3_out_ln", normed, attended, 1e-5, gain="a3_gamma", shift="a3_beta", add_to=state)

        with ExitStack() as ctx:
            plain = sb("m3_plain", [P, B, NT, D], F32, ctx)
            normalise("m3_ln", state, plain, 1e-5)
            normalise("m3_own_ln", plain, normed, 1e-5, gain="m3_gamma", shift="m3_beta")
        experts("m3", "m3_gate", None, ACT.Gelu)


        store()


def pack(inputs):
    w = [np.zeros((P, n), np.float32) for n in N_COLS]
    r = np.zeros((N_ROWS,), np.float32)
    a = {k: np.ascontiguousarray(v) for k, v in inputs.items()}

    def put(name, m):
        part, rows_, at, cols = COLS[name]
        m = np.ascontiguousarray(m)
        assert m.shape == (rows_, cols), (name, m.shape)
        w[part][0:rows_, at:at + cols] = m

    def row(name, v):
        at, cols = ROWS[name]
        r[at:at + cols] = np.ascontiguousarray(v).reshape(-1)

    def with_bias(m, bias):
        return np.concatenate([m, bias.reshape(1, -1)], 0)

    def halves(m):
        return np.concatenate([m[0:P], m[P:2 * P]], 1)

    idx = np.arange(P)
    put("ident", np.eye(P, dtype=np.float32))
    put("tri_lower", np.concatenate([(np.arange(T)[None, :] < (idx[:, None] + j * P)).astype(np.float32) for j in range(NT)], 1))
    put("causal", np.where(idx[None, :] > idx[:, None], np.float32(-BIG), np.float32(0)))
    head = np.arange(D) // 8
    put("head_mask", np.where(head[:, None] == head[None, :], np.float32(D ** -0.5), np.float32(0)))
    put("ones_row", np.ones((1, P), np.float32))
    put("tok_kernel", a["L0_tok_kernel"].transpose(1, 0, 2).reshape(C_IN, TAPS * D))
    for n in ("bias", "beta"):
        row(f"tok_{n}", a[f"L0_tok_{n}"])
    row("tok_mean", a["L0_tok_moving_mean"])
    row("tok_var", a["L0_tok_moving_var"])
    for n in ("pre_g", "pre_b", "post_g", "post_b", "normf_w"):
        row(n, a[f"L0_attn_{n}"])
    for l in range(LAYERS):
        row(f"norm_w{l}", a["L0_attn_norm_w"][l])
        row(f"conv_w{l}", a["L0_attn_conv_w"][l][:, 0, :].T)
        put(f"in_u{l}", a["L0_attn_inproj_w"][l][0:DI].T)
        put(f"in_g{l}", a["L0_attn_inproj_w"][l][DI:].T)
        put(f"conv_b{l}", halves(a["L0_attn_conv_b"][l][:, None]))
        xp = a["L0_attn_xproj_w"][l].T
        put(f"x_bc{l}", halves(np.concatenate([xp[:, RK:]] * 3, 1)))
        put(f"x_dt{l}", halves(xp[:, 0:RK]))
        put(f"dt_w{l}", a["L0_attn_dtproj_w"][l].T)
        put(f"dt_b{l}", halves(a["L0_attn_dtproj_b"][l][:, None]))
        put(f"a_log{l}", halves(a["L0_attn_A_log"][l]))
        put(f"skip{l}", halves(a["L0_attn_D_param"][l][:, None]))
        put(f"out_w{l}", halves(a["L0_attn_outproj_w"][l].T))
    put("route", np.repeat(with_bias(a["L0_ffn_wr"], a["L0_ffn_br"]), P, 1))
    put("f0_w1", with_bias(a["L0_ffn_w1"], a["L0_ffn_b1"]))
    put("f0_w2", halves(a["L0_ffn_w2"]))
    put("f0_b2", a["L0_ffn_b2"].reshape(1, D))
    for n in "qkv":
        put(f"a1_{n}", with_bias(a[f"L1_attn_W{n}"].T, a[f"L1_attn_b{n}"]))
    put("a1_scale", np.repeat(a["L1_attn_scale"].reshape(1, 1), D, 0))
    hl, hb = a["L1_ffn_hl_w"], a["L1_ffn_hl_b"]
    put("hl_tok", with_bias(hl.reshape(D, D).T, hb.reshape(-1)))
    wide = np.zeros((D + 1, P), np.float32)
    wq, wk, wv = (np.zeros((P, n), np.float32) for n in (LE * P, P, D))
    gw = np.zeros((P, 16), np.float32)
    fc1, fc2 = np.zeros((D + 1, D), np.float32), np.zeros((D + 1, D), np.float32)
    for n in range(LH):
        c, d = slice(32 * n, 32 * n + LD), slice(LD * n, LD * n + LD)
        wide[0:D, c], wide[D, c] = hl[n].T, hb[n]
        for e in range(LE):
            wq[c, e * P + 32 * n:e * P + 32 * n + LD] = a["L1_ffn_wq"][n, e].T
        wk[c, c] = a["L1_ffn_wk"][n].T
        wv[c, d] = a["L1_ffn_wv"][n].T
        gw[(n % 2) * D:(n % 2) * D + D, (n // 2) * 8 + (n % 2) * 4:(n // 2) * 8 + (n % 2) * 4 + 4] = a["L1_ffn_gate_w"][n].T
        for m, k in ((fc1, "fc1"), (fc2, "fc2")):
            m[d, d], m[D, d] = a[f"L1_ffn_{k}_w"].T, a[f"L1_ffn_{k}_b"]
    for name, m in (("hl_wide", wide), ("wq_wide", wq), ("wk_wide", wk), ("wv_wide", wv), ("gate_w", gw), ("fc1", fc1), ("fc2", fc2)):
        put(name, m)
    row("gate_b", a["L1_ffn_gate_b"])
    for n in ("ln_g", "ln_b", "fnorm_g", "fnorm_b"):
        row(n, a[f"L1_ffn_{n}"])
    row("fgate", a["L1_ffn_fgate_w"])
    put("a2_q", a["L2_attn_Q"].reshape(AH * AR, D).T)
    put("a2_k", a["L2_attn_K"].reshape(AH * AR, D).T)
    put("a2_vo", a["L2_attn_VO"].transpose(1, 0, 2).reshape(D, AH * D))
    for m, s, gate, gb in (("m2", "L2_ffn", "Wg", "bg"), ("m3", "L3_ffn", "Wr", "br")):
        put(f"{m}_gate", with_bias(a[f"{s}_{gate}"], a[f"{s}_{gb}"]))
        put(f"{m}_w1", with_bias(a[f"{s}_W1"].transpose(1, 0, 2).reshape(D, NE * EH), a[f"{s}_b1"].reshape(-1)))
        put(f"{m}_w2", a[f"{s}_W2"].transpose(1, 0, 2).reshape(EH, NE * D))
        put(f"{m}_b2", a[f"{s}_b2"].reshape(1, -1))
    row("m2_bias", a["L2_ffn_bias"])
    put("a3_qkv", a["L3_attn_Wqkv"])
    put("a3_out", a["L3_attn_Wout"].reshape(8, 8, D).transpose(1, 0, 2).reshape(8, 8 * D))
    put("a3_bias", a["L3_attn_bout"].reshape(1, D))
    row("a3_gamma", a["L3_attn_gamma"])
    row("a3_beta", a["L3_attn_beta"])
    row("m3_gamma", a["L3_ffn_gamma"])
    row("m3_beta", a["L3_ffn_beta"])
    row("countdown", np.arange(NE, 0, -1, dtype=np.float32))
    sel = (np.arange(96)[:, None, None] % 32 == np.arange(32)[None, :, None]) * np.ones((1, 1, P))
    x = np.pad(a["x"].transpose(2, 0, 1), ((0, 0), (0, 0), (0, TP + TAPS - 1 - T_IN)))
    return {"x": np.ascontiguousarray(x), "w": w[0], "w2": w[1], "r": r, "sel": np.ascontiguousarray(sel.astype(np.float32))}


def kernel(**inputs):
    import concourse.bacc as bacc
    from concourse.bass_utils import run_bass_kernel_spmd

    nc = bacc.Bacc("TRN2", target_bir_lowering=False, num_devices=1)
    arrays = pack(inputs)
    args = [nc.dram_tensor(n, v.shape, mybir.dt.from_np(v.dtype), kind="ExternalInput").ap() for n, v in arrays.items()]
    out = nc.dram_tensor("y", (B, T, D), F32, kind="ExternalOutput").ap()
    tower(nc, *args, out)
    r = run_bass_kernel_spmd(nc, [arrays], core_ids=[0])
    return r.results[0]["y"]
```

```python
from contextlib import ExitStack

import numpy as np
import concourse.bass as bass
from concourse import mybir

ALU = mybir.AluOpType
ACT = mybir.ActivationFunctionType
AX = mybir.AxisListType
F32 = mybir.dt.float32
BF16 = mybir.dt.bfloat16

P = 128
B, T_IN, C_IN = 8, 375, 128
TAPS = 3
T = T_IN - TAPS + 1
D = 64
NT = 3
TP = NT * P
LAST = T - 2 * P
TK = [P, P, LAST]
DI, NS, RK, KC, LAYERS = 256, 16, 16, 4, 2
KEEP = max(1, int(0.5 * T)) - 1
LH, LE, LD = 4, 4, 16
AH, AR = 8, 32
NE, EH = 8, 128
PADL = 4
BIG = 1.0e30
N_SEMAPHORES = 256


class Signal:

    def __init__(self, nc, ctx, name, buffers=2):
        self.sem = ctx.enter_context(nc.semaphore(name))
        self.buffers = buffers

    def at(self, step):
        return step + (self.buffers + 1)


class Chain:

    def __init__(self, nc, ctx, eng, name):
        self.sem = ctx.enter_context(nc.semaphore(name))
        self.eng, self.base, self.count = eng, 0, 0

    def loop(self, step, links):
        self.base, self.count, self.links = step * links, 0, links

    def close(self):
        assert self.count == self.links, self.count

    def link(self, ins):
        self.count += 1
        ins.then_inc(self.sem, 1)
        self.eng.wait_ge(self.sem, self.base + self.count)


def column_table():
    names = [("tok_kernel", C_IN, TAPS * D), ("ident", P, P), ("causal", P, P)]
    names += [("tri_lower", P, NT * T), ("head_mask", P, P), ("ones_row", P, P)]
    for l in range(LAYERS):
        names += [(f"in_u{l}", P, DI), (f"in_g{l}", P, DI), (f"conv_b{l}", P, 2), (f"x_all{l}", P, 2 * P),
                  (f"dt_w{l}", P, DI), (f"dt_b{l}", P, 2), (f"a_log{l}", P, 2 * NS), (f"skip{l}", P, 2), (f"out_w{l}", P, 2 * D)]
    names += [("route", P, P), ("f0_w1", P, 4 * D), ("f0_w2", P, 2 * D), ("f0_b2", P, D)]
    late = len(names)
    names += [("a1_q", P, D), ("a1_k", P, D), ("a1_v", P, D), ("a1_scale", D, 1)]
    names += [("hl_tok", P, D), ("hl_wide", P, P), ("wq_wide", P, LE * P), ("wk_wide", P, P), ("wv_wide", P, D)]
    names += [("gate_w", P, 2 * 8), ("fc1", P, P), ("fc1_b", P, 1), ("fc2", P, P)]
    names += [("a2_q", P, AH * AR), ("a2_k", P, AH * AR), ("a2_vo", P, AH * D)]
    for m in ("m2", "m3"):
        names += [(f"{m}_gate", P, NE), (f"{m}_w1", P, NE * EH), (f"{m}_w2", EH, NE * D)]
    names += [("a3_qkv", P, 3 * P), ("a3_out", P, 8 * P)]
    table, at = {}, [0, 0]
    for i, (name, rows, cols) in enumerate(names):
        part = int(i >= late)
        table[name] = (part, rows, at[part], cols)
        at[part] += cols
    return table, at


def row_table():
    names = [("tok_bias", D), ("tok_beta", D), ("tok_mean", D), ("tok_var", D), ("pre_g", D), ("pre_b", D), ("post_g", D),
             ("post_b", D), ("norm_w0", D), ("norm_w1", D), ("normf_w", D), ("conv_w0", KC * DI), ("conv_w1", KC * DI),
             ("gate_b", LH * LE), ("fc2_b", 2 * D), ("ln_g", LD), ("ln_b", LD), ("fnorm_g", LD), ("fnorm_b", LD), ("fgate", LH * D),
             ("m2_bias", NE), ("m2_b2", NE * D), ("m3_b2", NE * D), ("a3_gamma", D), ("a3_beta", D), ("m3_gamma", D), ("m3_beta", D), ("countdown", NE)]
    table, at = {}, 0
    for name, cols in names:
        table[name] = (at, cols)
        at += cols
    return table, at


COLS, N_COLS = column_table()
ROWS, N_ROWS = row_table()
FIRST_COLS, FIRST_ROWS = COLS["tri_lower"][2], ROWS["pre_g"][0]


def tower(nc, x_in, w_in, w2_in, r_in, sel_in, out):
    with ExitStack() as whole:
        def sb(name, shape, dt=F32, ctx=whole):
            return ctx.enter_context(nc.sbuf_tensor(name, shape, dt))

        bearer = whole.enter_context(nc.semaphore("wait_bearer"))
        late_loaded = whole.enter_context(nc.semaphore("late_loaded"))

        def renew_semaphores():
            with ExitStack() as ctx:
                block = ctx.enter_context(nc.Block())

                @block.sync
                def _(sp):
                    sp.sem_clear(range(late_loaded.num + 1, N_SEMAPHORES))

        weights = [sb("early_weights", [P, N_COLS[0]])]
        rows = sb("rows", [P, N_ROWS])
        state = sb("state", [P, B, NT, D])
        normed = sb("normed", [P, B, NT, D])
        scratch = sb("scratch", [P, B, NT, D])
        stat = sb("stat", [P, 4, B * NT * LH])
        flipped = sb("flipped", [P, B, PADL + TP])
        table_primer = sb("table_primer", [P, 1])
        ident_bf = sb("ident_bf", [P, P], BF16)
        causal_bf = sb("causal_bf", [P, P], BF16)

        def pairs(t):
            rest = " ".join("xyz"[0:len(t.shape) - 2])
            return t[tuple([slice(None)] * len(t.shape))].rearrange(f"p (c s) {rest} -> p c s {rest}", s=2)

        def W(name, lo=0, hi=None, rows_=None):
            part, r, at, cols = COLS[name]
            return weights[part][0:(rows_ or r), at + lo:at + (cols if hi is None else hi)]

        def R(name, parts=P):
            at, cols = ROWS[name]
            return rows[0:parts, at:at + cols]

        ident = W("ident")

        spread_life = whole.enter_context(ExitStack())
        spread = sb("spread", [P, 2 * NS, P], BF16, spread_life)

        with ExitStack() as ctx:
            sel_f32 = sb("sel_f32", [P, 2 * NS, P], F32, ctx)
            rest_loaded = ctx.enter_context(nc.semaphore("rest_loaded"))
            sel_loaded = ctx.enter_context(nc.semaphore("sel_loaded"))
            x_sb = sb("x_sb", [C_IN, B, TP + TAPS - 1], F32, ctx)
            x_sign = sb("x_sign", [C_IN, B, TP + TAPS - 1], BF16, ctx)
            k_sign = sb("k_sign", [C_IN, TAPS * D], BF16, ctx)
            affine = sb("affine", [P, 4, D], F32, ctx)
            conv_ps = ctx.enter_context(nc.psum_tensor("conv_ps", [P, 2, 512], F32))
            loaded = ctx.enter_context(nc.semaphore("tok_loaded"))
            signs = ctx.enter_context(nc.semaphore("tok_signs"))
            root = ctx.enter_context(nc.semaphore("tok_root"))
            var_ready = ctx.enter_context(nc.semaphore("tok_var_ready"))
            conv_done = Signal(nc, ctx, "tok_conv_done")
            placed = Signal(nc, ctx, "tok_placed")
            block = ctx.enter_context(nc.Block())

            @block.sync
            def _(sp):
                sp.dma_start(x_sb[:, :, :], x_in).then_inc(loaded, 16)
                every_row = r_in.rearrange("(a n) -> a n", a=1)
                sp.dma_start(weights[0][:, 0:FIRST_COLS], w_in[:, 0:FIRST_COLS]).then_inc(loaded, 16)
                sp.dma_start(rows[:, 0:FIRST_ROWS], every_row[:, 0:FIRST_ROWS].broadcast_to([P, FIRST_ROWS])).then_inc(loaded, 16)
                sp.dma_start(rows[:, FIRST_ROWS:], every_row[:, FIRST_ROWS:].broadcast_to([P, N_ROWS - FIRST_ROWS])).then_inc(rest_loaded, 16)
                sp.dma_start(sel_f32[:, :, :], sel_in).then_inc(sel_loaded, 16)
                sp.dma_start(weights[0][:, FIRST_COLS:], w_in[:, FIRST_COLS:]).then_inc(rest_loaded, 16)
                sp.wait_ge(rest_loaded, 32)

            @block.scalar
            def _(act):
                act.wait_ge(var_ready, 1)
                act.activation(affine[:, 1, :], affine[:, 0, :], ACT.Sqrt).then_inc(root, 1)
                act.wait_ge(sel_loaded, 16)
                act.activation(spread[:, :, :], sel_f32[:, :, :], ACT.Copy)

            @block.vector
            def _(dve):
                chain = Chain(nc, ctx, dve, "tok_chain")
                dve.sem_inc(placed.sem, placed.buffers)
                dve.wait_ge(loaded, 48)
                dve.tensor_scalar(affine[:, 0, :], R("tok_var"), 1e-3, None, ALU.add).then_inc(var_ready, 1)
                dve.tensor_scalar(k_sign[:, :], W("tok_kernel"), 0.0, 0.5, ALU.is_ge, ALU.subtract).then_inc(signs, 1)
                dve.tensor_scalar(x_sign[:, :, :], x_sb[:, :, :], 0.0, 0.5, ALU.is_ge, ALU.subtract).then_inc(signs, 1)
                dve.tensor_copy(ident_bf[:, :], ident)
                dve.tensor_copy(causal_bf[:, :], W("causal"))
                dve.memset(flipped[:, :, 0:PADL + 1], 0.0)
                chain.link(dve.tensor_tensor(affine[:, 3, :], R("tok_bias"), R("tok_mean"), ALU.subtract))
                dve.wait_ge(root, 1)
                chain.link(dve.reciprocal(affine[:, 2, :], affine[:, 1, :]))
                chain.link(dve.tensor_tensor(affine[:, 3, :], affine[:, 3, :], affine[:, 2, :], ALU.mult))
                chain.link(dve.tensor_tensor(affine[:, 3, :], affine[:, 3, :], R("tok_beta"), ALU.add))
                chain.link(dve.tensor_scalar(affine[:, 2, :], affine[:, 2, :], 4.0, None, ALU.mult))
                scale = affine[:, 2:3, :].broadcast_to([P, NT, D])
                shift = affine[:, 3:4, :].broadcast_to([P, NT, D])
                mul_sem = Chain(nc, ctx, dve, "tok_scaled")
                with dve.Fori(0, B // 2) as c:
                    b = 2 * c
                    mul_sem.loop(c, 2)
                    for s in range(2):
                        dve.wait_ge(conv_done.sem, conv_done.at(b + s))
                        ps = conv_ps[:, s, 0:NT * D].rearrange("p (j d) -> p j d", d=D)
                        mul_sem.link(dve.tensor_tensor(pairs(state)[:, c, s, :, :], ps, scale, ALU.mult))
                        dve.tensor_tensor(pairs(state)[:, c, s, :, :], pairs(state)[:, c, s, :, :], shift, ALU.add).then_inc(placed.sem, 1)
                    mul_sem.close()

            @block.tensor
            def _(pe):
                pe.sem_inc(conv_done.sem, conv_done.buffers)
                pe.wait_ge(signs, 2)
                with pe.Fori(0, B // 2) as c:
                    b = 2 * c
                    for s in range(2):
                        pe.wait_ge(placed.sem, placed.at(b + s - 2))
                        for j in range(NT):
                            for k in range(TAPS):
                                mm = pe.matmul(conv_ps[:, s, j * D:(j + 1) * D], pairs(x_sign)[:, c, s, j * P + k:j * P + k + P],
                                               k_sign[:, k * D:(k + 1) * D], start=(k == 0), stop=(k == TAPS - 1))
                        mm.then_inc(conv_done.sem, 1)

        def normalise(name, src, dst, eps, centre=True, gain=None, shift=None, add_to=None, width=D):
            with ExitStack() as ctx:
                group = B * NT * D // width
                root = ctx.enter_context(nc.semaphore(f"{name}_root"))
                spread = ctx.enter_context(nc.semaphore(f"{name}_spread"))
                block = ctx.enter_context(nc.Block())

                def v(t):
                    return t[:, :, :, :].rearrange("p b j (g w) -> p (b j g) w", w=width)

                def wide(k):
                    return stat[:, k, 0:group].unsqueeze(2).broadcast_to([P, group, width])

                @block.vector
                def _(dve):
                    chain = Chain(nc, ctx, dve, f"{name}_chain")
                    centred = src
                    if centre:
                        chain.link(dve.tensor_reduce(stat[:, 0, 0:group], v(src), AX.X, ALU.add))
                        chain.link(dve.tensor_scalar(stat[:, 0, 0:group], stat[:, 0, 0:group], 1.0 / width, None, ALU.mult))
                        chain.link(dve.tensor_tensor(v(dst), v(src), wide(0), ALU.subtract))
                        centred = dst
                    chain.link(dve.tensor_tensor(v(scratch), v(centred), v(centred), ALU.mult))
                    chain.link(dve.tensor_reduce(stat[:, 1, 0:group], v(scratch), AX.X, ALU.add))
                    dve.tensor_scalar(stat[:, 1, 0:group], stat[:, 1, 0:group], 1.0 / width, eps, ALU.mult, ALU.add).then_inc(spread, 1)
                    dve.wait_ge(root, 1)
                    chain.link(dve.reciprocal(stat[:, 3, 0:group], stat[:, 2, 0:group]))
                    chain.link(dve.tensor_tensor(v(dst), v(centred), wide(3), ALU.mult))
                    for vec, op in ((gain, ALU.mult), (shift, ALU.add)):
                        if vec is not None:
                            chain.link(dve.tensor_tensor(v(dst), v(dst), R(vec).unsqueeze(1).broadcast_to([P, group, width]), op))
                    if add_to is not None:
                        chain.link(dve.tensor_tensor(v(add_to), v(add_to), v(dst), ALU.add))

                @block.scalar
                def _(act):
                    act.activation(table_primer[:, :], ident[:, 0:1], ACT.Sqrt)
                    act.wait_ge(spread, 1)
                    act.activation(stat[:, 2, 0:group], stat[:, 1, 0:group], ACT.Sqrt).then_inc(root, 1)

        def flip(name, src, logits=None, gate=None, doubled=False):
            copies = 2 if doubled else 1
            with ExitStack() as ctx:
                tile = sb(f"{name}_tile", [P, 2, NT, copies, D], F32, ctx)
                turned = sb(f"{name}_turned", [P, 2, TP], F32, ctx)
                ps = ctx.enter_context(nc.psum_tensor(f"{name}_ps", [P, 2, 512], F32))
                lps = ctx.enter_context(nc.psum_tensor(f"{name}_lps", [P, 2, 512], F32))
                staged = Signal(nc, ctx, f"{name}_staged")
                turned_ps = Signal(nc, ctx, f"{name}_turned_ps")
                turned_sb = Signal(nc, ctx, f"{name}_turned_sb")
                kept = Signal(nc, ctx, f"{name}_kept")
                logit_ps = Signal(nc, ctx, f"{name}_logit_ps")
                logit_sb = Signal(nc, ctx, f"{name}_logit_sb")
                ones = ctx.enter_context(nc.semaphore(f"{name}_ones"))
                block = ctx.enter_context(nc.Block())

                @block.gpsimd
                def _(pool):
                    pool.sem_inc(staged.sem, staged.buffers)
                    pool.memset(turned[D:P, :, :], 1.0).then_inc(ones, 1)
                    pool.wait_ge(ones, 1)
                    with pool.Fori(0, B // 2) as c:
                        b = 2 * c
                        for s in range(2):
                            pool.wait_ge(turned_ps.sem, turned_ps.at(b + s - 2))
                            for k in range(copies):
                                ins = pool.tensor_copy(tile[:, s, :, k, :], pairs(src)[:, c, s, :, :])
                            ins.then_inc(staged.sem, 1)

                @block.tensor
                def _(pe):
                    pe.sem_inc(turned_ps.sem, turned_ps.buffers)
                    pe.sem_inc(logit_ps.sem, logit_ps.buffers)
                    pe.wait_ge(ones, 1)
                    with pe.Fori(0, B // 2) as c:
                        b = 2 * c
                        for s in range(2):
                            pe.wait_ge(staged.sem, staged.at(b + s))
                            pe.wait_ge(turned_sb.sem, turned_sb.at(b + s - 2))
                            pe.sem_inc(bearer, 1)
                            for j in range(NT):
                                mm = pe.transpose(ps[0:copies * D, s, j * P:(j + 1) * P], tile[:, s, j, :, :].rearrange("p k d -> p (k d)"), ident)
                            mm.then_inc(turned_ps.sem, 1)
                        for s in range(2):
                            pe.wait_ge(turned_sb.sem, turned_sb.at(b + s))
                            if logits is not None:
                                pe.wait_ge(logit_sb.sem, logit_sb.at(b + s - 2))
                                for j in range(NT):
                                    mm = pe.matmul(lps[:, s, j * NE:(j + 1) * NE], turned[:, s, j * P:(j + 1) * P], W(gate),
                                                   start=True, stop=True)
                                mm.then_inc(logit_ps.sem, 1)

                @block.scalar
                def _(act):
                    act.sem_inc(turned_sb.sem, turned_sb.buffers)
                    with act.Fori(0, B // 2) as c:
                        b = 2 * c
                        for s in range(2):
                            act.wait_ge(turned_ps.sem, turned_ps.at(b + s))
                            act.wait_ge(kept.sem, kept.at(b + s - 2))
                            if logits is not None:
                                act.wait_ge(logit_ps.sem, logit_ps.at(b + s - 2))
                            act.activation(turned[0:copies * D, s, :], ps[0:copies * D, s, 0:TP], ACT.Copy).then_inc(turned_sb.sem, 1)

                @block.vector
                def _(dve):
                    dve.sem_inc(kept.sem, kept.buffers)
                    dve.sem_inc(logit_sb.sem, logit_sb.buffers)
                    with dve.Fori(0, B // 2) as c:
                        b = 2 * c
                        for s in range(2):
                            dve.wait_ge(turned_sb.sem, turned_sb.at(b + s))
                            if doubled:
                                dve.tensor_copy(pairs(flipped)[D:P, c, s, PADL + 1:PADL + TP], turned[D:P, s, 0:TP - 1])
                            dve.tensor_copy(pairs(flipped)[0:D, c, s, PADL:PADL + TP], turned[0:D, s, :]).then_inc(kept.sem, 1)
                        for s in range(2):
                            if logits is not None:
                                dve.wait_ge(logit_ps.sem, logit_ps.at(b + s))
                                dve.tensor_copy(pairs(logits)[:, c, s, :, :], lps[:, s, 0:NT * NE].rearrange("p (j e) -> p j e", e=NE))\
                                   .then_inc(logit_sb.sem, 1)

        def store():
            with ExitStack() as ctx:
                stored = ctx.enter_context(nc.semaphore("stored"))
                block = ctx.enter_context(nc.Block())

                @block.sync
                def _(sp):
                    for j in range(NT):
                        sp.dma_start(out[:, j * P:j * P + TK[j], :].rearrange("b p d -> p b d"), state[0:TK[j], :, j, :]).then_inc(stored, 16)
                    sp.wait_ge(stored, 16 * NT)

        normalise("a0_ln", state, normed, 1e-5)
        with ExitStack() as mamba:
            mix = sb("mix", [P, B, NT, D], F32, mamba)
            conv_in = sb("conv_in", [P, 2, B, T], F32, mamba)
            gates = sb("gates", [P, 2, B, T], F32, mamba)
            steps = sb("steps", [P, 2, B, T], F32, mamba)
            drive = sb("drive", [P, 2, B, T], F32, mamba)
            bc_parts = sb("bc_parts", [P, B, T], BF16, mamba)
            tap_w = sb("tap_w", [P, KC // 2, DI], F32, mamba)
            decay = sb("decay", [P, 2, 2 * NS], F32, mamba)
            skip = sb("skip", [P, 2, P], F32, mamba)
            normalise("a0_pre", normed, mix, 1e-5, gain="pre_g", shift="pre_b")

            def project(l):
                with ExitStack() as ctx:
                    low = sb(f"low{l}", [P, T], F32, ctx)
                    rest = sb(f"rest{l}", [96, T], F32, ctx)
                    middle = sb(f"middle{l}", [96, T], BF16, ctx)
                    u_ps = ctx.enter_context(nc.psum_tensor(f"u_ps{l}", [P, 2, 512], F32))
                    g_ps = ctx.enter_context(nc.psum_tensor(f"g_ps{l}", [P, 2, 512], F32))
                    low_ps = ctx.enter_context(nc.psum_tensor(f"low_ps{l}", [P, 512], F32))
                    dt_ps = ctx.enter_context(nc.psum_tensor(f"dt_ps{l}", [P, 2, 512], F32))
                    exps = ctx.enter_context(nc.semaphore(f"decay_exp{l}"))
                    taps = ctx.enter_context(nc.semaphore(f"tap_weights{l}"))

                    def sig(n):
                        return Signal(nc, ctx, f"{n}{l}", 1)

                    u_sum, g_sum, u_done, g_done = sig("u_sum"), sig("g_sum"), sig("u_done"), sig("g_done")
                    low_sum, low_done, dt_sum, dt_done = sig("low_sum"), sig("low_done"), sig("dt_sum"), sig("dt_done")
                    block = ctx.enter_context(nc.Block())

                    @block.tensor
                    def _(pe):
                        for x in (u_sum, g_sum, low_sum, dt_sum):
                            pe.sem_inc(x.sem, x.buffers)
                        pe.wait_ge(taps, 2)

                        def step_sizes(b):
                            pe.wait_ge(low_done.sem, low_done.at(b))
                            pe.wait_ge(dt_done.sem, dt_done.at(b - 1))
                            for h in range(2):
                                mm = pe.matmul(dt_ps[:, h, 0:T], W(f"dt_w{l}", h * P, (h + 1) * P), low[:, :], start=True, stop=True)
                            mm.then_inc(dt_sum.sem, 1)

                        def projections(b, follows):
                            pe.wait_ge(u_done.sem, u_done.at(b - 1))
                            for h in range(2):
                                for k in range(KC // 2):
                                    at = PADL - (KC - 2) + 2 * k
                                    mm = pe.matmul(u_ps[:, h, 0:T], tap_w[:, k, h * P:(h + 1) * P], flipped[:, b, at:at + T],
                                                   start=(k == 0), stop=(k == KC // 2 - 1))
                            mm.then_inc(u_sum.sem, 1)
                            pe.wait_ge(g_done.sem, g_done.at(b - 1))
                            for h in range(2):
                                mm = pe.matmul(g_ps[:, h, 0:T], W(f"in_g{l}", h * P, (h + 1) * P), flipped[:, b, PADL:PADL + T],
                                               start=True, stop=True)
                            mm.then_inc(g_sum.sem, 1)
                            if follows:
                                step_sizes(b - 1)
                            pe.wait_ge(u_done.sem, u_done.at(b))
                            pe.wait_ge(low_done.sem, low_done.at(b - 1))
                            for h in range(2):
                                mm = pe.matmul(low_ps[:, 0:T], W(f"x_all{l}", h * P, (h + 1) * P), conv_in[:, h, b, :],
                                               start=(h == 0), stop=(h == 1))
                            mm.then_inc(low_sum.sem, 1)

                        projections(0, False)
                        with pe.Fori(1, B) as b:
                            projections(b, True)
                        step_sizes(B - 1)

                    @block.scalar
                    def _(act):
                        for x in (u_done, g_done):
                            act.sem_inc(x.sem, x.buffers)
                        act.activation(decay[:, 0, :], W(f"a_log{l}"), ACT.Exp).then_inc(exps, 1)
                        with act.Fori(0, B) as b:
                            act.wait_ge(u_sum.sem, u_sum.at(b))
                            act.sem_inc(bearer, 1)
                            for h in range(2):
                                ins = act.activation(conv_in[:, h, b, :], u_ps[:, h, 0:T], ACT.Silu, bias=W(f"conv_b{l}", h, h + 1))
                            ins.then_inc(u_done.sem, 1)
                            act.wait_ge(g_sum.sem, g_sum.at(b))
                            act.sem_inc(bearer, 1)
                            for h in range(2):
                                ins = act.activation(gates[:, h, b, :], g_ps[:, h, 0:T], ACT.Silu)
                            ins.then_inc(g_done.sem, 1)

                    @block.vector
                    def _(dve):
                        chain = Chain(nc, ctx, dve, f"project_chain{l}")
                        for x in (low_done, dt_done):
                            dve.sem_inc(x.sem, x.buffers)
                        for half in range(2):
                            ps = slice(half * D, half * D + D)
                            taps_row = R(f"conv_w{l}").rearrange("p (k t d) -> p k t d", k=KC // 2, t=2)[ps, :, 1 - half, :]
                            dve.tensor_tensor(tap_w[ps, :, :], taps_row, W(f"in_u{l}")[ps, :].unsqueeze(1).broadcast_to([D, KC // 2, DI]), ALU.mult)\
                               .then_inc(taps, 1)
                        if l == 0:
                            dve.memset(bc_parts[96:P, :, :], 0.0)
                        for h in range(2):
                            dve.tensor_scalar(skip[:, h, :], ident, W(f"skip{l}", h, h + 1), None, ALU.mult)
                        dve.wait_ge(exps, 1)
                        dve.tensor_scalar(decay[:, 1, :], decay[:, 0, :], -1.0, None, ALU.mult)

                        def step_sizes(b):
                            dve.wait_ge(dt_sum.sem, dt_sum.at(b))
                            for h in range(2):
                                ins = dve.tensor_scalar(steps[:, h, b, :], dt_ps[:, h, 0:T], W(f"dt_b{l}", h, h + 1), None, ALU.add)
                            ins.then_inc(dt_done.sem, 1)

                        def parts(b, follows):
                            chain.loop(b, 3)
                            if follows:
                                step_sizes(b - 1)
                            dve.wait_ge(low_sum.sem, low_sum.at(b))
                            dve.tensor_copy(low[:, :], low_ps[:, 0:T]).then_inc(low_done.sem, 1)
                            dve.wait_ge(low_done.sem, low_done.at(b))
                            chain.link(dve.tensor_copy(bc_parts[0:96, b, :], low[0:96, :]))
                            chain.link(dve.tensor_tensor(rest[:, :], low[0:96, :], bc_parts[0:96, b, :], ALU.subtract))
                            dve.tensor_copy(bc_parts[32:64, b, :], rest[32:64, :])
                            chain.link(dve.tensor_copy(middle[64:96, :], rest[64:96, :]))
                            dve.tensor_tensor(bc_parts[64:96, b, :], rest[64:96, :], middle[64:96, :], ALU.subtract)
                            chain.close()

                        parts(0, False)
                        with dve.Fori(1, B) as b:
                            parts(b, True)
                        step_sizes(B - 1)

            def softplus(l):
                batches = B // 4
                with ExitStack() as ctx:
                    def flat(t):
                        return t[:, :, :, :].rearrange("p b j d -> p (b j d)")[:, 0:2 * batches * T].rearrange("p (k b t) -> p k b t", k=2, b=batches)

                    one_plus, logs = flat(scratch), flat(normed)
                    log_ready = ctx.enter_context(nc.semaphore(f"log_ready{l}"))
                    log_used = ctx.enter_context(nc.semaphore(f"log_used{l}"))
                    abs_ready = ctx.enter_context(nc.semaphore(f"abs_ready{l}"))
                    block = ctx.enter_context(nc.Block())
                    chunks = [(h, slice(batches * k, batches * k + batches)) for h in range(2) for k in range(4)]

                    @block.scalar
                    def _(act):
                        chain = Chain(nc, ctx, act, f"softplus_chain{l}")
                        for i, (h, bs) in enumerate(chunks):
                            act.wait_ge(abs_ready, i + 1)
                            chain.link(act.activation(drive[:, h, bs, :], drive[:, h, bs, :], ACT.Exp, scale=-1.0))
                        for i, (h, bs) in enumerate(chunks):
                            if i > 1:
                                act.wait_ge(log_used, i - 1)
                            chain.link(act.activation(one_plus[:, i % 2, :, :], drive[:, h, bs, :], ACT.Identity, bias=1.0))
                            act.activation(logs[:, i % 2, :, :], one_plus[:, i % 2, :, :], ACT.Ln).then_inc(log_ready, 1)

                    @block.vector
                    def _(dve):
                        chain = Chain(nc, ctx, dve, f"steps_chain{l}")
                        for h, bs in chunks:
                            dve.scalar_tensor_tensor(drive[:, h, bs, :], steps[:, h, bs, :], -1.0, steps[:, h, bs, :], ALU.mult, ALU.max).then_inc(abs_ready, 1)
                        for i, (h, bs) in enumerate(chunks):
                            dve.wait_ge(log_ready, i + 1)
                            chain.link(dve.scalar_tensor_tensor(one_plus[:, i % 2, :, :], one_plus[:, i % 2, :, :], 1.0, drive[:, h, bs, :], ALU.subtract, ALU.subtract))
                            chain.link(dve.scalar_tensor_tensor(steps[:, h, bs, :], steps[:, h, bs, :], 0.0, logs[:, i % 2, :, :], ALU.max, ALU.add))
                            dve.tensor_tensor(steps[:, h, bs, :], steps[:, h, bs, :], one_plus[:, i % 2, :, :], ALU.subtract).then_inc(log_used, 1)

                    @block.gpsimd
                    def _(pool):
                        for i, (h, bs) in enumerate(chunks):
                            pool.wait_ge(log_used, i + 1)
                            pool.tensor_tensor(drive[:, h, bs, :], steps[:, h, bs, :], conv_in[:, h, bs, :], ALU.mult)

            def scan(l):
                units = 2 * NS
                with ExitStack() as ctx:
                    c_all = sb(f"c_all{l}", [P, 4, T], F32, ctx)
                    keep = sb(f"keep{l}", [P, 4, T], F32, ctx)
                    add = scratch[:, :, :, :].rearrange("p b j d -> p (b j d)")[:, 0:4 * T].rearrange("p (s t) -> p s t", s=4)
                    seen = normed[:, :, :, :].rearrange("p b j d -> p (b j d)")[:, 0:4 * T].rearrange("p (s t) -> p s t", s=4)
                    hidden = sb(f"hidden{l}", [P, 4, T], F32, ctx)
                    gated = sb(f"gated{l}", [P, 2, TP], F32, ctx)
                    b_ps = ctx.enter_context(nc.psum_tensor(f"b_ps{l}", [P, 2, 512], F32))
                    c_ps = ctx.enter_context(nc.psum_tensor(f"c_ps{l}", [P, 2, 512], F32))
                    y_ps = ctx.enter_context(nc.psum_tensor(f"y_ps{l}", [P, 2, 512], F32))
                    o_ps = ctx.enter_context(nc.psum_tensor(f"o_ps{l}", [P, 512], F32))

                    def sig(n, buffers):
                        return Signal(nc, ctx, f"{n}{l}", buffers)

                    b_spread, c_spread, c_copied = sig("b_spread", 2), sig("c_spread", 2), sig("c_copied", 2)
                    keep_ready, add_ready, hidden_ready = sig("keep_ready", 4), sig("add_ready", 4), sig("hidden_ready", 4)
                    seen_ready, seen_summed = sig("seen_ready", 8), sig("seen_summed", 4)
                    gated_ready, o_ready, mixed = sig("gated_ready", 1), sig("o_ready", 1), sig("mixed", 1)
                    block = ctx.enter_context(nc.Block())

                    @block.tensor
                    def _(pe):
                        for x in (b_spread, c_spread, seen_summed, o_ready):
                            pe.sem_inc(x.sem, x.buffers)

                        def spread_out(b, n):
                            pe.wait_ge(add_ready.sem, add_ready.at(units * b + 2 * (n - 2) + 1))
                            pe.matmul(b_ps[:, n % 2, 0:T], spread[:, n, :], bc_parts[:, b, :], start=True, stop=True).then_inc(b_spread.sem, 1)
                            pe.wait_ge(c_copied.sem, c_copied.at(NS * b + n - 2))
                            pe.matmul(c_ps[:, n % 2, 0:T], spread[:, NS + n, :], bc_parts[:, b, :], start=True, stop=True).then_inc(c_spread.sem, 1)

                        def output(b):
                            pe.wait_ge(gated_ready.sem, gated_ready.at(b))
                            pe.wait_ge(mixed.sem, mixed.at(b - 1))
                            for j in range(NT):
                                for h in range(2):
                                    mm = pe.matmul(o_ps[:, j * D:(j + 1) * D], gated[:, h, j * P:(j + 1) * P], W(f"out_w{l}", h * D, (h + 1) * D),
                                                   start=(h == 0), stop=(h == 1))
                            mm.then_inc(o_ready.sem, 1)

                        def sums(b, follows):
                            spread_out(b, 0)
                            spread_out(b, 1)
                            pe.wait_ge(gated_ready.sem, gated_ready.at(b - 1))
                            for h in range(2):
                                pe.matmul(y_ps[:, h, 0:T], skip[:, h, :], conv_in[:, h, b, :], start=True, stop=False)
                            spread_out(b, 2)
                            for n in range(NS):
                                for h in range(2):
                                    pe.wait_ge(seen_ready.sem, seen_ready.at(units * b + 2 * n + h))
                                    pe.matmul(y_ps[:, h, 0:T], ident, seen[:, (2 * n + h) % 4, :], start=False, stop=(n == NS - 1))\
                                      .then_inc(seen_summed.sem, 1)
                                    if h == 0 and n + 3 < NS:
                                        spread_out(b, n + 3)
                                if follows and n == 0:
                                    output(b - 1)

                        sums(0, False)
                        with pe.Fori(1, B) as b:
                            sums(b, True)
                        output(B - 1)

                    @block.scalar
                    def _(act):
                        for x in (c_copied, keep_ready):
                            act.sem_inc(x.sem, x.buffers)
                        with act.Fori(0, B) as b:
                            for n in range(NS):
                                act.wait_ge(c_spread.sem, c_spread.at(NS * b + n))
                                act.wait_ge(seen_ready.sem, seen_ready.at(units * b + 2 * (n - 4) + 1))
                                act.activation(c_all[:, n % 4, :], c_ps[:, n % 2, 0:T], ACT.Copy).then_inc(c_copied.sem, 1)
                                for h in range(2):
                                    u = 2 * n + h
                                    act.wait_ge(hidden_ready.sem, hidden_ready.at(units * b + u - 4))
                                    act.sem_inc(bearer, 1)
                                    act.activation(keep[:, u % 4, :], steps[:, h, b, :], ACT.Exp, scale=decay[:, 1, h * NS + n:h * NS + n + 1])\
                                       .then_inc(keep_ready.sem, 1)

                    @block.vector
                    def _(dve):
                        for x in (add_ready, hidden_ready, gated_ready, mixed):
                            dve.sem_inc(x.sem, x.buffers)
                        dve.memset(gated[:, :, T:TP], 0.0)

                        def inputs(b, u):
                            n, h = u // 2, u % 2
                            dve.wait_ge(b_spread.sem, b_spread.at(NS * b + n))
                            dve.tensor_tensor(add[:, u % 4, :], drive[:, h, b, :], b_ps[:, n % 2, 0:T], ALU.mult).then_inc(add_ready.sem, 1)

                        def gate(b):
                            dve.wait_ge(seen_summed.sem, seen_summed.at(units * b + units - 1))
                            dve.wait_ge(o_ready.sem, o_ready.at(b - 1))
                            for h in range(2):
                                ins = dve.tensor_tensor(gated[:, h, 0:T], gates[:, h, b, :], y_ps[:, h, 0:T], ALU.mult)
                            ins.then_inc(gated_ready.sem, 1)

                        def add_output(b):
                            dve.wait_ge(o_ready.sem, o_ready.at(b))
                            dve.tensor_tensor(mix[:, b, :, :], mix[:, b, :, :], o_ps[:, 0:NT * D].rearrange("p (j d) -> p j d", d=D), ALU.add)\
                               .then_inc(mixed.sem, 1)

                        def recur(b, follows):
                            inputs(b, 0)
                            for u in range(units):
                                if u + 1 < units:
                                    inputs(b, u + 1)
                                dve.wait_ge(keep_ready.sem, keep_ready.at(units * b + u))
                                dve.wait_ge(add_ready.sem, add_ready.at(units * b + u))
                                dve.wait_ge(seen_ready.sem, seen_ready.at(units * b + u - 4))
                                dve.tensor_tensor_scan(hidden[:, u % 4, :], keep[:, u % 4, :], add[:, u % 4, :], 0.0, ALU.mult, ALU.add)\
                                   .then_inc(hidden_ready.sem, 1)
                                if follows and u == 1:
                                    gate(b - 1)
                                if follows and u == 6:
                                    add_output(b - 1)

                        recur(0, False)
                        with dve.Fori(1, B) as b:
                            recur(b, True)
                        gate(B - 1)
                        add_output(B - 1)

                    @block.gpsimd
                    def _(pool):
                        pool.sem_inc(seen_ready.sem, seen_ready.buffers)
                        with pool.Fori(0, B) as b:
                            for u in range(units):
                                pool.wait_ge(hidden_ready.sem, hidden_ready.at(units * b + u))
                                if u % 2 == 0:
                                    pool.wait_ge(c_copied.sem, c_copied.at(NS * b + u // 2))
                                pool.wait_ge(seen_summed.sem, seen_summed.at(units * b + u - 4))
                                pool.tensor_tensor(seen[:, u % 4, :], hidden[:, u % 4, :], c_all[:, (u // 2) % 4, :], ALU.mult)\
                                    .then_inc(seen_ready.sem, 1)

            for l in range(LAYERS):
                normalise(f"rms{l}", mix, normed, 1e-5, centre=False, gain=f"norm_w{l}")
                flip(f"a0_flip{l}", normed, doubled=True)
                project(l)
                softplus(l)
                scan(l)
            normalise("a0_normf", mix, normed, 1e-5, centre=False, gain="normf_w")
            normalise("a0_post", normed, mix, 1e-5, gain="post_g", shift="post_b", add_to=state)

        renew_semaphores()
        spread_life.close()
        weights.append(sb("late_weights", [P, N_COLS[1]]))
        with ExitStack() as ctx:
            block = ctx.enter_context(nc.Block())

            @block.sync
            def _(sp):
                sp.dma_start(weights[1][:, :], w2_in).then_inc(late_loaded, 16)

            @block.vector
            def _(dve):
                dve.memset(flipped[D:P, :, :], 1.0)

        normalise("f0_ln", state, normed, 1e-5)
        flip("f0_flip", normed)
        with ExitStack() as ctx:
            score = sb("score", [P, 2, TP], F32, ctx)
            compared = sb("compared", [P, T], F32, ctx)
            count = sb("count", [P, 2, 3, NT], F32, ctx)
            factor = sb("factor", [P, 2, NT], F32, ctx)
            ffn_hidden = sb("ffn_hidden", [P, 2, 2, TP], F32, ctx)
            routed = sb("routed", [P, 2, NT, D], F32, ctx)
            score_ps = ctx.enter_context(nc.psum_tensor("score_ps", [P, 2, 512], F32))
            hidden_ps = ctx.enter_context(nc.psum_tensor("hidden_ps", [P, 2, 2, 512], F32))
            out_ps = ctx.enter_context(nc.psum_tensor("out_ps", [P, 2, 512], F32))
            score_sum, score_read = Signal(nc, ctx, "score_sum"), Signal(nc, ctx, "score_read")
            hidden_sum, hidden_done = Signal(nc, ctx, "hidden_sum"), Signal(nc, ctx, "hidden_done")
            out_sum, out_read = Signal(nc, ctx, "out_sum"), Signal(nc, ctx, "out_read")
            ranked = Signal(nc, ctx, "ranked")
            block = ctx.enter_context(nc.Block())

            @block.tensor
            def _(pe):
                for x in (score_sum, hidden_sum, out_sum):
                    pe.sem_inc(x.sem, x.buffers)
                with pe.Fori(0, B // 2) as c:
                    b = 2 * c
                    for s in range(2):
                        x = pairs(flipped)[:, c, s, PADL:PADL + TP]
                        pe.wait_ge(score_read.sem, score_read.at(b + s - 2))
                        pe.matmul(score_ps[:, s, 0:TP], W("route"), x, start=True, stop=True).then_inc(score_sum.sem, 1)
                        pe.wait_ge(hidden_done.sem, hidden_done.at(b + s - 2))
                        for h in range(2):
                            mm = pe.matmul(hidden_ps[:, s, h, 0:TP], W("f0_w1", h * P, (h + 1) * P), x, start=True, stop=True)
                        mm.then_inc(hidden_sum.sem, 1)
                    for s in range(2):
                        pe.wait_ge(hidden_done.sem, hidden_done.at(b + s))
                        pe.wait_ge(out_read.sem, out_read.at(b + s - 2))
                        for j in range(NT):
                            o = out_ps[:, s, j * D:(j + 1) * D]
                            pe.matmul(o, W("ones_row"), W("f0_b2"), start=True, stop=False)
                            for h in range(2):
                                mm = pe.matmul(o, ffn_hidden[:, s, h, j * P:(j + 1) * P], W("f0_w2", h * D, (h + 1) * D), start=False, stop=(h == 1))
                        mm.then_inc(out_sum.sem, 1)

            @block.scalar
            def _(act):
                act.sem_inc(score_read.sem, score_read.buffers)
                act.sem_inc(hidden_done.sem, hidden_done.buffers)
                with act.Fori(0, B // 2) as c:
                    b = 2 * c
                    for s in range(2):
                        act.wait_ge(score_sum.sem, score_sum.at(b + s))
                        act.wait_ge(ranked.sem, ranked.at(b + s - 2))
                        act.activation(score[:, s, :], score_ps[:, s, 0:TP], ACT.Copy).then_inc(score_read.sem, 1)
                        act.wait_ge(hidden_sum.sem, hidden_sum.at(b + s))
                        act.wait_ge(out_sum.sem, out_sum.at(b + s - 2))
                        act.activation(ffn_hidden[:, s, :, :], hidden_ps[:, s, :, 0:TP], ACT.Gelu_apprx_tanh).then_inc(hidden_done.sem, 1)

            @block.vector
            def _(dve):
                chain = Chain(nc, ctx, dve, "route_chain")
                dve.sem_inc(ranked.sem, ranked.buffers)
                dve.sem_inc(out_read.sem, out_read.buffers)
                with dve.Fori(0, B // 2) as c:
                    b = 2 * c
                    chain.loop(c, 2 * (3 * NT + 2 + NT))
                    for s in range(2):
                        dve.wait_ge(score_read.sem, score_read.at(b + s))
                        for j in range(NT):
                            own = count[:, s, 2, j:j + 1]
                            chain.link(dve.scalar_tensor_tensor(compared[:, 0:P], score[:, s, j * P:(j + 1) * P], 1.0, ident, ALU.mult, ALU.mult,
                                                                accum_out=own))
                            chain.link(dve.tensor_scalar(compared[:, :], score[:, s, 0:T], own, None, ALU.is_gt, ALU.add,
                                                         accum_out=count[:, s, 0, j:j + 1]))
                            chain.link(dve.scalar_tensor_tensor(compared[:, :], score[:, s, 0:T], own, W("tri_lower", j * T, (j + 1) * T),
                                                                ALU.is_equal, ALU.mult, accum_out=count[:, s, 1, j:j + 1]))
                        chain.link(dve.tensor_tensor(count[:, s, 0, :], count[:, s, 0, :], count[:, s, 1, :], ALU.add))
                        chain.link(dve.scalar_tensor_tensor(factor[:, s, :], count[:, s, 0, :], KEEP - 0.5, count[:, s, 2, :], ALU.is_lt, ALU.mult))
                        dve.sem_inc(ranked.sem, 1)
                    for s in range(2):
                        dve.wait_ge(out_sum.sem, out_sum.at(b + s))
                        for j in range(NT):
                            chain.link(dve.scalar_tensor_tensor(routed[:, s, j, :], out_ps[:, s, j * D:(j + 1) * D], factor[:, s, j:j + 1],
                                                                pairs(normed)[:, c, s, j, :], ALU.mult, ALU.add))
                        dve.tensor_tensor(pairs(state)[:, c, s, :, :], pairs(state)[:, c, s, :, :], routed[:, s, :, :], ALU.add)\
                           .then_inc(out_read.sem, 1)
                    chain.close()

        def attention(name, iterations, units, causal, width, group, q_of, k_of, v_of, prepare, finish, ctx):
            steps, batches = units * NT, B // iterations
            tile = sb(f"{name}_tile", [P, batches, NT, D], F32, ctx)
            probs = sb(f"{name}_probs", [P, 3, TP], F32, ctx)
            turned = sb(f"{name}_turned", [P, 2, TP], F32, ctx)
            neg_max = sb(f"{name}_neg_max", [P, 3], F32, ctx)
            s_ps = ctx.enter_context(nc.psum_tensor(f"{name}_s_ps", [P, NT, 512], F32))
            t_ps = ctx.enter_context(nc.psum_tensor(f"{name}_t_ps", [P, 2, 512], F32))
            o_ps = ctx.enter_context(nc.psum_tensor(f"{name}_o_ps", [P, 2, 512], F32))
            x_ps = ctx.enter_context(nc.psum_tensor(f"{name}_x_ps", [P, 512], F32))

            def sig(n, buffers):
                return Signal(nc, ctx, f"{name}_{n}", buffers)

            staged, flipped_sum, projected = sig("staged", 1), sig("flipped_sum", 1), sig("projected", 2)
            ready_act, ready_dve = sig("ready_act", 1), sig("ready_dve", 1)
            scores_sum, max_ready, probs_ready = sig("scores_sum", 3), sig("max_ready", 3), sig("probs_ready", 3)
            turned_sum, turned_dve, turned_act = sig("turned_sum", 3), sig("turned_dve", 1), sig("turned_act", 1)
            product_sum, finished = sig("product_sum", 3), sig("finished", 2)
            block = ctx.enter_context(nc.Block())
            used = (s_ps, t_ps, o_ps, x_ps, flipped_sum, projected, ready_act, ready_dve, finished)

            def keys(qt):
                return range(qt + 1) if causal else range(NT)

            def score_width(qt):
                return min((qt + 1) * P, T) if causal else T

            @block.gpsimd
            def _(pool):
                pool.sem_inc(staged.sem, staged.buffers)
                with pool.Fori(0, iterations) as c:
                    pool.wait_ge(flipped_sum.sem, flipped_sum.at(c - 1))
                    for s in range(batches):
                        source = pairs(normed)[:, c, s, :, :] if batches == 2 else normed[:, c, :, :]
                        ins = pool.tensor_copy(tile[:, s, :, :], source)
                    ins.then_inc(staged.sem, 1)

            @block.tensor
            def _(pe):
                for x in (flipped_sum, projected, scores_sum, turned_sum, product_sum):
                    pe.sem_inc(x.sem, x.buffers)

                def scores(c, i):
                    u, qt = i // NT, i % NT
                    w = score_width(qt)
                    pe.wait_ge(probs_ready.sem, probs_ready.at(steps * c + i - 3))
                    mm = pe.matmul(s_ps[:, i % 3, 0:w], q_of(u, qt), k_of(u, w), start=True, stop=not causal)
                    if causal:
                        lo, n = qt * P, TK[qt]
                        mm = pe.matmul(s_ps[:, i % 3, lo:lo + n], ident_bf[:, :], causal_bf[:, 0:n], start=False, stop=True)
                    mm.then_inc(scores_sum.sem, 1)

                def turn(c, i):
                    pe.wait_ge(probs_ready.sem, probs_ready.at(steps * c + i))
                    copied = (turned_dve, turned_act)[i % 2]
                    pe.wait_ge(copied.sem, copied.at(steps // 2 * c + i // 2 - 1))
                    for kt in keys(i % NT):
                        mm = pe.transpose(t_ps[:, i % 2, kt * P:(kt + 1) * P], probs[:, i % 3, kt * P:(kt + 1) * P], ident)
                    mm.then_inc(turned_sum.sem, 1)

                def products(c, i):
                    u, qt = i // NT, i % NT
                    copied = (turned_dve, turned_act)[i % 2]
                    if u % group == 0 and qt == 0:
                        pe.wait_ge(finished.sem, finished.at(units // group * c + u // group - 2))
                    pe.wait_ge(copied.sem, copied.at(steps // 2 * c + i // 2))
                    o = ((u % group) * NT + qt) * width
                    for kt in keys(qt):
                        mm = pe.matmul(o_ps[:, (u // group) % 2, o:o + width], turned[:, i % 2, kt * P:(kt + 1) * P], v_of(u, kt),
                                       start=(kt == 0), stop=(kt == keys(qt)[-1]))
                    mm.then_inc(product_sum.sem, 1)

                with pe.Fori(0, iterations) as c:
                    pe.wait_ge(staged.sem, staged.at(c))
                    pe.sem_inc(bearer, 1)
                    for s in range(batches):
                        for j in range(NT):
                            to = (x_ps, t_ps[:, 0, :])[s]
                            mm = pe.transpose(to[0:D, j * P:(j + 1) * P], tile[:, s, j, :], ident)
                    mm.then_inc(flipped_sum.sem, 1)
                    prepare["pe"](pe, c, *used)
                    scores(c, 0)
                    scores(c, 1)
                    for i in range(steps):
                        if i + 2 < steps:
                            scores(c, i + 2)
                        turn(c, i)
                        if i > 0:
                            products(c, i - 1)
                    products(c, steps - 1)

            @block.scalar
            def _(act):
                for x in (ready_act, probs_ready, turned_act):
                    act.sem_inc(x.sem, x.buffers)

                def exp(c, i):
                    w = score_width(i % NT)
                    act.wait_ge(turned_sum.sem, turned_sum.at(steps * c + i - 3))
                    act.wait_ge(max_ready.sem, max_ready.at(steps * c + i))
                    act.activation(probs[:, i % 3, 0:w], s_ps[:, i % 3, 0:w], ACT.Exp, bias=neg_max[:, i % 3:i % 3 + 1])\
                       .then_inc(probs_ready.sem, 1)

                with act.Fori(0, iterations) as c:
                    act.wait_ge(product_sum.sem, product_sum.at(steps * c - 1))
                    prepare["act"](act, c, *used)
                    exp(c, 0)
                    for i in range(steps):
                        if i + 1 < steps:
                            exp(c, i + 1)
                        if i % 2 == 1:
                            n = P * len(keys(i % NT))
                            act.wait_ge(product_sum.sem, product_sum.at(steps * c + i - 2))
                            act.wait_ge(turned_sum.sem, turned_sum.at(steps * c + i))
                            act.activation(turned[:, 1, 0:n], t_ps[:, 1, 0:n], ACT.Copy).then_inc(turned_act.sem, 1)

            @block.vector
            def _(dve):
                chain = Chain(nc, ctx, dve, f"{name}_chain")
                prepare["once"](dve)
                chain.link(dve.memset(probs[:, :, :], 0.0))
                first = chain.count
                for x in (ready_dve, max_ready, turned_dve, finished):
                    dve.sem_inc(x.sem, x.buffers)

                def maximum(c, i):
                    dve.wait_ge(scores_sum.sem, scores_sum.at(steps * c + i))
                    dve.tensor_reduce(neg_max[:, i % 3:i % 3 + 1], s_ps[:, i % 3, 0:score_width(i % NT)], AX.X, ALU.max, negate=True)\
                       .then_inc(max_ready.sem, 1)

                def finish_group(c, i):
                    u = i // NT
                    if i % NT == NT - 1 and u % group == group - 1:
                        dve.wait_ge(product_sum.sem, product_sum.at(steps * c + i))
                        finish(dve, chain, c, u // group, o_ps[:, (u // group) % 2, 0:group * NT * width]).then_inc(finished.sem, 1)

                with dve.Fori(0, iterations) as c:
                    chain.loop(c, finish.links * (units // group))
                    chain.base = chain.base + first
                    prepare["dve"](dve, c, *used)
                    maximum(c, 0)
                    maximum(c, 1)
                    for i in range(steps):
                        if i + 2 < steps:
                            maximum(c, i + 2)
                        if i % 2 == 0:
                            n = P * len(keys(i % NT))
                            dve.wait_ge(product_sum.sem, product_sum.at(steps * c + i - 2))
                            dve.wait_ge(turned_sum.sem, turned_sum.at(steps * c + i))
                            dve.tensor_copy(turned[:, 0, 0:n], t_ps[:, 0, 0:n]).then_inc(turned_dve.sem, 1)
                        if i > 1:
                            finish_group(c, i - 2)
                    for i in range(steps - 2, steps):
                        finish_group(c, i)
                    chain.close()

        normalise("a1_ln", state, normed, 1e-5)
        with ExitStack() as ctx:
            x_t = sb("a1_x", [P, 2, TP], F32, ctx)
            q_t = sb("a1_q", [P, 2, TP], F32, ctx)
            k_t = sb("a1_k", [P, 2, TP], F32, ctx)
            values = sb("a1_values", [P, 2, NT, D + 1], F32, ctx)
            inverse = sb("a1_inverse", [D, 1], F32, ctx)
            sums = sb("a1_sums", [P, NT], F32, ctx)
            weighted = sb("a1_weighted", [P, NT, D], F32, ctx)

            def once(dve):
                dve.wait_ge(late_loaded, 16)
                dve.memset(x_t[D:P, :, :], 1.0)
                dve.memset(q_t[D:P, :, :], 0.0)
                dve.memset(k_t[D:P, :, :], 0.0)
                dve.memset(values[:, :, :, D:D + 1], 1.0)
                dve.reciprocal(inverse[:, :], W("a1_scale"))

            def prepare_pe(pe, c, s_ps, t_ps, o_ps, x_ps, flipped_sum, projected, ready_act, ready_dve, finished):
                pe.wait_ge(finished.sem, finished.at(2 * c - 1))
                pe.wait_ge(ready_dve.sem, ready_dve.at(2 * c))
                q_banks, k_banks, v_banks = (s_ps[:, 0, :], s_ps[:, 1, :]), (s_ps[:, 2, :], x_ps), (o_ps[:, 0, :], o_ps[:, 1, :])
                for s in range(2):
                    pe.matmul(q_banks[s][0:D, 0:TP], W("a1_q"), x_t[:, s, :], start=True, stop=True)
                    pe.matmul(k_banks[s][0:D, 0:TP], W("a1_k"), x_t[:, s, :], start=True, stop=True)
                    for j in range(NT):
                        mm = pe.matmul(v_banks[s][:, j * D:(j + 1) * D], x_t[:, s, j * P:(j + 1) * P], W("a1_v"), start=True, stop=True)
                mm.then_inc(projected.sem, 1)
                pe.wait_ge(ready_dve.sem, ready_dve.at(2 * c + 1))
                pe.wait_ge(ready_act.sem, ready_act.at(c))

            def prepare_act(act, c, s_ps, t_ps, o_ps, x_ps, flipped_sum, projected, ready_act, ready_dve, finished):
                act.wait_ge(projected.sem, projected.at(c))
                act.activation(values[:, 0, :, 0:D], o_ps[:, 0, 0:NT * D].rearrange("p (j d) -> p j d", d=D), ACT.Copy)
                act.activation(values[:, 1, :, 0:D], o_ps[:, 1, 0:NT * D].rearrange("p (j d) -> p j d", d=D), ACT.Copy)
                act.activation(k_t[0:D, 1, :], x_ps[0:D, 0:TP], ACT.Copy).then_inc(ready_act.sem, 1)

            def prepare_dve(dve, c, s_ps, t_ps, o_ps, x_ps, flipped_sum, projected, ready_act, ready_dve, finished):
                dve.wait_ge(flipped_sum.sem, flipped_sum.at(c))
                dve.tensor_copy(x_t[0:D, 0, :], x_ps[0:D, 0:TP])
                dve.tensor_copy(x_t[0:D, 1, :], t_ps[0:D, 0, 0:TP]).then_inc(ready_dve.sem, 1)
                dve.wait_ge(projected.sem, projected.at(c))
                dve.tensor_scalar(q_t[0:D, :, :], s_ps[0:D, 0:2, 0:TP], inverse[:, :], None, ALU.mult)
                dve.tensor_copy(k_t[0:D, 0, :], s_ps[0:D, 2, 0:TP]).then_inc(ready_dve.sem, 1)

            def finish(dve, chain, c, n, products):
                o = products.rearrange("p (j w) -> p j w", w=D + 1)
                chain.link(dve.reciprocal(sums[:, :], o[:, :, D]))
                chain.link(dve.tensor_tensor(weighted[:, :, :], o[:, :, 0:D], sums[:, :].unsqueeze(2).broadcast_to([P, NT, D]), ALU.mult))
                return dve.tensor_tensor(pairs(state)[:, c, n, :, :], pairs(state)[:, c, n, :, :], weighted[:, :, :], ALU.add)

            finish.links = 2
            attention("a1", B // 2, 2, False, D + 1, 1, lambda u, qt: q_t[:, u, qt * P:(qt + 1) * P], lambda u, w: k_t[:, u, 0:w],
                      lambda u, kt: values[:, u, kt, :],
                      {"pe": prepare_pe, "act": prepare_act, "dve": prepare_dve, "once": once}, finish, ctx)

        def small_softmax(name, logits, groups, n):
            with ExitStack() as ctx:
                top = sb(f"{name}_top", [P, groups], F32, ctx)
                total = sb(f"{name}_total", [P, groups], F32, ctx)
                shifted = ctx.enter_context(nc.semaphore(f"{name}_shifted"))
                exped = ctx.enter_context(nc.semaphore(f"{name}_exped"))
                block = ctx.enter_context(nc.Block())

                def wide(t):
                    return t[:, :].unsqueeze(2).broadcast_to([P, groups, n])

                @block.vector
                def _(dve):
                    chain = Chain(nc, ctx, dve, f"{name}_chain")
                    chain.link(dve.tensor_reduce(top[:, :], logits, AX.X, ALU.max))
                    dve.tensor_tensor(logits, logits, wide(top), ALU.subtract).then_inc(shifted, 1)
                    dve.wait_ge(exped, 1)
                    chain.link(dve.tensor_reduce(total[:, :], logits, AX.X, ALU.add))
                    chain.link(dve.reciprocal(total[:, :], total[:, :]))
                    chain.link(dve.tensor_tensor(logits, logits, wide(total), ALU.mult))

                @block.scalar
                def _(act):
                    act.activation(table_primer[:, :], ident[:, 0:1], ACT.Exp)
                    act.wait_ge(shifted, 1)
                    act.activation(logits, logits, ACT.Exp).then_inc(exped, 1)

        renew_semaphores()

        normalise("f1_ln", state, normed, 1e-5)
        with ExitStack() as f1:
            inputs_tok = sb("f1_inputs", [P, B, NT, D], F32, f1)
            answers = sb("f1_answers", [P, B, NT, LH, LE * LD], F32, f1)
            mixed = sb("f1_mixed", [P, B, NT, D], F32, f1)
            with ExitStack() as ctx:
                x_t = sb("f1_x", [P, TP], F32, ctx)
                wide_t = sb("f1_wide", [P, TP], F32, ctx)
                q_t = sb("f1_q", [P, LE, TP], F32, ctx)
                k_t = sb("f1_k", [P, LH, TP], F32, ctx)
                values = sb("f1_values", [P, NT, LH, LD + 1], F32, ctx)
                present = sb("f1_present", [P, NT, LH, LD], F32, ctx)
                sums = sb("f1_sums", [P, LE * NT], F32, ctx)
                weighted = sb("f1_weighted", [P, LE * NT, LD], F32, ctx)

                def once(dve):
                    dve.memset(k_t[:, :, :], 0.0)
                    dve.memset(x_t[D:P, :], 1.0)
                    dve.memset(values[:, :, :, LD:LD + 1], 1.0)

                def prepare_pe(pe, b, s_ps, t_ps, o_ps, x_ps, flipped_sum, projected, ready_act, ready_dve, finished):
                    pe.wait_ge(ready_dve.sem, ready_dve.at(3 * b))
                    pe.matmul(s_ps[:, 0, 0:TP], W("hl_wide"), x_t[:, :], start=True, stop=True)
                    for j in range(NT):
                        mm = pe.matmul(s_ps[:, 1, j * D:(j + 1) * D], x_t[:, j * P:(j + 1) * P], W("hl_tok"), start=True, stop=True)
                    mm.then_inc(projected.sem, 1)
                    pe.wait_ge(ready_act.sem, ready_act.at(2 * b))
                    pe.wait_ge(ready_dve.sem, ready_dve.at(3 * b + 1))
                    for e, o in enumerate((s_ps[:, 0, 0:TP], s_ps[:, 1, 0:TP], s_ps[:, 2, 0:TP], x_ps[:, 0:TP])):
                        pe.matmul(o, W("wq_wide", e * P, (e + 1) * P), wide_t[:, :], start=True, stop=True)
                    pe.matmul(t_ps[:, 0, 0:TP], W("wk_wide"), wide_t[:, :], start=True, stop=True)
                    for j in range(NT):
                        mm = pe.matmul(t_ps[:, 1, j * D:(j + 1) * D], wide_t[:, j * P:(j + 1) * P], W("wv_wide"), start=True, stop=True)
                    mm.then_inc(projected.sem, 1)
                    pe.wait_ge(ready_act.sem, ready_act.at(2 * b + 1))
                    pe.wait_ge(ready_dve.sem, ready_dve.at(3 * b + 2))

                def prepare_act(act, b, s_ps, t_ps, o_ps, x_ps, flipped_sum, projected, ready_act, ready_dve, finished):
                    act.wait_ge(projected.sem, projected.at(2 * b))
                    act.activation(wide_t[:, :], s_ps[:, 0, 0:TP], ACT.Copy).then_inc(ready_act.sem, 1)
                    act.wait_ge(projected.sem, projected.at(2 * b + 1))
                    for n in range(LH):
                        rows_n = slice(32 * n, 32 * n + 32)
                        ins = act.activation(k_t[rows_n, n, :], t_ps[rows_n, 0, 0:TP], ACT.Copy)
                    ins.then_inc(ready_act.sem, 1)

                def prepare_dve(dve, b, s_ps, t_ps, o_ps, x_ps, flipped_sum, projected, ready_act, ready_dve, finished):
                    dve.wait_ge(flipped_sum.sem, flipped_sum.at(b))
                    dve.tensor_copy(x_t[0:D, :], x_ps[0:D, 0:TP]).then_inc(ready_dve.sem, 1)
                    dve.wait_ge(projected.sem, projected.at(2 * b))
                    heads = s_ps[:, 1, 0:NT * D]
                    dve.tensor_scalar(present[:, :, :, :].rearrange("p j n d -> p (j n d)"), heads, 0.0, None, ALU.not_equal)
                    dve.tensor_copy(inputs_tok[:, b, :, :], heads.rearrange("p (j d) -> p j d", d=D)).then_inc(ready_dve.sem, 1)
                    dve.wait_ge(projected.sem, projected.at(2 * b + 1))
                    dve.tensor_scalar(q_t[:, 0:3, :], s_ps[:, :, 0:TP], float(LD) ** 0.5, None, ALU.mult)
                    dve.tensor_scalar(q_t[:, 3, :], x_ps[:, 0:TP], float(LD) ** 0.5, None, ALU.mult)
                    dve.tensor_copy(values[:, :, :, 0:LD], t_ps[:, 1, 0:NT * D].rearrange("p (j n d) -> p j n d", n=LH, d=LD))\
                       .then_inc(ready_dve.sem, 1)

                def finish(dve, chain, b, n, products):
                    o = products.rearrange("p (g w) -> p g w", w=LD + 1)
                    chain.link(dve.reciprocal(sums[:, :], o[:, :, LD]))
                    chain.link(dve.tensor_tensor(weighted[:, :, :], o[:, :, 0:LD], sums[:, :].unsqueeze(2).broadcast_to([P, LE * NT, LD]), ALU.mult))
                    return dve.tensor_tensor(answers[:, b, :, n, :].rearrange("p j (e d) -> p e j d", e=LE),
                                             weighted[:, :, :].rearrange("p (e j) d -> p e j d", e=LE),
                                             present[:, :, n, :].unsqueeze(1).broadcast_to([P, LE, NT, LD]), ALU.mult)

                finish.links = 2
                attention("f1", B, LH * LE, True, LD + 1, LE,
                          lambda u, qt: q_t[:, u % LE, qt * P:(qt + 1) * P],
                          lambda u, w: k_t[:, u // LE, 0:w],
                          lambda u, kt: values[:, kt, u // LE, :],
                          {"pe": prepare_pe, "act": prepare_act, "dve": prepare_dve, "once": once}, finish, ctx)

            gates1 = sb("f1_gates", [P, B, NT, LH * LE], F32, f1)
            with ExitStack() as ctx:
                tile = sb("g1_tile", [P, 2, NT, LH * D], F32, ctx)
                turned = sb("g1_turned", [P, 2, 2, TP], F32, ctx)
                turned_ps = ctx.enter_context(nc.psum_tensor("g1_turned_ps", [P, 2, 2, 512], F32))
                logit_ps = ctx.enter_context(nc.psum_tensor("g1_logit_ps", [P, 2, 512], F32))
                staged, turned_sum, copied = Signal(nc, ctx, "g1_staged"), Signal(nc, ctx, "g1_turned_sum"), Signal(nc, ctx, "g1_copied")
                logit_sum, logit_read = Signal(nc, ctx, "g1_logit_sum"), Signal(nc, ctx, "g1_logit_read")
                block = ctx.enter_context(nc.Block())

                @block.gpsimd
                def _(pool):
                    pool.sem_inc(staged.sem, staged.buffers)
                    with pool.Fori(0, B // 2) as c:
                        for s in range(2):
                            pool.wait_ge(turned_sum.sem, turned_sum.at(2 * c + s - 2))
                            pool.tensor_copy(tile[:, s, :, :], pairs(answers)[:, c, s, :, :, :].rearrange("p j n f -> p j (n f)"))\
                                .then_inc(staged.sem, 1)

                @block.tensor
                def _(pe):
                    pe.sem_inc(turned_sum.sem, turned_sum.buffers)
                    pe.sem_inc(logit_sum.sem, logit_sum.buffers)
                    with pe.Fori(0, B // 2) as c:
                        for s in range(2):
                            pe.wait_ge(staged.sem, staged.at(2 * c + s))
                            pe.wait_ge(copied.sem, copied.at(2 * c + s - 2))
                            for h in range(2):
                                for j in range(NT):
                                    mm = pe.transpose(turned_ps[:, s, h, j * P:(j + 1) * P], tile[:, s, j, h * P:(h + 1) * P], ident)
                            mm.then_inc(turned_sum.sem, 1)
                        for s in range(2):
                            pe.wait_ge(copied.sem, copied.at(2 * c + s))
                            pe.wait_ge(logit_read.sem, logit_read.at(2 * c + s - 2))
                            for j in range(NT):
                                for h in range(2):
                                    at = j * 16 + h * 8
                                    mm = pe.matmul(logit_ps[:, s, at:at + 8], turned[:, s, h, j * P:(j + 1) * P], W("gate_w", h * 8, h * 8 + 8),
                                                   start=True, stop=True)
                            mm.then_inc(logit_sum.sem, 1)

                @block.scalar
                def _(act):
                    act.sem_inc(copied.sem, copied.buffers)
                    with act.Fori(0, B // 2) as c:
                        for s in range(2):
                            act.wait_ge(turned_sum.sem, turned_sum.at(2 * c + s))
                            act.wait_ge(logit_sum.sem, logit_sum.at(2 * c + s - 2))
                            act.activation(turned[:, s, :, :], turned_ps[:, s, :, 0:TP], ACT.Copy).then_inc(copied.sem, 1)

                @block.vector
                def _(dve):
                    dve.sem_inc(logit_read.sem, logit_read.buffers)
                    with dve.Fori(0, B // 2) as c:
                        for s in range(2):
                            dve.wait_ge(logit_sum.sem, logit_sum.at(2 * c + s))
                            dve.tensor_tensor(pairs(gates1)[:, c, s, :, :], logit_ps[:, s, 0:NT * 16].rearrange("p (j g) -> p j g", g=16),
                                              R("gate_b").unsqueeze(1).broadcast_to([P, NT, 16]), ALU.add).then_inc(logit_read.sem, 1)

            small_softmax("g1", gates1[:, :, :, :].rearrange("p b j (n e) -> p (b j n) e", e=LE), B * NT * LH, LE)
            with ExitStack() as ctx:
                residual = sb("f1_residual", [P, NT, LH, LD], F32, ctx)
                block = ctx.enter_context(nc.Block())

                @block.vector
                def _(dve):
                    chain = Chain(nc, ctx, dve, "mix_chain")
                    for n in range(LH):
                        dve.tensor_copy(residual[:, :, n, :], inputs_tok[:, n, :, n * LD:(n + 1) * LD])
                    a = answers[:, :, :, :, :].rearrange("p b j n (e d) -> p (b j n e) d", d=LD)
                    g = gates1[:, :, :, :].rearrange("p b j g -> p (b j g)").unsqueeze(2).broadcast_to([P, B * NT * LH * LE, LD])
                    chain.link(dve.tensor_tensor(a, a, g, ALU.mult))
                    chain.link(dve.tensor_reduce(normed[:, :, :, :].rearrange("p b j (n d) -> p (b j n) d", d=LD),
                                                 answers[:, :, :, :, :].rearrange("p b j n (e d) -> p (b j n) d e", d=LD), AX.X, ALU.add))
                    flat = normed[:, :, :, :].rearrange("p b j d -> p b (j d)")
                    r = residual[:, :, :, :].rearrange("p j n d -> p (j n d)").unsqueeze(1).broadcast_to([P, B, NT * D])
                    chain.link(dve.tensor_tensor(flat, flat, r, ALU.add))

            normalise("f1_ln1", normed, mixed, 1e-8, gain="ln_g", shift="ln_b", width=LD)
            with ExitStack() as ctx:
                tile = sb("fc_tile", [P, NT, 2, D], F32, ctx)
                x_t = sb("fc_x", [P, TP], F32, ctx)
                nonzero = sb("fc_nonzero", [P, TP], F32, ctx)
                positive = sb("fc_positive", [P, TP], F32, ctx)
                middle = sb("fc_middle", [P, TP], F32, ctx)
                result = sb("fc_result", [P, 2, NT, 2, D], F32, ctx)
                x_ps = ctx.enter_context(nc.psum_tensor("fc_x_ps", [P, 512], F32))
                m_ps = ctx.enter_context(nc.psum_tensor("fc_m_ps", [P, 512], F32))
                y_ps = ctx.enter_context(nc.psum_tensor("fc_y_ps", [P, 512], F32))
                names = ("staged", "x_sum", "x_ready", "m_sum", "m_positive", "m_ready", "y_sum", "y_read")
                staged, x_sum, x_ready, m_sum, m_positive, m_ready, y_sum, y_read = (Signal(nc, ctx, f"fc_{n}", 1) for n in names)
                block = ctx.enter_context(nc.Block())

                @block.gpsimd
                def _(pool):
                    pool.sem_inc(staged.sem, staged.buffers)
                    with pool.Fori(0, B // 2) as c:
                        pool.wait_ge(y_read.sem, y_read.at(c - 1))
                        for s in range(2):
                            ins = pool.tensor_copy(tile[:, :, s, :], pairs(mixed)[:, c, s, :, :])
                        ins.then_inc(staged.sem, 1)

                @block.tensor
                def _(pe):
                    for x in (x_sum, m_sum, y_sum):
                        pe.sem_inc(x.sem, x.buffers)
                    with pe.Fori(0, B // 2) as c:
                        pe.wait_ge(staged.sem, staged.at(c))
                        pe.wait_ge(x_ready.sem, x_ready.at(c - 1))
                        for j in range(NT):
                            mm = pe.transpose(x_ps[:, j * P:(j + 1) * P], tile[:, j, :, :].rearrange("p s d -> p (s d)"), ident)
                        mm.then_inc(x_sum.sem, 1)
                        pe.wait_ge(x_ready.sem, x_ready.at(c))
                        pe.wait_ge(m_positive.sem, m_positive.at(c - 1))
                        pe.matmul(m_ps[:, 0:TP], W("fc1"), x_t[:, :], start=True, stop=True).then_inc(m_sum.sem, 1)
                        pe.wait_ge(m_ready.sem, m_ready.at(c))
                        pe.wait_ge(y_read.sem, y_read.at(c - 1))
                        for j in range(NT):
                            mm = pe.matmul(y_ps[:, j * P:(j + 1) * P], middle[:, j * P:(j + 1) * P], W("fc2"), start=True, stop=True)
                        mm.then_inc(y_sum.sem, 1)

                @block.scalar
                def _(act):
                    act.sem_inc(x_ready.sem, x_ready.buffers)
                    act.sem_inc(m_positive.sem, m_positive.buffers)
                    with act.Fori(0, B // 2) as c:
                        act.wait_ge(x_sum.sem, x_sum.at(c))
                        act.wait_ge(m_ready.sem, m_ready.at(c - 1))
                        act.activation(x_t[:, :], x_ps[:, 0:TP], ACT.Copy).then_inc(x_ready.sem, 1)
                        act.wait_ge(m_sum.sem, m_sum.at(c))
                        act.activation(positive[:, :], m_ps[:, 0:TP], ACT.Relu, bias=W("fc1_b")).then_inc(m_positive.sem, 1)

                @block.vector
                def _(dve):
                    chain = Chain(nc, ctx, dve, "fc_chain")
                    for x in (m_ready, y_read):
                        dve.sem_inc(x.sem, x.buffers)
                    is_input, answer = (result[:, k, :, :, :].rearrange("p j s d -> p (j s d)") for k in range(2))
                    bias = R("fc2_b").unsqueeze(1).broadcast_to([P, NT, 2 * D])
                    with dve.Fori(0, B // 2) as c:
                        chain.loop(c, 4)
                        dve.wait_ge(staged.sem, staged.at(c))
                        dve.tensor_scalar(is_input, tile[:, :, :, :].rearrange("p j s d -> p (j s d)"), 0.0, None, ALU.not_equal)
                        dve.wait_ge(x_ready.sem, x_ready.at(c))
                        chain.link(dve.tensor_scalar(nonzero[:, :], x_t[:, :], 0.0, None, ALU.not_equal))
                        dve.wait_ge(m_positive.sem, m_positive.at(c))
                        dve.wait_ge(y_sum.sem, y_sum.at(c - 1))
                        dve.tensor_tensor(middle[:, :], positive[:, :], nonzero[:, :], ALU.mult).then_inc(m_ready.sem, 1)
                        dve.wait_ge(y_sum.sem, y_sum.at(c))
                        chain.link(dve.tensor_tensor(answer.rearrange("p (j f) -> p j f", j=NT), y_ps[:, 0:NT * P].rearrange("p (j f) -> p j f", j=NT),
                                                     bias, ALU.add))
                        chain.link(dve.tensor_tensor(answer, answer, is_input, ALU.mult))
                        chain.link(dve.tensor_tensor(answer, answer, tile[:, :, :, :].rearrange("p j s d -> p (j s d)"), ALU.add))
                        for s in range(2):
                            ins = dve.tensor_copy(pairs(normed)[:, c, s, :, :], result[:, 1, :, s, :])
                        ins.then_inc(y_read.sem, 1)
                        chain.close()

            normalise("f1_ln2", normed, mixed, 1e-8, gain="fnorm_g", shift="fnorm_b", width=LD)
            head_gates = sb("f1_head_gates", [P, B * NT, LH], F32, f1)
            with ExitStack() as ctx:
                block = ctx.enter_context(nc.Block())

                @block.vector
                def _(dve):
                    chain = Chain(nc, ctx, dve, "fgate_chain")
                    for n in range(LH):
                        row = R("fgate")[:, n * D:(n + 1) * D].unsqueeze(1).broadcast_to([P, B * NT, D])
                        s = scratch[:, :, :, :].rearrange("p b j d -> p (b j) d")
                        chain.link(dve.tensor_tensor(s, mixed[:, :, :, :].rearrange("p b j d -> p (b j) d"), row, ALU.mult))
                        chain.link(dve.tensor_reduce(head_gates[:, :, n], s, AX.X, ALU.add))

            small_softmax("g2", head_gates[:, :, :], B * NT, LH)
            with ExitStack() as ctx:
                block = ctx.enter_context(nc.Block())

                @block.vector
                def _(dve):
                    chain = Chain(nc, ctx, dve, "f1_chain")
                    m = mixed[:, :, :, :].rearrange("p b j (n d) -> p (b j n) d", d=LD)
                    chain.link(dve.tensor_tensor(m, m, head_gates[:, :, :].rearrange("p g n -> p (g n)").unsqueeze(2)
                                                 .broadcast_to([P, B * NT * LH, LD]), ALU.mult))
                    chain.link(dve.tensor_tensor(state[:, :, :, :], state[:, :, :, :], mixed[:, :, :, :], ALU.add))

        renew_semaphores()

        normalise("a2_ln", state, normed, 1e-5)
        with ExitStack() as ctx:
            x_t = sb("a2_x", [P, TP], F32, ctx)
            q_t = sb("a2_q", [P, 2, TP], F32, ctx)
            k_t = sb("a2_k", [P, AH, TP], F32, ctx)
            values = sb("a2_values", [P, NT, AH, D + 1], F32, ctx)
            sums = sb("a2_sums", [P, NT], F32, ctx)
            weighted = sb("a2_weighted", [P, NT, D], F32, ctx)

            def once(dve):
                dve.memset(x_t[D:P, :], 0.0)
                dve.memset(k_t[:, :, :], 0.0)
                dve.memset(values[:, :, :, D:D + 1], 1.0)

            def prepare_pe(pe, b, s_ps, t_ps, o_ps, x_ps, flipped_sum, projected, ready_act, ready_dve, finished):
                pe.wait_ge(ready_dve.sem, ready_dve.at(2 * b))
                pe.wait_ge(finished.sem, finished.at(AH * b - 1))
                for h in range(2):
                    pe.matmul(s_ps[:, h, 0:TP], W("a2_q", h * P, (h + 1) * P), x_t[:, :], start=True, stop=True)
                pe.matmul(s_ps[:, 2, 0:TP], W("a2_k", 0, P), x_t[:, :], start=True, stop=True)
                pe.matmul(x_ps[:, 0:TP], W("a2_k", P, 2 * P), x_t[:, :], start=True, stop=True)
                for j in range(NT):
                    mm = pe.matmul((t_ps[:, 0, :], t_ps[:, 1, :], o_ps[:, 0, :])[j], x_t[:, j * P:(j + 1) * P], W("a2_vo"), start=True, stop=True)
                mm.then_inc(projected.sem, 1)
                pe.wait_ge(ready_dve.sem, ready_dve.at(2 * b + 1))
                pe.wait_ge(ready_act.sem, ready_act.at(b))

            def prepare_act(act, b, s_ps, t_ps, o_ps, x_ps, flipped_sum, projected, ready_act, ready_dve, finished):
                act.wait_ge(projected.sem, projected.at(b))
                act.activation(q_t[:, :, :], s_ps[:, 0:2, 0:TP], ACT.Copy, scale=float(D) ** -0.5)
                for j in range(2):
                    ins = act.activation(values[:, j, :, 0:D], t_ps[:, j, :].rearrange("p (n d) -> p n d", d=D), ACT.Copy)
                ins.then_inc(ready_act.sem, 1)

            def prepare_dve(dve, b, s_ps, t_ps, o_ps, x_ps, flipped_sum, projected, ready_act, ready_dve, finished):
                dve.wait_ge(flipped_sum.sem, flipped_sum.at(b))
                dve.tensor_copy(x_t[0:D, :], x_ps[0:D, 0:TP]).then_inc(ready_dve.sem, 1)
                dve.wait_ge(projected.sem, projected.at(b))
                for u in range(AH):
                    rows_u = slice(AR * (u % 4), AR * (u % 4) + AR)
                    dve.tensor_copy(k_t[rows_u, u, :], (s_ps[:, 2, :], x_ps)[u // 4][rows_u, 0:TP])
                dve.tensor_copy(values[:, 2, :, 0:D], o_ps[:, 0, :].rearrange("p (n d) -> p n d", d=D)).then_inc(ready_dve.sem, 1)

            def finish(dve, chain, b, n, products):
                o = products.rearrange("p (j w) -> p j w", w=D + 1)
                chain.link(dve.reciprocal(sums[:, :], o[:, :, D]))
                chain.link(dve.tensor_tensor(weighted[:, :, :], o[:, :, 0:D], sums[:, :].unsqueeze(2).broadcast_to([P, NT, D]), ALU.mult))
                ins = dve.tensor_tensor(state[:, b, :, :], state[:, b, :, :], weighted[:, :, :], ALU.add)
                return ins

            finish.links = 2
            attention("a2", B, AH, False, D + 1, 1,
                      lambda u, qt: q_t[:, u // 4, qt * P:(qt + 1) * P],
                      lambda u, w: k_t[:, u, 0:w],
                      lambda u, kt: values[:, kt, u, :],
                      {"pe": prepare_pe, "act": prepare_act, "dve": prepare_dve, "once": once}, finish, ctx)

        def experts(name, gate, bias, function):
            with ExitStack() as whole_mix:
                logits = sb(f"{name}_logits", [P, B, NT, NE], F32, whole_mix)
                combine = sb(f"{name}_combine", [P, B, NT, NE], F32, whole_mix)
                flip(f"{name}_flip", normed, logits, gate)
                groups = B * NT
                with ExitStack() as ctx:
                    first = sb(f"{name}_first", [P, groups, NE], F32, ctx)
                    work = sb(f"{name}_work", [P, groups, NE], F32, ctx)
                    value = sb(f"{name}_value", [P, 4, groups], F32, ctx)
                    apart = ctx.enter_context(nc.semaphore(f"{name}_apart"))
                    exped = ctx.enter_context(nc.semaphore(f"{name}_exped"))
                    block = ctx.enter_context(nc.Block())
                    g = logits[:, :, :, :].rearrange("p b j e -> p (b j) e")
                    second = combine[:, :, :, :].rearrange("p b j e -> p (b j) e")

                    def wide(t):
                        return t.unsqueeze(2).broadcast_to([P, groups, NE])

                    @block.vector
                    def _(dve):
                        chain = Chain(nc, ctx, dve, f"{name}_route_chain")
                        countdown = R("countdown").unsqueeze(1).broadcast_to([P, groups, NE])

                        def pick(best, mark):
                            chain.link(dve.tensor_reduce(best, g, AX.X, ALU.max))
                            chain.link(dve.tensor_tensor(work[:, :, :], g, wide(best), ALU.is_equal))
                            chain.link(dve.tensor_tensor(work[:, :, :], work[:, :, :], countdown, ALU.mult))
                            chain.link(dve.tensor_reduce(value[:, 2, :], work[:, :, :], AX.X, ALU.max))
                            chain.link(dve.tensor_tensor(mark, work[:, :, :], wide(value[:, 2, :]), ALU.is_equal))

                        if bias is not None:
                            chain.link(dve.tensor_tensor(g, g, R(bias).unsqueeze(1).broadcast_to([P, groups, NE]), ALU.add))
                        pick(value[:, 0, :], first[:, :, :])
                        chain.link(dve.scalar_tensor_tensor(g, first[:, :, :], -BIG, g, ALU.mult, ALU.add))
                        pick(value[:, 1, :], second)
                        dve.tensor_tensor(value[:, 3, :], value[:, 1, :], value[:, 0, :], ALU.subtract).then_inc(apart, 1)
                        dve.wait_ge(exped, 1)
                        chain.link(dve.tensor_scalar(value[:, 0, :], value[:, 3, :], 1.0, None, ALU.add))
                        chain.link(dve.reciprocal(value[:, 0, :], value[:, 0, :]))
                        chain.link(dve.tensor_tensor(value[:, 1, :], value[:, 0, :], value[:, 3, :], ALU.mult))
                        chain.link(dve.tensor_tensor(first[:, :, :], first[:, :, :], wide(value[:, 0, :]), ALU.mult))
                        chain.link(dve.tensor_tensor(second, second, wide(value[:, 1, :]), ALU.mult))
                        chain.link(dve.tensor_tensor(second, second, first[:, :, :], ALU.add))

                    @block.scalar
                    def _(act):
                        act.activation(table_primer[:, :], ident[:, 0:1], ACT.Exp)
                        act.wait_ge(apart, 1)
                        act.activation(value[:, 3, :], value[:, 3, :], ACT.Exp).then_inc(exped, 1)

                with ExitStack() as ctx:
                    ahead, slots = 3, 4
                    hidden = sb(f"{name}_hidden", [P, slots, TP], F32, ctx)
                    weighted = sb(f"{name}_weighted", [P, NT, NE * D], F32, ctx)
                    total = sb(f"{name}_total", [P, NT, D], F32, ctx)
                    h_ps = ctx.enter_context(nc.psum_tensor(f"{name}_h_ps", [P, slots, 512], F32))
                    y_ps = ctx.enter_context(nc.psum_tensor(f"{name}_y_ps", [P, NT, 512], F32))

                    def sig(n, buffers):
                        return Signal(nc, ctx, f"{name}_{n}", buffers)

                    hidden_sum, hidden_ready, used = sig("hidden_sum", slots), sig("hidden_ready", slots), sig("used", slots)
                    y_read = sig("y_read", 1)
                    block = ctx.enter_context(nc.Block())

                    @block.tensor
                    def _(pe):
                        for x in (hidden_sum, used):
                            pe.sem_inc(x.sem, x.buffers)
                        with pe.Fori(0, B // 2) as c:
                            def up(i):
                                s, e = i // NE, i % NE
                                pe.wait_ge(hidden_ready.sem, hidden_ready.at(2 * NE * c + i - slots))
                                pe.matmul(h_ps[:, i % slots, 0:TP], W(f"{name}_w1", e * EH, (e + 1) * EH),
                                          pairs(flipped)[:, c, s, PADL:PADL + TP], start=True, stop=True).then_inc(hidden_sum.sem, 1)

                            for i in range(ahead):
                                up(i)
                            for i in range(2 * NE):
                                s, e = i // NE, i % NE
                                if i + ahead < 2 * NE:
                                    up(i + ahead)
                                if e == 0:
                                    pe.wait_ge(y_read.sem, y_read.at(2 * c + s - 1))
                                pe.wait_ge(hidden_ready.sem, hidden_ready.at(2 * NE * c + i))
                                for j in range(NT):
                                    mm = pe.matmul(y_ps[:, j, e * D:(e + 1) * D], hidden[:, i % slots, j * P:(j + 1) * P],
                                                   W(f"{name}_w2", e * D, (e + 1) * D), start=True, stop=True)
                                mm.then_inc(used.sem, 1)

                    @block.scalar
                    def _(act):
                        act.sem_inc(hidden_ready.sem, hidden_ready.buffers)
                        with act.Fori(0, B) as b:
                            for e in range(NE):
                                act.wait_ge(hidden_sum.sem, hidden_sum.at(NE * b + e))
                                act.wait_ge(used.sem, used.at(NE * b + e - slots))
                                act.activation(hidden[:, e % slots, :], h_ps[:, e % slots, 0:TP], function).then_inc(hidden_ready.sem, 1)

                    @block.vector
                    def _(dve):
                        dve.sem_inc(y_read.sem, y_read.buffers)
                        chain = Chain(nc, ctx, dve, f"{name}_chain")
                        with dve.Fori(0, B // 2) as c:
                            chain.loop(c, 2 * 2)
                            for s in range(2):
                                dve.wait_ge(used.sem, used.at(NE * (2 * c + s) + NE - 1))
                                for j in range(NT):
                                    ins = dve.tensor_tensor(weighted[:, j, :], y_ps[:, j, 0:NE * D], R(f"{name}_b2"), ALU.add)
                                ins.then_inc(y_read.sem, 1)
                                dve.wait_ge(y_read.sem, y_read.at(2 * c + s))
                                for j in range(NT):
                                    w = weighted[:, j, :].rearrange("p (e d) -> p e d", e=NE)
                                    ins = dve.tensor_tensor(w, w, pairs(combine)[:, c, s, j, :].unsqueeze(2).broadcast_to([P, NE, D]), ALU.mult)
                                chain.link(ins)
                                chain.link(dve.tensor_reduce(total[:, :, :], weighted[:, :, :].rearrange("p j (e d) -> p j d e", e=NE), AX.X, ALU.add))
                                dve.tensor_tensor(pairs(state)[:, c, s, :, :], pairs(state)[:, c, s, :, :], total[:, :, :], ALU.add)
                            chain.close()

        normalise("m2_ln", state, normed, 1e-5)
        experts("m2", "m2_gate", "m2_bias", ACT.Relu)
        renew_semaphores()

        normalise("a3_ln", state, normed, 1e-5)
        with ExitStack() as ctx:
            tile = sb("a3_tile", [P, NT, 2, D], F32, ctx)
            x_t = sb("a3_x", [P, TP], F32, ctx)
            k_exp = sb("a3_k_exp", [P, TP], F32, ctx)
            v_t = sb("a3_v", [P, TP], F32, ctx)
            q_tok = sb("a3_q_tok", [P, NT, P], F32, ctx)
            k_tok = sb("a3_k_tok", [P, NT, P], F32, ctx)
            mass = sb("a3_mass", [P, 4], F32, ctx)
            pair = sb("a3_pair", [P, P], F32, ctx)
            o_t = sb("a3_o", [P, T], F32, ctx)
            in_line = sb("a3_in_line", [P, 8 * T], F32, ctx)
            banks = [ctx.enter_context(nc.psum_tensor(f"a3_{n}_ps", [P, 512], F32)) for n in ("x", "k", "v", "q", "kt", "pair", "o", "y")]
            x_ps, k_ps, v_ps, q_ps, kt_ps, pair_ps, o_ps, y_ps = banks
            lined_up = ctx.enter_context(nc.semaphore("a3_lined_up"))
            names = ("staged", "x_sum", "x_ready", "k_sum", "v_sum", "q_sum", "top", "exped", "v_ready", "q_ready", "kt_sum", "kt_ready",
                     "pair_sum", "pair_ready", "o_sum", "o_ready", "y_sum", "y_read")
            (staged, x_sum, x_ready, k_sum, v_sum, q_sum, top, exped, v_ready, q_ready, kt_sum, kt_ready, pair_sum, pair_ready,
             o_sum, o_ready, y_sum, y_read) = (Signal(nc, ctx, f"a3_{n}", 1) for n in names)
            lines = 2 * 8 * 16
            block = ctx.enter_context(nc.Block())

            @block.sync
            def _(sp):
                sp.wait_ge(lined_up, 1)
                with sp.Fori(0, B // 2) as c:
                    sp.wait_ge(o_ready.sem, o_ready.at(c))
                    sp.sem_inc(bearer, 1)
                    sp.wait_ge(y_sum.sem, y_sum.at(c - 1))
                    sp.sem_inc(bearer, 1)
                    for s in range(2):
                        for h in range(8):
                            sp.dma_start(in_line[8 * s:8 * s + 8, h * T:(h + 1) * T], o_t[D * s + 8 * h:D * s + 8 * h + 8, :]).then_inc(lined_up, 16)

            @block.gpsimd
            def _(pool):
                pool.sem_inc(staged.sem, staged.buffers)
                with pool.Fori(0, B // 2) as c:
                    pool.wait_ge(x_sum.sem, x_sum.at(c - 1))
                    for s in range(2):
                        ins = pool.tensor_copy(tile[:, :, s, :], pairs(normed)[:, c, s, :, :])
                    ins.then_inc(staged.sem, 1)

            @block.tensor
            def _(pe):
                for x in (x_sum, k_sum, v_sum, q_sum, kt_sum, pair_sum, o_sum, y_sum):
                    pe.sem_inc(x.sem, x.buffers)

                def output(c):
                    pe.wait_ge(y_read.sem, y_read.at(c - 1))
                    pe.wait_ge(lined_up, c * lines + (lines + 1))
                    for j in range(NT):
                        y = y_ps[0:TK[j], j * P:(j + 1) * P]
                        for g in range(8):
                            at = 8 * P * j + g
                            mm = pe.matmul(y, in_line[:, at:at + 8 * (TK[j] - 1) + 1:8], W("a3_out", g * P, (g + 1) * P), start=(g == 0), stop=(g == 7))
                    mm.then_inc(y_sum.sem, 1)

                def attend(c, follows):
                    pe.wait_ge(staged.sem, staged.at(c))
                    pe.wait_ge(x_ready.sem, x_ready.at(c - 1))
                    for j in range(NT):
                        mm = pe.transpose(x_ps[:, j * P:(j + 1) * P], tile[:, j, :, :].rearrange("p s d -> p (s d)"), ident)
                    mm.then_inc(x_sum.sem, 1)
                    pe.wait_ge(x_ready.sem, x_ready.at(c))
                    pe.wait_ge(exped.sem, exped.at(c - 1))
                    pe.matmul(k_ps[:, 0:TP], W("a3_qkv", P, 2 * P), x_t[:, :], start=True, stop=True).then_inc(k_sum.sem, 1)
                    pe.wait_ge(v_ready.sem, v_ready.at(c - 1))
                    pe.matmul(v_ps[:, 0:TP], W("a3_qkv", 2 * P, 3 * P), x_t[:, :], start=True, stop=True).then_inc(v_sum.sem, 1)
                    pe.wait_ge(q_ready.sem, q_ready.at(c - 1))
                    for j in range(NT):
                        mm = pe.matmul(q_ps[:, j * P:(j + 1) * P], x_t[:, j * P:(j + 1) * P], W("a3_qkv", 0, P), start=True, stop=True)
                    mm.then_inc(q_sum.sem, 1)
                    pe.wait_ge(exped.sem, exped.at(c))
                    pe.wait_ge(kt_ready.sem, kt_ready.at(c - 1))
                    for j in range(NT):
                        mm = pe.transpose(kt_ps[:, j * P:(j + 1) * P], k_exp[:, j * P:(j + 1) * P], ident)
                    mm.then_inc(kt_sum.sem, 1)
                    pe.wait_ge(kt_ready.sem, kt_ready.at(c))
                    pe.wait_ge(q_ready.sem, q_ready.at(c))
                    pe.wait_ge(pair_ready.sem, pair_ready.at(c - 1))
                    for j in range(NT):
                        mm = pe.matmul(pair_ps[:, 0:P], k_tok[0:TK[j], j, :], q_tok[0:TK[j], j, :], start=(j == 0), stop=(j == NT - 1))
                    mm.then_inc(pair_sum.sem, 1)
                    pe.wait_ge(pair_ready.sem, pair_ready.at(c))
                    pe.wait_ge(v_ready.sem, v_ready.at(c))
                    pe.wait_ge(o_ready.sem, o_ready.at(c - 1))
                    pe.matmul(o_ps[:, 0:TP], pair[:, :], v_t[:, :], start=True, stop=True).then_inc(o_sum.sem, 1)
                    if follows:
                        output(c - 1)

                attend(0, False)
                with pe.Fori(1, B // 2) as c:
                    attend(c, True)
                output(B // 2 - 1)

            @block.scalar
            def _(act):
                for x in (exped, q_ready, kt_ready):
                    act.sem_inc(x.sem, x.buffers)
                with act.Fori(0, B // 2) as c:
                    act.wait_ge(top.sem, top.at(c))
                    act.wait_ge(kt_sum.sem, kt_sum.at(c - 1))
                    act.wait_ge(pair_ready.sem, pair_ready.at(c - 1))
                    act.activation(k_exp[:, 0:T], k_ps[:, 0:T], ACT.Exp, bias=mass[:, 0:1], accum_out=mass[:, 1:2]).then_inc(exped.sem, 1)
                    act.wait_ge(q_sum.sem, q_sum.at(c))
                    act.wait_ge(pair_sum.sem, pair_sum.at(c - 1))
                    act.activation(q_tok[:, :, :], q_ps[:, 0:NT * P].rearrange("p (j d) -> p j d", d=P), ACT.Copy).then_inc(q_ready.sem, 1)
                    act.wait_ge(kt_sum.sem, kt_sum.at(c))
                    act.activation(k_tok[:, :, :], kt_ps[:, 0:NT * P].rearrange("p (j d) -> p j d", d=P), ACT.Copy).then_inc(kt_ready.sem, 1)

            @block.vector
            def _(dve):
                chain = Chain(nc, ctx, dve, "a3_chain")
                chain.link(dve.memset(k_exp[:, T:TP], 0.0))
                for x in (x_ready, top, v_ready, pair_ready, o_ready, y_read):
                    dve.sem_inc(x.sem, x.buffers)
                chain.link(dve.memset(in_line[0:D, :], 0.0))
                chain.link(dve.memset(in_line[D:P, :], 1.0))
                dve.sem_inc(lined_up, 1)
                reciprocals = Chain(nc, ctx, dve, "a3_reciprocals")

                def keep_output(c):
                    dve.wait_ge(y_sum.sem, y_sum.at(c))
                    y = y_ps[:, 0:NT * P].rearrange("p (j s d) -> p s j d", s=2, d=D)
                    for s in range(2):
                        dve.tensor_copy(pairs(normed)[:, c, s, 0:2, :], y[:, s, 0:2, :])
                        ins = dve.tensor_copy(pairs(normed)[0:LAST, c, s, 2, :], y[0:LAST, s, 2, :])
                    ins.then_inc(y_read.sem, 1)

                def attend(c, follows):
                    reciprocals.loop(c, 1)
                    dve.wait_ge(x_sum.sem, x_sum.at(c))
                    dve.wait_ge(q_sum.sem, q_sum.at(c - 1))
                    dve.tensor_copy(x_t[:, :], x_ps[:, 0:TP]).then_inc(x_ready.sem, 1)
                    dve.wait_ge(k_sum.sem, k_sum.at(c))
                    dve.tensor_reduce(mass[:, 0:1], k_ps[:, 0:T], AX.X, ALU.max, negate=True).then_inc(top.sem, 1)
                    dve.wait_ge(v_sum.sem, v_sum.at(c))
                    dve.wait_ge(o_sum.sem, o_sum.at(c - 1))
                    dve.tensor_copy(v_t[:, :], v_ps[:, 0:TP]).then_inc(v_ready.sem, 1)
                    dve.wait_ge(exped.sem, exped.at(c))
                    reciprocals.link(dve.reciprocal(mass[:, 2:3], mass[:, 1:2]))
                    dve.wait_ge(pair_sum.sem, pair_sum.at(c))
                    dve.scalar_tensor_tensor(pair[:, :], pair_ps[:, 0:P], mass[:, 2:3], W("head_mask"), ALU.mult, ALU.mult).then_inc(pair_ready.sem, 1)
                    dve.wait_ge(o_sum.sem, o_sum.at(c))
                    dve.wait_ge(lined_up, c * lines + 1)
                    dve.tensor_copy(o_t[:, :], o_ps[:, 0:T]).then_inc(o_ready.sem, 1)
                    if follows:
                        keep_output(c - 1)
                    reciprocals.close()

                attend(0, False)
                with dve.Fori(1, B // 2) as c:
                    attend(c, True)
                keep_output(B // 2 - 1)

        with ExitStack() as ctx:
            attended = sb("a3_attended", [P, B, NT, D], F32, ctx)
            normalise("a3_out_ln", normed, attended, 1e-5, gain="a3_gamma", shift="a3_beta", add_to=state)

        with ExitStack() as ctx:
            plain = sb("m3_plain", [P, B, NT, D], F32, ctx)
            normalise("m3_ln", state, plain, 1e-5)
            normalise("m3_own_ln", plain, normed, 1e-5, gain="m3_gamma", shift="m3_beta")
        experts("m3", "m3_gate", None, ACT.Gelu)


        store()


def pack(inputs):
    w = [np.zeros((P, n), np.float32) for n in N_COLS]
    r = np.zeros((N_ROWS,), np.float32)
    a = {k: np.ascontiguousarray(v) for k, v in inputs.items()}

    def put(name, m):
        part, rows_, at, cols = COLS[name]
        m = np.ascontiguousarray(m)
        assert m.shape == (rows_, cols), (name, m.shape)
        w[part][0:rows_, at:at + cols] = m

    def row(name, v):
        at, cols = ROWS[name]
        r[at:at + cols] = np.ascontiguousarray(v).reshape(-1)

    def to_all_rows(m):
        return np.pad(m, ((0, P - m.shape[0]), (0, 0)))

    def with_bias(m, bias):
        return to_all_rows(np.concatenate([m, bias.reshape(1, -1)], 0))

    def halves(m):
        return np.concatenate([m[0:P], m[P:2 * P]], 1)

    idx = np.arange(P)
    put("ident", np.eye(P, dtype=np.float32))
    put("tri_lower", np.concatenate([(np.arange(T)[None, :] < (idx[:, None] + j * P)).astype(np.float32) for j in range(NT)], 1))
    put("causal", np.where(idx[None, :] > idx[:, None], np.float32(-BIG), np.float32(0)))
    head = np.arange(P) // 8
    put("head_mask", np.where(head[:, None] == head[None, :], np.float32(D ** -0.5), np.float32(0)))
    put("ones_row", to_all_rows(np.ones((1, P), np.float32)))
    put("tok_kernel", a["L0_tok_kernel"].transpose(1, 0, 2).reshape(C_IN, TAPS * D))
    for n in ("bias", "beta"):
        row(f"tok_{n}", a[f"L0_tok_{n}"])
    row("tok_mean", a["L0_tok_moving_mean"])
    row("tok_var", a["L0_tok_moving_var"])
    for n in ("pre_g", "pre_b", "post_g", "post_b", "normf_w"):
        row(n, a[f"L0_attn_{n}"])
    for l in range(LAYERS):
        row(f"norm_w{l}", a["L0_attn_norm_w"][l])
        row(f"conv_w{l}", a["L0_attn_conv_w"][l][:, 0, :].T)
        put(f"in_u{l}", np.concatenate([a["L0_attn_inproj_w"][l][0:DI].T] * 2, 0))
        put(f"in_g{l}", np.pad(a["L0_attn_inproj_w"][l][DI:].T, ((0, D), (0, 0))))
        put(f"conv_b{l}", halves(a["L0_attn_conv_b"][l][:, None]))
        xp = a["L0_attn_xproj_w"][l].T
        put(f"x_all{l}", halves(np.pad(np.concatenate([xp[:, RK:]] * 3 + [xp[:, 0:RK]], 1), ((0, 0), (0, P - 96 - RK)))))
        put(f"dt_w{l}", np.pad(a["L0_attn_dtproj_w"][l].T, ((96, P - 96 - RK), (0, 0))))
        put(f"dt_b{l}", halves(a["L0_attn_dtproj_b"][l][:, None]))
        put(f"a_log{l}", halves(a["L0_attn_A_log"][l]))
        put(f"skip{l}", halves(a["L0_attn_D_param"][l][:, None]))
        put(f"out_w{l}", halves(a["L0_attn_outproj_w"][l].T))
    put("route", np.repeat(with_bias(a["L0_ffn_wr"], a["L0_ffn_br"]), P, 1))
    put("f0_w1", with_bias(a["L0_ffn_w1"], a["L0_ffn_b1"]))
    put("f0_w2", halves(a["L0_ffn_w2"]))
    put("f0_b2", to_all_rows(a["L0_ffn_b2"].reshape(1, D)))
    for n in "qkv":
        put(f"a1_{n}", with_bias(a[f"L1_attn_W{n}"].T, a[f"L1_attn_b{n}"]))
    put("a1_scale", np.repeat(a["L1_attn_scale"].reshape(1, 1), D, 0))
    hl, hb = a["L1_ffn_hl_w"], a["L1_ffn_hl_b"]
    put("hl_tok", with_bias(hl.reshape(D, D).T, hb.reshape(-1)))
    wide = np.zeros((P, P), np.float32)
    wq, wk, wv = (np.zeros((P, n), np.float32) for n in (LE * P, P, D))
    gw = np.zeros((P, 16), np.float32)
    fc1, fc2 = np.zeros((P, P), np.float32), np.zeros((P, P), np.float32)
    for n in range(LH):
        c, d = slice(32 * n, 32 * n + LD), slice(LD * n, LD * n + LD)
        wide[0:D, c], wide[D, c] = hl[n].T, hb[n]
        for e in range(LE):
            wq[c, e * P + 32 * n:e * P + 32 * n + LD] = a["L1_ffn_wq"][n, e].T
        wk[c, c] = a["L1_ffn_wk"][n].T
        wv[c, d] = a["L1_ffn_wv"][n].T
        gw[(n % 2) * D:(n % 2) * D + D, (n // 2) * 8 + (n % 2) * 4:(n // 2) * 8 + (n % 2) * 4 + 4] = a["L1_ffn_gate_w"][n].T
        for m, k in ((fc1, "fc1"), (fc2, "fc2")):
            for s in range(2):
                block = slice(D * s + LD * n, D * s + LD * n + LD)
                m[block, block] = a[f"L1_ffn_{k}_w"].T
    for name, m in (("hl_wide", wide), ("wq_wide", wq), ("wk_wide", wk), ("wv_wide", wv), ("gate_w", gw), ("fc1", fc1), ("fc2", fc2)):
        put(name, m)
    put("fc1_b", np.concatenate([a["L1_ffn_fc1_b"]] * (2 * LH)).reshape(P, 1))
    row("fc2_b", np.concatenate([a["L1_ffn_fc2_b"]] * (2 * LH)))
    row("gate_b", a["L1_ffn_gate_b"])
    for n in ("ln_g", "ln_b", "fnorm_g", "fnorm_b"):
        row(n, a[f"L1_ffn_{n}"])
    row("fgate", a["L1_ffn_fgate_w"])
    put("a2_q", to_all_rows(a["L2_attn_Q"].reshape(AH * AR, D).T))
    put("a2_k", to_all_rows(a["L2_attn_K"].reshape(AH * AR, D).T))
    put("a2_vo", to_all_rows(a["L2_attn_VO"].transpose(1, 0, 2).reshape(D, AH * D)))
    for m, s, gate, gb in (("m2", "L2_ffn", "Wg", "bg"), ("m3", "L3_ffn", "Wr", "br")):
        put(f"{m}_gate", with_bias(a[f"{s}_{gate}"], a[f"{s}_{gb}"]))
        put(f"{m}_w1", with_bias(a[f"{s}_W1"].transpose(1, 0, 2).reshape(D, NE * EH), a[f"{s}_b1"].reshape(-1)))
        put(f"{m}_w2", a[f"{s}_W2"].transpose(1, 0, 2).reshape(EH, NE * D))
        row(f"{m}_b2", a[f"{s}_b2"])
    row("m2_bias", a["L2_ffn_bias"])
    qkv, a3_out = np.zeros((2, D, 3, 2, D), np.float32), np.zeros((2, 8, 8, 2, D), np.float32)
    for s in range(2):
        qkv[s, :, :, s, :] = a["L3_attn_Wqkv"].reshape(D, 3, D)
        a3_out[s, :, :, s, :] = a["L3_attn_Wout"].reshape(8, 8, D).transpose(1, 0, 2)
    put("a3_qkv", qkv.reshape(P, 3 * P))
    a3_out = to_all_rows(a3_out.reshape(2 * 8, 8 * P))
    a3_out[D, 0:P] = np.concatenate([a["L3_attn_bout"]] * 2)
    put("a3_out", a3_out)
    row("a3_gamma", a["L3_attn_gamma"])
    row("a3_beta", a["L3_attn_beta"])
    row("m3_gamma", a["L3_ffn_gamma"])
    row("m3_beta", a["L3_ffn_beta"])
    row("countdown", np.arange(NE, 0, -1, dtype=np.float32))
    sel = (np.arange(96)[:, None, None] % 32 == np.arange(32)[None, :, None]) * np.ones((1, 1, P))
    sel = np.pad(sel, ((0, P - 96), (0, 0), (0, 0)))
    x = np.pad(a["x"].transpose(2, 0, 1), ((0, 0), (0, 0), (0, TP + TAPS - 1 - T_IN)))
    return {"x": np.ascontiguousarray(x), "w": w[0], "w2": w[1], "r": r, "sel": np.ascontiguousarray(sel.astype(np.float32))}


def kernel(**inputs):
    import concourse.bacc as bacc
    from concourse.bass_utils import run_bass_kernel_spmd

    nc = bacc.Bacc("TRN2", target_bir_lowering=False, num_devices=1)
    arrays = pack(inputs)
    args = [nc.dram_tensor(n, v.shape, mybir.dt.from_np(v.dtype), kind="ExternalInput").ap() for n, v in arrays.items()]
    out = nc.dram_tensor("y", (B, T, D), F32, kind="ExternalOutput").ap()
    tower(nc, *args, out)
    r = run_bass_kernel_spmd(nc, [arrays], core_ids=[0])
    return r.results[0]["y"]
```
